# Optimizing a Trainium2 kernel written in Bass

```python
import numpy as np
import jax
import jax.numpy as jnp

def _softmax(x, axis=-1):
    return jax.nn.softmax(x, axis=axis)

def _gelu(x):
    return jax.nn.gelu(x, approximate=True)

def _silu(x):
    return jax.nn.silu(x)

def _sigmoid(x):
    return jax.nn.sigmoid(x)

def _layernorm(x, axis=-1, eps=1e-05):
    m = jnp.mean(x, axis=axis, keepdims=True)
    v = jnp.var(x, axis=axis, keepdims=True)
    return (x - m) / jnp.sqrt(v + eps)

def _scatter_add(tgt, idx, src, axis=0):
    return tgt.at[idx].add(src)

def _segment_sum(src, seg, n):
    return jax.ops.segment_sum(src, seg, n)
kernel_name = 'mk_macaron_d2_jaxref_r8_201f1c'

def setup_inputs(seed: int=0):
    np.random.seed(seed)
    _w = jnp.asarray

    def _L0_attn_setup():
        import jax, jax.numpy as jnp
        import numpy as np
        H, DK, DV = (8, 128, 32)
        GATE_NORM = 16.0
        EPS = 1e-05

        def _gla_core(q, k, v, gk):
            B = q.shape[0]
            qs, ks_, vs, gs = (jnp.moveaxis(x, 1, 0) for x in (q, k, v, gk))
            S0 = jnp.zeros((B, H, DK, DV), dtype=q.dtype)

            def step(S, inp):
                qt, kt, vt, gt = inp
                S = S * jnp.exp(gt)[..., None] + kt[..., :, None] * vt[..., None, :]
                ot = jnp.einsum('bhk,bhkv->bhv', qt, S)
                return (S, ot)
            _, o = jax.lax.scan(step, S0, (qs, ks_, vs, gs))
            return jnp.moveaxis(o, 0, 1)
        key = jax.random.key(seed)
        ks = jax.random.split(key, 10)
        B, T, D = (2, 512, 256)
        KD, VD, LR = (H * DK, H * DV, 16)
        s = 0.02
        return {'hidden_states': jax.random.normal(ks[0], (B, T, D), dtype=jnp.float32), 'Wq': jax.random.normal(ks[1], (D, KD), dtype=jnp.float32) * s, 'Wk': jax.random.normal(ks[2], (D, KD), dtype=jnp.float32) * s, 'Wv': jax.random.normal(ks[3], (D, VD), dtype=jnp.float32) * s, 'Wg': jax.random.normal(ks[4], (D, VD), dtype=jnp.float32) * s, 'Wgk0': jax.random.normal(ks[5], (D, LR), dtype=jnp.float32) * s, 'Wgk1': jax.random.normal(ks[6], (LR, KD), dtype=jnp.float32) * s, 'bgk1': jnp.zeros((KD,), dtype=jnp.float32), 'g_norm_w': jnp.ones((DV,), dtype=jnp.float32), 'Wo': jax.random.normal(ks[7], (VD, D), dtype=jnp.float32) * s}
    _L0_attn_in = _L0_attn_setup()

    def _L0_ffn_setup():
        import jax, jax.numpy as jnp
        import numpy as np
        TOP_K = 6
        N_GROUP = 8
        TOPK_GROUP = 3
        CAPACITY = 96
        RSF = 1.0
        key = jax.random.key(seed)
        ks = jax.random.split(key, 8)
        B, S, H = (1, 512, 256)
        E, M = (64, 176)
        MS = 352
        sc = 0.02
        return {'hidden_states': jax.random.normal(ks[0], (B, S, H), jnp.float32), 'gate_weight': jax.random.normal(ks[1], (E, H), jnp.float32) * sc, 'Wg': jax.random.normal(ks[2], (E, M, H), jnp.float32) * sc, 'Wu': jax.random.normal(ks[3], (E, M, H), jnp.float32) * sc, 'Wd': jax.random.normal(ks[4], (E, H, M), jnp.float32) * sc, 'Sg': jax.random.normal(ks[5], (MS, H), jnp.float32) * sc, 'Su': jax.random.normal(ks[6], (MS, H), jnp.float32) * sc, 'Sd': jax.random.normal(ks[7], (H, MS), jnp.float32) * sc}
    _L0_ffn_in = _L0_ffn_setup()

    def _L1_attn_setup():
        import jax, jax.numpy as jnp
        import numpy as np
        D_MODEL = 256
        N_HEADS = 16
        D_HEAD = 128
        D_LATENT = 64
        key = jax.random.key(seed)
        ks = jax.random.split(key, 5)
        s = lambda fan_in: 1.0 / np.sqrt(fan_in)
        x = jax.random.normal(ks[0], (2, 256, D_MODEL), dtype=jnp.float32)
        W_q = jax.random.uniform(ks[1], (D_MODEL, N_HEADS * D_HEAD), jnp.float32, -s(D_MODEL), s(D_MODEL))
        W_kv_down = jax.random.uniform(ks[2], (D_MODEL, D_LATENT), jnp.float32, -s(D_MODEL), s(D_MODEL))
        W_kv_up = jax.random.uniform(ks[3], (D_LATENT, N_HEADS * D_HEAD), jnp.float32, -s(D_LATENT), s(D_LATENT))
        W_o = jax.random.uniform(ks[4], (N_HEADS * D_HEAD, D_MODEL), jnp.float32, -s(N_HEADS * D_HEAD), s(N_HEADS * D_HEAD))
        return {'x': x, 'W_q': W_q, 'W_kv_down': W_kv_down, 'W_kv_up': W_kv_up, 'W_o': W_o}
    _L1_attn_in = _L1_attn_setup()

    def _L1_ffn_setup():
        import jax, jax.numpy as jnp
        import numpy as np
        K_TOP = 2
        key = jax.random.key(seed)
        k0, k1, k2 = jax.random.split(key, 3)
        B, S, D, E, F = (4, 256, 256, 8, 256)
        x = jax.random.normal(k0, (B, S, D), dtype=jnp.float32)
        Wr = jax.random.normal(k1, (D, E), dtype=jnp.float32) * 0.02
        We = jax.random.normal(k2, (E, D, F), dtype=jnp.float32) * 0.02
        be = jnp.zeros((E, F), dtype=jnp.float32)
        return {'x': x, 'Wr': Wr, 'We': We, 'be': be}
    _L1_ffn_in = _L1_ffn_setup()
    _d = {'L0_attn_hidden_states': _L0_attn_in['hidden_states'], 'L0_attn_Wq': _L0_attn_in['Wq'], 'L0_attn_Wk': _L0_attn_in['Wk'], 'L0_attn_Wv': _L0_attn_in['Wv'], 'L0_attn_Wg': _L0_attn_in['Wg'], 'L0_attn_Wgk0': _L0_attn_in['Wgk0'], 'L0_attn_Wgk1': _L0_attn_in['Wgk1'], 'L0_attn_bgk1': _L0_attn_in['bgk1'], 'L0_attn_g_norm_w': _L0_attn_in['g_norm_w'], 'L0_attn_Wo': _L0_attn_in['Wo'], 'L0_ffn_gate_weight': _L0_ffn_in['gate_weight'], 'L0_ffn_Wg': _L0_ffn_in['Wg'], 'L0_ffn_Wu': _L0_ffn_in['Wu'], 'L0_ffn_Wd': _L0_ffn_in['Wd'], 'L0_ffn_Sg': _L0_ffn_in['Sg'], 'L0_ffn_Su': _L0_ffn_in['Su'], 'L0_ffn_Sd': _L0_ffn_in['Sd'], 'L1_attn_W_q': _L1_attn_in['W_q'], 'L1_attn_W_kv_down': _L1_attn_in['W_kv_down'], 'L1_attn_W_kv_up': _L1_attn_in['W_kv_up'], 'L1_attn_W_o': _L1_attn_in['W_o'], 'L1_ffn_Wr': _L1_ffn_in['Wr'], 'L1_ffn_We': _L1_ffn_in['We'], 'L1_ffn_be': _L1_ffn_in['be']}
    _x0 = _d['L0_attn_hidden_states']
    _d['L0_attn_hidden_states'] = jax.random.normal(jax.random.fold_in(jax.random.key(seed), 1), (4, 512, 256), dtype=_x0.dtype)
    del _x0
    return _d

def reference(L0_attn_hidden_states, L0_attn_Wq, L0_attn_Wk, L0_attn_Wv, L0_attn_Wg, L0_attn_Wgk0, L0_attn_Wgk1, L0_attn_bgk1, L0_attn_g_norm_w, L0_attn_Wo, L0_ffn_gate_weight, L0_ffn_Wg, L0_ffn_Wu, L0_ffn_Wd, L0_ffn_Sg, L0_ffn_Su, L0_ffn_Sd, L1_attn_W_q, L1_attn_W_kv_down, L1_attn_W_kv_up, L1_attn_W_o, L1_ffn_Wr, L1_ffn_We, L1_ffn_be):

    def _L0_attn_ref(hidden_states, Wq, Wk, Wv, Wg, Wgk0, Wgk1, bgk1, g_norm_w, Wo):
        import jax, jax.numpy as jnp
        import numpy as np
        H, DK, DV = (8, 128, 32)
        GATE_NORM = 16.0
        EPS = 1e-05

        def _gla_core(q, k, v, gk):
            B = q.shape[0]
            qs, ks_, vs, gs = (jnp.moveaxis(x, 1, 0) for x in (q, k, v, gk))
            S0 = jnp.zeros((B, H, DK, DV), dtype=q.dtype)

            def step(S, inp):
                qt, kt, vt, gt = inp
                S = S * jnp.exp(gt)[..., None] + kt[..., :, None] * vt[..., None, :]
                ot = jnp.einsum('bhk,bhkv->bhv', qt, S)
                return (S, ot)
            _, o = jax.lax.scan(step, S0, (qs, ks_, vs, gs))
            return jnp.moveaxis(o, 0, 1)
        B, T, D = hidden_states.shape
        scale = DK ** (-0.5)
        q = (hidden_states @ Wq).reshape(B, T, H, DK) * scale
        k = (hidden_states @ Wk).reshape(B, T, H, DK)
        v = (hidden_states @ Wv).reshape(B, T, H, DV)
        gk = jax.nn.log_sigmoid(hidden_states @ Wgk0 @ Wgk1 + bgk1) / GATE_NORM
        gk = gk.reshape(B, T, H, DK)
        o = _gla_core(q, k, v, gk)
        g = (hidden_states @ Wg).reshape(B, T, H, DV)
        o = o * jax.lax.rsqrt(jnp.mean(o * o, axis=-1, keepdims=True) + EPS)
        o = o * g_norm_w * (g * jax.nn.sigmoid(g))
        return o.reshape(B, T, H * DV) @ Wo

    def _L0_ffn_ref(hidden_states, gate_weight, Wg, Wu, Wd, Sg, Su, Sd):
        import jax, jax.numpy as jnp
        import numpy as np
        TOP_K = 6
        N_GROUP = 8
        TOPK_GROUP = 3
        CAPACITY = 96
        RSF = 1.0
        B, S, H = hidden_states.shape
        E, M, _ = Wg.shape
        K, NG, TG, C = (TOP_K, N_GROUP, TOPK_GROUP, CAPACITY)
        x = hidden_states.reshape(-1, H)
        T = x.shape[0]
        logits = x.astype(jnp.float32) @ gate_weight.astype(jnp.float32).T
        scores = jax.nn.softmax(logits, axis=-1)
        group_scores = scores.reshape(T, NG, E // NG).max(axis=-1)
        _, gidx = jax.lax.top_k(group_scores, TG)
        gmask = jnp.zeros((T, NG), scores.dtype).at[jnp.arange(T)[:, None], gidx].set(1.0)
        smask = jnp.repeat(gmask, E // NG, axis=1)
        tmp_scores = jnp.where(smask > 0, scores, 0.0)
        topk_w, topk_i = jax.lax.top_k(tmp_scores, K)
        topk_w = topk_w * RSF
        flat = topk_i.reshape(-1)
        oh = jax.nn.one_hot(flat, E, dtype=jnp.int32)
        pos = jnp.sum(jnp.cumsum(oh, axis=0) * oh, axis=-1) - 1
        slot = flat * C + jnp.minimum(pos, C - 1)
        tok = jnp.arange(T * K) // K
        buf = jnp.zeros((E * C, H), x.dtype).at[slot].set(x[tok]).reshape(E, C, H)
        g = jnp.einsum('ech,emh->ecm', buf, Wg)
        u = jnp.einsum('ech,emh->ecm', buf, Wu)
        out = jnp.einsum('ecm,ehm->ech', jax.nn.silu(g) * u, Wd).reshape(E * C, H)
        yk = out[slot].reshape(T, K, H)
        y = jnp.sum(yk * topk_w[..., None].astype(yk.dtype), axis=1)
        shared = jax.nn.silu(x @ Sg.T) * (x @ Su.T) @ Sd.T
        return (y + shared).reshape(B, S, H)

    def _L1_attn_ref(x, W_q, W_kv_down, W_kv_up, W_o):
        import jax, jax.numpy as jnp
        import numpy as np
        D_MODEL = 256
        N_HEADS = 16
        D_HEAD = 128
        D_LATENT = 64
        B, S, _ = x.shape
        q = (x @ W_q).reshape(B, S, N_HEADS, D_HEAD).transpose(0, 2, 1, 3)
        latent = x @ W_kv_down
        kv = (latent @ W_kv_up).reshape(B, S, N_HEADS, D_HEAD).transpose(0, 2, 1, 3)
        scale = 1.0 / np.sqrt(D_HEAD).astype(np.float32)
        scores = jnp.einsum('bhqd,bhkd->bhqk', q, kv) * scale
        probs = jax.nn.softmax(scores, axis=-1)
        out = jnp.einsum('bhqk,bhkd->bhqd', probs, kv)
        out = out.transpose(0, 2, 1, 3).reshape(B, S, N_HEADS * D_HEAD)
        return out @ W_o

    def _L1_ffn_ref(x, Wr, We, be):
        import jax, jax.numpy as jnp
        import numpy as np
        K_TOP = 2
        logits = jnp.einsum('bsd,de->bse', x, Wr)
        w, sel = jax.lax.top_k(logits, K_TOP)
        w = jax.nn.softmax(w, axis=-1)
        E = We.shape[0]
        gate = jnp.einsum('bsk,bske->bse', w, jax.nn.one_hot(sel, E, dtype=w.dtype))
        out = jnp.zeros(x.shape[:2] + (We.shape[2],), dtype=x.dtype)
        for e in range(E):
            out = out + gate[..., e:e + 1] * (jnp.einsum('bsd,df->bsf', x, We[e]) + be[e])
        return out
    x = L0_attn_hidden_states
    x = x + 0.5 * _L0_ffn_ref(_layernorm(x, axis=-1), L0_ffn_gate_weight, L0_ffn_Wg, L0_ffn_Wu, L0_ffn_Wd, L0_ffn_Sg, L0_ffn_Su, L0_ffn_Sd)
    x = x + _L0_attn_ref(_layernorm(x, axis=-1), L0_attn_Wq, L0_attn_Wk, L0_attn_Wv, L0_attn_Wg, L0_attn_Wgk0, L0_attn_Wgk1, L0_attn_bgk1, L0_attn_g_norm_w, L0_attn_Wo)
    x = x + 0.5 * _L0_ffn_ref(_layernorm(x, axis=-1), L0_ffn_gate_weight, L0_ffn_Wg, L0_ffn_Wu, L0_ffn_Wd, L0_ffn_Sg, L0_ffn_Su, L0_ffn_Sd)
    x = x + 0.5 * _L1_ffn_ref(_layernorm(x, axis=-1), L1_ffn_Wr, L1_ffn_We, L1_ffn_be)
    x = x + _L1_attn_ref(_layernorm(x, axis=-1), L1_attn_W_q, L1_attn_W_kv_down, L1_attn_W_kv_up, L1_attn_W_o)
    x = x + 0.5 * _L1_ffn_ref(_layernorm(x, axis=-1), L1_ffn_Wr, L1_ffn_We, L1_ffn_be)
    return x

_drawn_inputs = setup_inputs


def setup_inputs(seed=0):
    import zlib

    import numpy as np

    out = dict(_drawn_inputs(seed))
    spreads = {'L0_attn_bgk1': (0.0, 0.785), 'L0_attn_g_norm_w': (1.0, 0.6), 'L1_ffn_be': (0.0, 0.1)}
    factors = {'L0_attn_Wgk0': 8.0,
     'L0_attn_Wgk1': 8.0,
     'L0_ffn_gate_weight': 8.0,
     'L0_ffn_Wg': 8.0,
     'L0_ffn_Wu': 8.0,
     'L0_ffn_Wd': 8.0,
     'L1_attn_W_q': 5.417,
     'L1_attn_W_kv_down': 4.414,
     'L1_attn_W_kv_up': 3.906,
     'L1_attn_W_o': 3.895}
    for name, (base, spread) in spreads.items():
        noise = np.random.default_rng([zlib.crc32(name.encode()), seed]).standard_normal(out[name].shape)
        drawn = base * np.exp(spread * noise) if base else spread * noise
        out[name] = jnp.asarray(drawn.astype(out[name].dtype))
    for name, factor in factors.items():
        out[name] = (out[name] * factor).astype(out[name].dtype)
    return out
```

```python
from contextlib import ExitStack

import concourse.bass as bass
from concourse import mybir

ALU = mybir.AluOpType
ACT = mybir.ActivationFunctionType
AX = mybir.AxisListType.X
F32 = mybir.dt.float32
BF16 = mybir.dt.bfloat16
U32 = mybir.dt.uint32
F32R = mybir.dt.float32r

P = 128
B, T, D = 4, 512, 256
N = B * T
NT = N // P
TB = T // P
DC = D // P
EPS = 1e-5

E0, M0, TOPK, NG, TG, CAP = 64, 176, 6, 8, 3, 96
MH = M0 // 2
MS = 352
MSC = [(0, 128), (128, 128), (256, 96)]
H0, DK, DV, LR = 8, 128, 32, 16
GATE_NORM = 16.0
SUB = 64
NSUB = T // SUB
E1 = 8
H1, DH, LAT = 16, 128, 64
PAIRS = H1 // 2


class Steps:

    passed = None

    def __init__(self, eng, sem, step, per):
        self.eng, self.sem, self.before, self.per, self.n = eng, sem, step * per, per, 0

    def mark(self, ins):
        ins.then_inc(self.sem, 1)
        self.n += 1

    def settle(self, back=0):
        self.eng.wait_ge(self.sem, self.before + self.n - back)

    def settle_apart(self):
        self.settle()
        self.eng.sem_inc(self.passed, 1)

    def close(self):
        assert self.n == self.per, (self.n, self.per)


class Kit:

    def __init__(self, nc, ctx):
        self.nc, self.ctx, self.sems = nc, ctx, {}

    def sb(self, name, shape, dt=F32):
        return self.ctx.enter_context(self.nc.sbuf_tensor("sb_" + name, shape, dt))

    def sem(self, name):
        if name not in self.sems:
            self.sems[name] = self.ctx.enter_context(self.nc.semaphore(name))
        return self.sems[name]


def scoped(nc, ctx):
    def sb(name, shape, dt=F32):
        return ctx.enter_context(nc.sbuf_tensor("sb_" + name, shape, dt))

    def ps(name, shape):
        width = 1
        for m in shape[1:]:
            width *= m
        bank = ctx.enter_context(nc.psum_tensor(name, [P, 512], F32))[0:shape[0], 0:width]
        if len(shape) == 3:
            return bank.rearrange("p (a b) -> p a b", a=shape[1])
        return bank
    return sb, ps


def row_stats(dve, k):
    done = k.sem("row_stats_steps")
    first = 2 * NT * k.norms
    for n in range(NT):
        dve.bn_stats(k.row_raw[:, n, :], k.X[:, n, :]).then_inc(done, 1)
    for n in range(NT):
        dve.wait_ge(done, first + n + 1)
        dve.bn_aggr(k.row_mv[:, n, :], k.row_raw[:, n, :]).then_inc(done, 1)


def row_std(act, k):
    act.wait_ge(k.sem("row_stats_steps"), 2 * NT * (k.norms + 1))
    act.activation(k.row_rstd[:, :], k.row_mv[:, :, 1], ACT.Sqrt, bias=k.eps[:, 0:1]).then_inc(k.sem("row_std_ready"), 1)


def row_rstd(dve, k):
    dve.wait_ge(k.sem("row_std_ready"), k.norms + 1)
    dve.reciprocal(k.row_rstd[:, :], k.row_rstd[:, :]).then_inc(k.sem("row_rstd_ready"), 1)
    dve.wait_ge(k.sem("row_rstd_ready"), k.norms + 1)


def layernorm(dve, k, n, out, ready):
    dve.tensor_scalar(out, k.X[:, n, :], k.row_mv[:, n, 0:1], k.row_rstd[:, bass.ds(n, 1)],
                      ALU.subtract, ALU.mult).then_inc(ready, 1)


def pool_copy(pool, k, out, in_):
    pool.sem_inc(k.sem("passed"), 1)
    return pool.tensor_copy(out, in_)


def load_and_prepare(nc, k, w):
    loaded_x, loaded_w0, loaded_w1 = k.sem("x_loaded"), k.sem("w0_loaded"), k.sem("w1_loaded")
    prep_loaded, made = k.sem("prep_loaded"), k.sem("constants_made")
    pre_ready, pre_free = k.sem("prep_psum_ready"), k.sem("prep_psum_free")
    with ExitStack() as ctx:
        sb, ps = scoped(nc, ctx)
        wqT = sb("wqT", [P, H1, D])
        upT = sb("upT", [P, H1, LAT])
        wo1 = sb("wo1", [P, H1, D])
        pa = [ps(f"prep_psum{u}", [P, 512]) for u in range(2)]
        block = ctx.enter_context(nc.Block())

        @block.sync
        def _(sp):
            sp.dma_start(k.X[:, :, :], w["x"].rearrange("(n p) d -> p n d", p=P)).then_inc(loaded_x, 16)
            sp.dma_start(wqT[:, :, :], w["wqT1"].rearrange("(h p) d -> p h d", p=DH)).then_inc(prep_loaded, 16)
            sp.dma_start(upT[:, :, :], w["upT1"].rearrange("(h p) d -> p h d", p=DH)).then_inc(prep_loaded, 16)
            sp.dma_start(wo1[:, :, :], w["wo1"].rearrange("(h p) d -> p h d", p=DH)).then_inc(prep_loaded, 16)
            for dst, name in ((k.gateT, "gateT"), (k.sguT, "sguT"), (k.wvg, "wvg"), (k.wgk0, "wgk0"),
                              (k.wq0, "wq0"), (k.wk0, "wk0"), (k.wo0, "wo0")):
                sp.dma_start(dst[:, :, :], w[name].rearrange("(c p) n -> p c n", p=P)).then_inc(loaded_w0, 16)
            for c, (m0, m) in enumerate(MSC):
                sp.dma_start(k.sdT[0:m, c, :], w["sdT"][m0:m0 + m, :]).then_inc(loaded_w0, 16)
            sp.dma_start(k.wgk1[:, :], w["wgk1"]).then_inc(loaded_w0, 16)
            sp.dma_start(k.bgk1[:, :], w["bgk1"]).then_inc(loaded_w0, 16)
            sp.dma_start(k.gnorm_row[:, :], w["gnorm"].rearrange("(a n) -> a n", a=1)).then_inc(k.sem("gnorm_loaded"), 16)
            for dst, name in ((k.wr1, "wr1"), (k.wkv1, "wkv1")):
                sp.dma_start(dst[:, :, :], w[name].rearrange("(c p) n -> p c n", p=P)).then_inc(loaded_w1, 16)
            for c in range(DC):
                sp.dma_start(k.we1[:, c, :, :], w["we1"].rearrange("e (c p) f -> c p e f", p=P)[c]).then_inc(loaded_w1, 16)
            sp.dma_start(k.be1[:, :], w["be1"]).then_inc(loaded_w1, 16)

        @block.gpsimd
        def _(pool):
            s = Steps(pool, made, 0, 20)
            s.mark(pool.memset(k.ident[:, :], 0.0))
            s.mark(pool.memset(k.before_bf[:, :], 1.0))
            s.mark(pool.memset(k.ones_bf[:, :], 1.0))
            s.mark(pool.memset(k.causal[:, :], 1.0))
            s.mark(pool.memset(k.chunk_keep[:, :], 1.0))
            s.mark(pool.memset(k.last_slot[:, :], 0.0))
            s.mark(pool.memset(k.eps[:, :], EPS))
            s.mark(pool.memset(k.zeros[:, :], 0.0))
            s.settle()
            s.mark(pool.affine_select(out=k.ident[:, :], in_=k.ident[:, :], compare_op=ALU.not_equal, fill=1.0,
                                      base=0, pattern=[[-1, P]], channel_multiplier=1))
            s.mark(pool.affine_select(out=k.before_bf[:, :], in_=k.before_bf[:, :], compare_op=ALU.is_gt, fill=0.0,
                                      base=0, pattern=[[1, P]], channel_multiplier=-1))
            s.settle()
            for half in range(2):
                rows = k.causal[SUB * half:SUB * half + SUB, :]
                s.mark(pool.affine_select(out=rows, in_=rows, compare_op=ALU.is_ge, fill=0.0,
                                          base=0, pattern=[[1, SUB]], channel_multiplier=-1))
            s.settle()
            s.mark(pool.memset(k.chunk_keep[:, :].rearrange("p (c s) -> p c s", s=SUB)[:, :, 0:1], 0.0))
            s.mark(pool.iota(k.iota64[:, :], pattern=[[1, E0]], base=0, channel_multiplier=0,
                             allow_small_or_imprecise_dtypes=True))
            s.mark(pool.iota(k.iota_slot[:, :], pattern=[[1, CAP]], base=0, channel_multiplier=0,
                             allow_small_or_imprecise_dtypes=True))
            s.mark(pool.iota(k.token[:, :], pattern=[[P, NT]], base=0, channel_multiplier=1,
                             allow_small_or_imprecise_dtypes=True))
            s.mark(pool.iota(k.token1[:, :], pattern=[[P, NT]], base=1, channel_multiplier=1,
                             allow_small_or_imprecise_dtypes=True))
            s.settle()
            s.mark(pool.memset(k.iota_slot[:, CAP - 1:CAP], -1.0))
            pool.wait_ge(k.sem("gnorm_loaded"), 16)
            s.mark(pool.partition_broadcast(k.gnorm[:, :], k.gnorm_row[:, :], channels=P))
            s.settle()
            s.mark(pool.memset(k.member_sum[:, :, :], 0.0))
            s.settle()
            s.close()

        @block.tensor
        def _(pe):
            pe.wait_ge(prep_loaded, 48)
            n = 0
            for h0 in range(0, H1, 8):
                for c in range(DC):
                    if n >= 2:
                        pe.wait_ge(pre_free, n - 1)
                    for h in range(h0, h0 + 8):
                        last = pe.matmul(pa[n % 2][:, (h - h0) * LAT:(h - h0 + 1) * LAT], wqT[:, h, c * P:(c + 1) * P],
                                         upT[:, h, :], start=True, stop=True)
                    last.then_inc(pre_ready, 1)
                    n += 1
            for p in range(PAIRS):
                pe.wait_ge(pre_free, n - 1)
                for hh in range(2):
                    h = 2 * p + hh
                    last = pe.matmul(pa[n % 2][hh * LAT:(hh + 1) * LAT, 0:D], upT[:, h, :], wo1[:, h, :],
                                     start=True, stop=True)
                last.then_inc(pre_ready, 1)
                n += 1

        @block.vector
        def _(dve):
            n = 0
            for h0 in range(0, H1, 8):
                for c in range(DC):
                    dve.wait_ge(pre_ready, n + 1)
                    dve.tensor_copy(k.absorb[:, c, h0 * LAT:(h0 + 8) * LAT], pa[n % 2][:, :]).then_inc(pre_free, 1)
                    n += 1
            for p in range(PAIRS):
                dve.wait_ge(pre_ready, n + 1)
                dve.tensor_copy(k.mix[:, p, :], pa[n % 2][:, 0:D]).then_inc(pre_free, 1)
                n += 1


def dense_experts(nc, k, r, store=None):
    xn_ready, xT_raw, xT_ready = k.sem("d_xn_ready"), k.sem("d_xT_psum_ready"), k.sem("d_xT_ready")
    logits_ready, gate_ready = k.sem("d_logits_ready"), k.sem("d_gate_ready")
    gap_ready, egap_ready = k.sem("d_logit_gap_ready"), k.sem("d_exp_gap_ready")
    gateT_raw, gateT_ready = k.sem("d_gateT_psum_ready"), k.sem("d_gateT_ready")
    pair_ready, pair_free = k.sem("d_pair_ready"), k.sem("d_pair_free")
    bias_ready, out_ready, stored = k.sem("d_bias_ready"), k.sem("d_out_ready"), k.sem("d_stored")
    NP = E1 // 2
    with ExitStack() as ctx:
        sb, ps = scoped(nc, ctx)
        xn = [sb(f"d{r}_xn{u}", [P, D]) for u in range(2)]
        xT = [sb(f"d{r}_xT{u}", [P, DC, P]) for u in range(2)]
        top = sb(f"d{r}_top", [P, 8])
        top_i = sb(f"d{r}_top_i", [P, 8], U32)
        top_f = sb(f"d{r}_top_f", [P, 2])
        gap = sb(f"d{r}_gap", [P, 1])
        egap = sb(f"d{r}_egap", [P, 1])
        den = sb(f"d{r}_den", [P, 1])
        w1 = sb(f"d{r}_w1", [P, 1])
        w2 = sb(f"d{r}_w2", [P, 1])
        g1 = sb(f"d{r}_g1", [P, E1])
        g2 = sb(f"d{r}_g2", [P, E1])
        gate = [sb(f"d{r}_gate{u}", [P, E1]) for u in range(2)]
        gateT = sb(f"d{r}_gateT", [E1, P])
        acc = [sb(f"d{r}_acc{u}", [P, D]) for u in range(2)]
        ps_x = ps(f"d{r}_ps_x", [P, DC, P])
        ps_r = ps(f"d{r}_ps_r", [P, E1])
        ps_g = ps(f"d{r}_ps_g", [P, P])
        ps_b = ps(f"d{r}_ps_b", [P, D])
        ps_e = [ps(f"d{r}_ps_e{j}", [P, 2, D]) for j in range(NP)]
        block = ctx.enter_context(nc.Block())

        @block.tensor
        def _(pe):
            pe.wait_ge(k.sem("w1_loaded"), 16 * 5)
            with pe.Fori(0, NT // 2) as i:
                for u in range(2):
                    g = i * 2 + (r * NT + u)
                    pe.wait_ge(xn_ready, g + 1)
                    for c in range(DC):
                        last = pe.transpose(ps_x[:, c, :], xn[u][:, c * P:(c + 1) * P], k.ident[:, :])
                    last.then_inc(xT_raw, 1)
                    pe.wait_ge(xT_ready, g + 1)
                    for c in range(DC):
                        last = pe.matmul(ps_r[:, :], xT[u][:, c, :], k.wr1[:, c, :], start=(c == 0), stop=(c == DC - 1))
                    last.then_inc(logits_ready, 1)
                    for j in range(NP):
                        pe.wait_ge(pair_free, g * NP + (j + 1))
                        for c in range(DC):
                            last = pe.matmul(ps_e[j][:, :, :], xT[u][:, c, :], k.we1[:, c, 2 * j:2 * j + 2, :],
                                             start=(c == 0), stop=(c == DC - 1))
                        last.then_inc(pair_ready, 1)
                        if j == 1:
                            pe.wait_ge(gate_ready, g + 1)
                            pe.transpose(ps_g[0:E1, :], gate[u][:, :], k.ident[:, :]).then_inc(gateT_raw, 1)
                    pe.wait_ge(gateT_ready, g + 1)
                    pe.matmul(ps_b[:, :], gateT[:, :], k.be1[:, :], start=True, stop=True).then_inc(bias_ready, 1)

        @block.scalar
        def _(act):
            row_std(act, k)
            with act.Fori(0, NT // 2) as i:
                for u in range(2):
                    g = i * 2 + (r * NT + u)
                    act.wait_ge(xT_raw, g + 1)
                    act.wait_ge(pair_free, g * NP + 1)
                    act.activation(xT[u][:, :, :], ps_x[:, :, :], ACT.Copy).then_inc(xT_ready, 1)
                    act.wait_ge(gap_ready, g + 1)
                    act.activation(egap[:, :], gap[:, :], ACT.Exp).then_inc(egap_ready, 1)
                    act.wait_ge(gateT_raw, g + 1)
                    act.activation(gateT[:, :], ps_g[0:E1, :], ACT.Copy).then_inc(gateT_ready, 1)

        @block.vector
        def _(dve):
            dve.wait_ge(k.sem("x_loaded"), 16)
            row_stats(dve, k)
            if r == 0:
                dve.sem_inc(pair_free, NP)

            def gates(u, g):
                s = Steps(dve, k.sem("d_gate_steps"), g, 8)
                dve.wait_ge(logits_ready, g + 1)
                dve.sem_inc(s.passed, 1)
                s.mark(dve.max(top[:, :], ps_r[:, :]))
                s.settle_apart()
                s.mark(dve.max_index(top_i[:, :], top[:, :], ps_r[:, :]))
                dve.tensor_tensor(gap[:, :], top[:, 1:2], top[:, 0:1], ALU.subtract).then_inc(gap_ready, 1)
                s.settle()
                s.mark(dve.tensor_copy(top_f[:, :], top_i[:, 0:2]))
                dve.wait_ge(egap_ready, g + 1)
                s.mark(dve.tensor_scalar(den[:, :], egap[:, :], 1.0, None, ALU.add))
                s.settle()
                s.mark(dve.reciprocal(w1[:, :], den[:, :]))
                s.settle()
                s.mark(dve.tensor_scalar(w2[:, :], egap[:, :], w1[:, 0:1], None, ALU.mult))
                s.mark(dve.tensor_scalar(g1[:, :], k.iota64[:, 0:E1], top_f[:, 0:1], w1[:, 0:1], ALU.is_equal, ALU.mult))
                s.settle()
                s.mark(dve.tensor_scalar(g2[:, :], k.iota64[:, 0:E1], top_f[:, 1:2], w2[:, 0:1], ALU.is_equal, ALU.mult))
                s.settle()
                s.close()
                dve.tensor_tensor(gate[u][:, :], g1[:, :], g2[:, :], ALU.add).then_inc(gate_ready, 1)
                dve.wait_ge(gate_ready, g + 1)

            def combine(n, u, g):
                s = Steps(dve, k.sem("d_combine_steps"), g, NP + 2)
                for e in range(E1):
                    j, odd = e // 2, e % 2
                    src, w = ps_e[j][:, odd, :], gate[u][:, e:e + 1]
                    if not odd:
                        dve.wait_ge(pair_ready, g * NP + (j + 1))
                    if e < 2:
                        ins = dve.tensor_scalar(acc[odd][:, :], src, w, None, ALU.mult)
                    else:
                        if odd:
                            dve.wait_ge(pair_free, g * NP + (NP + j))
                        else:
                            s.settle()
                        ins = dve.scalar_tensor_tensor(out=acc[odd][:, :], in0=src, scalar=w, in1=acc[odd][:, :],
                                                       op0=ALU.mult, op1=ALU.add)
                    if odd:
                        ins.then_inc(pair_free, 1)
                    else:
                        s.mark(ins)
                dve.wait_ge(bias_ready, g + 1)
                x = k.X[:, n, :]
                s.mark(dve.scalar_tensor_tensor(out=x, in0=ps_b[:, :], scalar=0.5, in1=x, op0=ALU.mult, op1=ALU.add))
                s.settle()
                s.mark(dve.scalar_tensor_tensor(out=x, in0=acc[0][:, :], scalar=0.5, in1=x, op0=ALU.mult, op1=ALU.add))
                s.settle()
                s.close()
                dve.wait_ge(pair_free, g * NP + 2 * NP)
                dve.scalar_tensor_tensor(out=x, in0=acc[1][:, :], scalar=0.5, in1=x,
                                         op0=ALU.mult, op1=ALU.add).then_inc(out_ready, 1)

            def tile(n, u, more):
                g = n + r * NT
                gates(u, g)
                if more:
                    layernorm(dve, k, n + 1, xn[1 - u][:, :], xn_ready)
                combine(n, u, g)

            row_rstd(dve, k)
            layernorm(dve, k, 0, xn[0][:, :], xn_ready)
            with dve.Fori(0, NT // 2 - 1) as i:
                for u in range(2):
                    tile(i * 2 + u, u, True)
            tile(NT - 2, 0, True)
            tile(NT - 1, 1, False)

        if store is not None:
            @block.sync
            def _(sp):
                with sp.Fori(0, NT) as n:
                    sp.wait_ge(out_ready, n + (r * NT + 1))
                    sp.dma_start(store.rearrange("(n p) d -> n p d", p=P)[n], k.X[:, n, :]).then_inc(stored, 16)
                sp.wait_ge(stored, 16 * NT)
    k.norms += 1


def route(nc, k, r):
    xn_ready, xT_raw, xT_ready = k.sem("r_xn_ready"), k.sem("r_xT_psum_ready"), k.sem("r_xT_ready")
    xn_stored = [k.sem(f"r_xn_stored{u}") for u in range(2)]
    kept = k.sem("r_xT_kept")
    logits_ready, nmax_ready, exp_ready = k.sem("r_logits_ready"), k.sem("r_neg_max_ready"), k.sem("r_exp_ready")
    member_ready, pos_ready = k.sem("r_member_ready"), k.sem("r_positions_ready")
    posf_ready, onehot_ready, onehot_free = k.sem("r_position_k_ready"), k.sem("r_onehots_ready"), k.sem("r_onehots_free")
    slots_ready, table_done = k.sem("r_slots_ready"), k.sem("r_table_done")
    begin_ready, lastT_ready, last_ready = k.sem("r_begin_ready"), k.sem("r_lastT_ready"), k.sem("r_last_ready")
    with ExitStack() as ctx:
        sb, ps = scoped(nc, ctx)
        xn = [sb(f"r{r}_xn{u}", [P, D]) for u in range(2)]
        xT = [sb(f"r{r}_xT{u}", [P, DC, P]) for u in range(2)]
        nmax = sb(f"r{r}_nmax", [P, 1])
        ex = sb(f"r{r}_ex", [P, E0])
        esum = sb(f"r{r}_esum", [P, 1])
        rsum = sb(f"r{r}_rsum", [P, 1])
        score = sb(f"r{r}_score", [P, E0])
        gmax = sb(f"r{r}_gmax", [P, NG])
        gtop = sb(f"r{r}_gtop", [P, 8])
        gtop_i = sb(f"r{r}_gtop_i", [P, 8], U32)
        gtop_f = sb(f"r{r}_gtop_f", [P, TG])
        ghot = sb(f"r{r}_ghot", [P, TG, NG])
        gmask = sb(f"r{r}_gmask", [P, NG])
        masked = sb(f"r{r}_masked", [P, E0])
        top = sb(f"r{r}_top", [P, 8])
        top_i = sb(f"r{r}_top_i", [P, 8], U32)
        top_f = sb(f"r{r}_top_f", [P, TOPK])
        hot = [sb(f"r{r}_hot{u}", [P, TOPK, E0]) for u in range(2)]
        hot_tok = [sb(f"r{r}_hot_tok{u}", [P, TOPK, E0]) for u in range(2)]
        hot_pos = [sb(f"r{r}_hot_pos{u}", [P, TOPK, CAP]) for u in range(2)]
        member = [sb(f"r{r}_member{u}", [P, E0], BF16) for u in range(2)]
        last = sb(f"r{r}_last", [P, E0])
        picked = sb(f"r{r}_picked", [P, TOPK, E0])
        posf = [sb(f"r{r}_posf{u}", [P, TOPK]) for u in range(2)]
        slot_c = sb(f"r{r}_slot_c", [P, TOPK])
        last_col = sb(f"r{r}_last_col", [E0, 1])
        ps_x = ps(f"r{r}_ps_x", [P, DC, P])
        ps_r = [ps(f"r{r}_ps_r{u}", [P, E0]) for u in range(2)]
        ps_p = [ps(f"r{r}_ps_p{u}", [P, E0]) for u in range(2)]
        ps_t = ps(f"r{r}_ps_t", [P, E0])
        block = ctx.enter_context(nc.Block())
        kept_table = ps_t[0:CAP, :]

        def spread(ap, n, m):
            return ap.unsqueeze(2).to_broadcast([P, n, m])

        def repeat(ap, n, m):
            return ap.unsqueeze(1).to_broadcast([P, n, m])

        @block.sync
        def _(sp):
            if r == 0:
                for u in range(2):
                    sp.sem_inc(xn_stored[u], 16)
            with sp.Fori(0, NT // 2) as i:
                for u in range(2):
                    n = i * 2 + u
                    sp.wait_ge(xn_ready, n + (r * NT + 1))
                    sp.dma_start(k.xn_rows.rearrange("(n p) d -> n p d", p=P)[n], xn[u][:, :]).then_inc(xn_stored[u], 16)

        @block.tensor
        def _(pe):
            pe.wait_ge(k.sem("w0_loaded"), 16 * 12)
            if r == 0:
                pe.sem_inc(onehot_free, 2)
            pe.wait_ge(begin_ready, 2 * r + 2)
            pe.matmul(kept_table, k.zeros[:, 0:CAP], k.zeros[:, 0:E0], start=True, stop=False)

            def logits(u, g):
                pe.wait_ge(xn_ready, g + 1)
                for c in range(DC):
                    ins = pe.transpose(ps_x[:, c, :], xn[u][:, c * P:(c + 1) * P], k.ident[:, :])
                ins.then_inc(xT_raw, 1)
                pe.wait_ge(xT_ready, g + 1)
                for c in range(DC):
                    ins = pe.matmul(ps_r[u][:, :], xT[u][:, c, :], k.gateT[:, c, :], start=(c == 0), stop=(c == DC - 1))
                ins.then_inc(logits_ready, 1)

            def tile(n, u, more):
                g = n + r * NT
                pe.wait_ge(member_ready, g + 1)
                pe.matmul(ps_p[u][:, :], k.before_bf[:, :], member[u][:, :], start=True, stop=False)
                pe.matmul(ps_p[u][:, :], k.ones_bf[:, :], k.member_sum[:, 1 - u, :], start=False,
                          stop=True).then_inc(pos_ready, 1)
                if more:
                    logits(1 - u, g + 1)
                pe.wait_ge(onehot_ready, g + 1)
                for j in range(TOPK):
                    ins = pe.matmul(kept_table, hot_pos[u][:, j, :], hot_tok[u][:, j, :], start=False, stop=False)
                ins.then_inc(onehot_free, 1)

            logits(0, r * NT)
            with pe.Fori(0, NT // 2 - 1) as i:
                for u in range(2):
                    tile(i * 2 + u, u, True)
            tile(NT - 2, 0, True)
            tile(NT - 1, 1, False)
            pe.wait_ge(slots_ready, (r + 1) * NT)
            pe.transpose(ps_x[0:E0, 0, :], last[:, :], k.ident[:, :]).then_inc(lastT_ready, 1)
            pe.wait_ge(last_ready, r + 1)
            pe.matmul(kept_table, k.last_slot[:, :], k.ident[0:E0, 0:E0], start=False, stop=True).then_inc(table_done, 1)

        @block.scalar
        def _(act):
            row_std(act, k)
            with act.Fori(0, NT // 2) as i:
                for u in range(2):
                    g = i * 2 + (r * NT + u)
                    act.wait_ge(xT_raw, g + 1)
                    act.wait_ge(kept, g + 1)
                    act.activation(xT[u][:, :, :], ps_x[:, :, :], ACT.Copy).then_inc(xT_ready, 1)
                    act.wait_ge(nmax_ready, g + 1)
                    act.activation(ex[:, :], ps_r[u][:, :], ACT.Exp, bias=nmax[:, 0:1],
                                   accum_out=esum[:, 0:1]).then_inc(exp_ready, 1)

        @block.gpsimd
        def _(pool):
            if r == 0:
                pool.sem_inc(kept, 2)
            with pool.Fori(0, NT // 2) as i:
                for u in range(2):
                    n = i * 2 + u
                    g = i * 2 + (r * NT + u)
                    pool.wait_ge(xT_ready, g + 1)
                    pool_copy(pool, k, k.xnT[:, :, bass.ds(n * P, P)], xT[u][:, :, :]).then_inc(kept, 1)
                    pool.wait_ge(onehot_free, g + 1)
                    pool.wait_ge(posf_ready, g + 1)
                    pool.tensor_tensor(hot_tok[u][:, :, :], hot[u][:, :, :], spread(k.token[:, bass.ds(n, 1)], 1, E0)
                                       .to_broadcast([P, TOPK, E0]), ALU.mult)
                    for j in range(TOPK):
                        ins = pool.tensor_scalar(hot_pos[u][:, j, :], k.iota_slot[:, :], posf[u][:, j:j + 1], None,
                                                 ALU.is_equal)
                    ins.then_inc(onehot_ready, 1)

        @block.vector
        def _(dve):
            PER = 16
            dve.wait_ge(k.sem("x_loaded"), 16)
            row_stats(dve, k)
            dve.memset(last[:, :], 0.0).then_inc(begin_ready, 1)
            dve.memset(k.member_sum[:, 1, :], 0.0).then_inc(begin_ready, 1)
            dve.wait_ge(begin_ready, 2 * r + 2)

            def tile(n, u, more):
                g = n + r * NT
                s = Steps(dve, k.sem("r_steps"), g, PER)
                dve.wait_ge(logits_ready, g + 1)
                dve.tensor_reduce(nmax[:, :], ps_r[u][:, :], AX, ALU.max, negate=True).then_inc(nmax_ready, 1)
                if more:
                    dve.wait_ge(xn_stored[1 - u], (n + (r * NT + 2 + u)) * 8)
                    layernorm(dve, k, n + 1, xn[1 - u][:, :], xn_ready)
                dve.wait_ge(exp_ready, g + 1)
                s.mark(dve.reciprocal(rsum[:, :], esum[:, :]))
                s.settle()
                s.mark(dve.tensor_scalar(score[:, :], ex[:, :], rsum[:, 0:1], None, ALU.mult))
                s.settle()
                s.mark(dve.tensor_reduce(gmax[:, :], score[:, :].rearrange("p (g e) -> p g e", g=NG), AX, ALU.max))
                s.settle_apart()
                s.mark(dve.max(gtop[:, :], gmax[:, :]))
                s.settle_apart()
                s.mark(dve.max_index(gtop_i[:, :], gtop[:, :], gmax[:, :]))
                s.settle()
                s.mark(dve.tensor_copy(gtop_f[:, :], gtop_i[:, 0:TG]))
                s.settle()
                s.mark(dve.tensor_tensor(ghot[:, :, :], repeat(k.iota64[:, 0:NG], TG, NG),
                                         spread(gtop_f[:, :], TG, NG), ALU.is_equal))
                s.settle()
                s.mark(dve.tensor_reduce(gmask[:, :], ghot[:, :, :].rearrange("p k g -> p g k"), AX, ALU.add))
                s.settle()
                s.mark(dve.tensor_tensor(masked[:, :].rearrange("p (g e) -> p g e", g=NG),
                                         score[:, :].rearrange("p (g e) -> p g e", g=NG),
                                         spread(gmask[:, :], NG, E0 // NG), ALU.mult))
                s.settle_apart()
                s.mark(dve.max(top[:, :], masked[:, :]))
                s.settle_apart()
                s.mark(dve.max_index(top_i[:, :], top[:, :], masked[:, :]))
                dve.wait_ge(onehot_free, g + 1)
                s.settle()
                s.mark(dve.tensor_copy(top_f[:, :], top_i[:, 0:TOPK]))
                s.settle()
                s.mark(dve.tensor_tensor(hot[u][:, :, :], repeat(k.iota64[:, :], TOPK, E0),
                                         spread(top_f[:, :], TOPK, E0), ALU.is_equal))
                s.settle()
                with nc.allow_low_precision(reason="sums of zeros and ones up to 16 are exact"):
                    dve.tensor_reduce(member[u][:, :], hot[u][:, :, :].rearrange("p k e -> p e k"), AX,
                                      ALU.add).then_inc(member_ready, 1)
                    dve.wait_ge(member_ready, g + 1)
                    s.mark(dve.tensor_tensor(k.member_sum[:, u, :], k.member_sum[:, 1 - u, :], member[u][:, :], ALU.add))
                s.mark(dve.scalar_tensor_tensor(out=last[:, :], in0=member[u][:, :], scalar=k.token1[:, bass.ds(n, 1)],
                                                in1=last[:, :], op0=ALU.mult, op1=ALU.max))
                dve.tensor_scalar(k.weight[:, n, :], top[:, 0:TOPK], 0.5, None, ALU.mult)
                dve.wait_ge(pos_ready, g + 1)
                s.mark(dve.tensor_tensor(picked[:, :, :], hot[u][:, :, :], repeat(ps_p[u][:, :], TOPK, E0), ALU.mult))
                s.settle()
                dve.tensor_reduce(posf[u][:, :], picked[:, :, :], AX, ALU.add).then_inc(posf_ready, 1)
                dve.wait_ge(posf_ready, g + 1)
                s2 = k.sem("r_slot_steps")
                dve.tensor_scalar(slot_c[:, :], posf[u][:, :], float(CAP - 1), None, ALU.min).then_inc(s2, 1)
                dve.wait_ge(s2, g + 1)
                dve.scalar_tensor_tensor(out=k.slot[:, n, :], in0=top_f[:, :], scalar=float(CAP), in1=slot_c[:, :],
                                         op0=ALU.mult, op1=ALU.add).then_inc(slots_ready, 1)
                s.close()

            dve.wait_ge(xn_stored[0], 16 * (r * NT // 2 + 1))
            row_rstd(dve, k)
            layernorm(dve, k, 0, xn[0][:, :], xn_ready)
            with dve.Fori(0, NT // 2 - 1) as i:
                for u in range(2):
                    tile(i * 2 + u, u, True)
            tile(NT - 2, 0, True)
            tile(NT - 1, 1, False)
            dve.wait_ge(lastT_ready, r + 1)
            f = k.sem("r_last_steps")
            dve.tensor_reduce(last_col[:, :], ps_x[0:E0, 0, :], AX, ALU.max).then_inc(f, 1)
            dve.wait_ge(f, r + 1)
            dve.tensor_scalar(k.last_slot[:, CAP - 1:CAP], last_col[:, :], -1.0, 0.0, ALU.add,
                              ALU.max).then_inc(last_ready, 1)
            dve.wait_ge(table_done, r + 1)
            dve.tensor_copy(k.table[:, :], kept_table)
    k.norms += 1


def pipelined(eng, body, first, last, unroll):
    rounds = (last + 1 - first) // unroll
    for s in range(first):
        body(s, s % unroll)
    assert first % unroll == 0
    with eng.Fori(0, rounds) as i:
        for u in range(unroll):
            body(i * unroll + (first + u), u)
    for s in range(first + rounds * unroll, last + 1):
        body(s, s % unroll)


def routed_experts(nc, k, r):
    U, LAG = 4, 3
    staged = k.sem("e_index_staged")
    got = [k.sem(f"e_tokens_got{u}") for u in range(2)]
    gu_got = [k.sem(f"e_gate_up_got{u}") for u in range(U)]
    dn_got = [k.sem(f"e_down_got{u}") for u in range(U)]
    xT_raw, xT_ready = k.sem("e_xT_psum_ready"), k.sem("e_xT_ready")
    gu_ready, act_ready, h_ready = k.sem("e_gate_up_ready"), k.sem("e_silu_ready"), k.sem("e_hidden_ready")
    hT_raw, hT_ready = k.sem("e_hT_psum_ready"), k.sem("e_hT_ready")
    dn_ready, y_ready = k.sem("e_down_ready"), k.sem("e_y_ready")
    y_stored = [k.sem(f"e_y_stored{u}") for u in range(2)]
    with ExitStack() as ctx:
        sb, ps = scoped(nc, ctx)
        index = [sb(f"e{r}_index{u}", [CAP, 1], U32) for u in range(2)]
        x = [sb(f"e{r}_x{u}", [CAP, D]) for u in range(2)]
        xT = [sb(f"e{r}_xT{u}", [P, DC, CAP]) for u in range(2)]
        wgu = [sb(f"e{r}_wgu{u}", [P, DC, 2 * M0]) for u in range(U)]
        wdn = [sb(f"e{r}_wdn{u}", [MH, 2, D]) for u in range(U)]
        sg = [sb(f"e{r}_sg{u}", [CAP, M0]) for u in range(2)]
        h = [sb(f"e{r}_h{u}", [CAP, M0]) for u in range(2)]
        hT = [sb(f"e{r}_hT{u}", [MH, 2, CAP]) for u in range(2)]
        y = [sb(f"e{r}_y{u}", [CAP, D]) for u in range(2)]
        ps_x = [ps(f"e{r}_ps_x{u}", [P, DC, CAP]) for u in range(2)]
        ps_gu = [ps(f"e{r}_ps_gu{u}", [CAP, 2 * M0]) for u in range(2)]
        ps_h = [ps(f"e{r}_ps_h{u}", [MH, 2, CAP]) for u in range(2)]
        ps_y = [ps(f"e{r}_ps_y{u}", [CAP, D]) for u in range(2)]
        block = ctx.enter_context(nc.Block())
        last = E0 - 1 + LAG

        def later(s, n):
            return not isinstance(s, int) or s >= n or r > 0

        def live(s, lag):
            return not isinstance(s, int) or 0 <= s - lag < E0

        @block.sync
        def _(sp):
            def load(e, u):
                g = e + r * E0
                if later(e, U):
                    sp.wait_ge(gu_ready, g - (U - 1))
                sp.dma_start(wgu[u][:, :, :], k.w["wgu0"][e]).then_inc(gu_got[u], 16)
                if later(e, U):
                    sp.wait_ge(dn_ready, g - (U - 1))
                sp.dma_start(wdn[u][:, :, :], k.w["wdn0"][e]).then_inc(dn_got[u], 16)

            pipelined(sp, load, U, E0 - 1, U)

        @block.gpsimd
        def _(pool):
            for u in range(2):
                pool.wait_ge(k.sem(f"r_xn_stored{u}"), 16 * ((r + 1) * NT // 2 + 1))

            def gather(e, u):
                g = e + r * E0
                if later(e, 2):
                    pool.wait_ge(xT_raw, g - 1)
                pool_copy(pool, k, index[u][:, :], k.table[:, bass.ds(e, 1)]).then_inc(staged, 1)
                pool.wait_ge(staged, g + 1)
                pool.sem_inc(k.sem("passed"), 1)
                pool.indirect_dma_start(x[u][:, :], None, k.xn_rows[:, :],
                                        bass.IndirectOffsetOnAxis(ap=index[u][:, 0:1], axis=0)).then_inc(got[u], 16)

            pipelined(pool, gather, 2, E0 - 1, 2)

        @block.tensor
        def _(pe):
            def step(s, u):
                g = s + r * E0
                if live(s, 0):
                    v = u % 2
                    pe.wait_ge(got[v], (g + (2 - v)) * 8)
                    if later(s, 2):
                        pe.wait_ge(xT_ready, g - 1)
                    for c in range(DC):
                        ins = pe.transpose(ps_x[v][:, c, :], x[v][:, c * P:(c + 1) * P], k.ident[0:CAP, 0:CAP])
                    ins.then_inc(xT_raw, 1)
                if live(s, 1):
                    v = (u - 1) % 2
                    pe.wait_ge(xT_ready, g)
                    pe.wait_ge(gu_got[(u - 1) % U], (g - 1 + (U - (u - 1) % U)) * (16 // U))
                    if later(s, 3):
                        pe.wait_ge(h_ready, g - 2)
                    for c in range(DC):
                        ins = pe.matmul(ps_gu[v][:, :], xT[v][:, c, :], wgu[(u - 1) % U][:, c, :],
                                        start=(c == 0), stop=(c == DC - 1))
                    ins.then_inc(gu_ready, 1)
                if live(s, 2):
                    v = u % 2
                    pe.wait_ge(h_ready, g - 1)
                    if later(s, 4):
                        pe.wait_ge(hT_ready, g - 3)
                    for c in range(2):
                        ins = pe.transpose(ps_h[v][:, c, :], h[v][:, c * MH:(c + 1) * MH], k.ident[0:CAP, 0:CAP])
                    ins.then_inc(hT_raw, 1)
                if live(s, 3):
                    v = (u - 1) % 2
                    pe.wait_ge(hT_ready, g - 2)
                    pe.wait_ge(dn_got[(u - 3) % U], (g - 3 + (U - (u - 3) % U)) * (16 // U))
                    if later(s, 5):
                        pe.wait_ge(y_ready, g - 4)
                    for c in range(2):
                        ins = pe.matmul(ps_y[v][:, :], hT[v][:, c, :], wdn[(u - 3) % U][:, c, :],
                                        start=(c == 0), stop=(c == 1))
                    ins.then_inc(dn_ready, 1)

            pipelined(pe, step, U, last, U)

        @block.scalar
        def _(act):
            def step(s, u):
                g = s + r * E0
                if live(s, 0):
                    v = u % 2
                    act.wait_ge(xT_raw, g + 1)
                    if later(s, 2):
                        act.wait_ge(gu_ready, g - 1)
                    act.activation(xT[v][:, :, :], ps_x[v][:, :, :], ACT.Copy).then_inc(xT_ready, 1)
                if live(s, 1):
                    v = (u - 1) % 2
                    act.wait_ge(gu_ready, g)
                    if later(s, 3):
                        act.wait_ge(h_ready, g - 2)
                    act.activation(sg[v][:, :], ps_gu[v][:, 0:M0], ACT.Silu).then_inc(act_ready, 1)
                if live(s, 3):
                    v = (u - 1) % 2
                    act.wait_ge(dn_ready, g - 2)
                    if later(s, 5):
                        act.wait_ge(y_stored[v], (g - (3 + v)) * 8)
                    act.activation(y[v][:, :], ps_y[v][:, :], ACT.Copy).then_inc(y_ready, 1)
                    act.wait_ge(y_ready, g - 2)
                    act.dma_start(k.slot_rows.rearrange("(e c) d -> e c d", c=CAP)[s - 3], y[v][:, :])\
                       .then_inc(y_stored[v], 16)

            pipelined(act, step, U, last, U)
            for v in range(2):
                act.wait_ge(y_stored[v], 16 * ((r + 1) * E0 // 2))

        @block.vector
        def _(dve):
            def step(s, u):
                g = s + r * E0
                if live(s, 1):
                    v = (u - 1) % 2
                    dve.wait_ge(act_ready, g)
                    if later(s, 3):
                        dve.wait_ge(hT_raw, g - 2)
                    dve.tensor_tensor(h[v][:, :], sg[v][:, :], ps_gu[v][:, M0:2 * M0], ALU.mult).then_inc(h_ready, 1)
                if live(s, 2):
                    v = u % 2
                    dve.wait_ge(hT_raw, g - 1)
                    if later(s, 4):
                        dve.wait_ge(dn_ready, g - 3)
                    dve.tensor_copy(hT[v][:, :, :], ps_h[v][:, :, :]).then_inc(hT_ready, 1)

            pipelined(dve, step, U, last, U)


def shared_and_combine(nc, k, r):
    staged, picked, used = k.sem("c_slots_staged"), [k.sem(f"c_rows_got{u}") for u in range(2)], k.sem("c_rows_used")
    gu_ready, silu_ready, hid_ready, down_ready = (k.sem("s_gate_up_ready"), k.sem("s_silu_ready"),
                                                   k.sem("s_hidden_ready"), k.sem("s_down_ready"))
    down_used, summed = k.sem("s_down_used"), k.sem("c_sum_steps")
    BT = 512
    NBT = N // BT
    with ExitStack() as ctx:
        sb, ps = scoped(nc, ctx)
        rows = [[sb(f"c{r}_rows{u}_{j}", [P, D]) for j in range(TOPK)] for u in range(2)]
        at = [[sb(f"c{r}_at{u}_{j}", [P, 1], U32) for j in range(TOPK)] for u in range(2)]
        sg = [sb(f"s{r}_sg{u}", [P, BT]) for u in range(2)]
        hid = sb(f"s{r}_hid", [P, 3, BT])
        ps_g = [ps(f"s{r}_ps_g{u}", [P, BT]) for u in range(2)]
        ps_u = [ps(f"s{r}_ps_u{u}", [P, BT]) for u in range(2)]
        ps_d = [ps(f"s{r}_ps_d{u}", [P, D]) for u in range(2)]
        block = ctx.enter_context(nc.Block())

        @block.gpsimd
        def _(pool):
            if r == 0:
                pool.sem_inc(used, 2)
            with pool.Fori(0, NT // 2) as i:
                for u in range(2):
                    n = i * 2 + u
                    g = i * 2 + (r * NT + u)
                    pool.wait_ge(used, g + 1)
                    for j in range(TOPK):
                        pool_copy(pool, k, at[u][j][:, :], k.slot[:, n, j:j + 1]).then_inc(staged, 1)
                    pool.wait_ge(staged, (g + 1) * TOPK)
                    pool.sem_inc(k.sem("passed"), 1)
                    for j in range(TOPK):
                        pool.indirect_dma_start(rows[u][j][:, :], None, k.slot_rows[:, :],
                                                bass.IndirectOffsetOnAxis(ap=at[u][j][:, 0:1], axis=0)).then_inc(picked[u], 16)

        @block.tensor
        def _(pe):
            with pe.Fori(0, NBT) as i:
                bb = i + r * NBT
                for c, (m0, m) in enumerate(MSC):
                    v = c % 2
                    pe.wait_ge(hid_ready, bb * 3 + (3, 3, 4)[c])
                    for which, bank in ((0, ps_g[v]), (1, ps_u[v])):
                        for d in range(DC):
                            ins = pe.matmul(bank[0:m, :], k.sguT[:, d, which * MS + m0:which * MS + m0 + m],
                                            k.xnT[:, d, bass.ds(i * BT, BT)], start=(d == 0), stop=(d == DC - 1))
                    ins.then_inc(gu_ready, 1)
                pe.wait_ge(hid_ready, bb * 3 + 6)
                for t in range(BT // P):
                    v = t % 2
                    pe.wait_ge(down_used, bb * 4 + (t + 1))
                    for c, (m0, m) in enumerate(MSC):
                        ins = pe.matmul(ps_d[v][:, :], hid[0:m, c, t * P:(t + 1) * P], k.sdT[0:m, c, :],
                                        start=(c == 0), stop=(c == 2))
                    ins.then_inc(down_ready, 1)

        @block.scalar
        def _(act):
            with act.Fori(0, NBT) as i:
                bb = i + r * NBT
                for c, (m0, m) in enumerate(MSC):
                    act.wait_ge(gu_ready, bb * 3 + (c + 1))
                    act.activation(sg[c % 2][0:m, :], ps_g[c % 2][0:m, :], ACT.Silu).then_inc(silu_ready, 1)

        @block.vector
        def _(dve):
            if r == 0:
                dve.sem_inc(hid_ready, 3)
                dve.sem_inc(down_used, 2)
            with dve.Fori(0, NBT) as i:
                bb = i + r * NBT
                for c, (m0, m) in enumerate(MSC):
                    dve.wait_ge(silu_ready, bb * 3 + (c + 1))
                    dve.tensor_tensor(hid[0:m, c, :], sg[c % 2][0:m, :], ps_u[c % 2][0:m, :], ALU.mult)\
                       .then_inc(hid_ready, 1)
                for t in range(BT // P):
                    x = k.X[:, i * 4 + t, :]
                    v = t % 2
                    s = Steps(dve, summed, bb * 4 + t, TOPK)
                    dve.wait_ge(down_ready, bb * 4 + (t + 1))
                    dve.scalar_tensor_tensor(out=x, in0=ps_d[v][:, :], scalar=0.5, in1=x,
                                             op0=ALU.mult, op1=ALU.add).then_inc(down_used, 1)
                    dve.wait_ge(down_used, bb * 4 + (t + 3))
                    dve.wait_ge(picked[v], (bb * 2 + (t // 2 + 1)) * (16 * TOPK))
                    for j in range(TOPK):
                        s.mark(dve.scalar_tensor_tensor(out=x, in0=rows[v][j][:, :],
                                                        scalar=k.weight[:, i * 4 + t, j:j + 1],
                                                        in1=x, op0=ALU.mult, op1=ALU.add))
                        s.settle()
                    s.close()
                    dve.sem_inc(used, 1)


def linear_attention(nc, k):
    A = 3
    UNITS = 4 + 1 + H0 + TB + 2 * H0 + 3 * TB
    QB = UNITS // A
    assert UNITS % A == 0
    HG = H0 // 2
    MID = SUB // 2 - 1
    xn_ready, zmin_ready, soft_ready = k.sem("g_xn_ready"), k.sem("g_zmin_ready"), k.sem("g_softplus_ready")
    gk_ready, cen_ready = k.sem("g_log_gate_ready"), k.sem("g_centred_ready")
    edge_ready = k.sem("g_edges_ready")
    up_ready, down_ready, gw_ready = k.sem("g_exp_up_ready"), k.sem("g_exp_down_ready"), k.sem("g_gate_ready")
    act_steps, dve_steps = k.sem("g_act_steps"), k.sem("g_dve_steps")
    at_ready, at_masked = k.sem("g_scores_ready"), k.sem("g_scores_masked")
    sm_ready, kv_ready, kv_used = k.sem("g_state_ready"), k.sem("g_kv_ready"), k.sem("g_kv_used")
    o_ready, o_copied, sq_ready, on_ready = (k.sem("g_o_ready"), k.sem("g_o_copied"), k.sem("g_squares_ready"),
                                             k.sem("g_normed_ready"))
    out_ready, out_used = k.sem("g_out_ready"), k.sem("g_out_used")
    ms_ready, rms_ready = k.sem("g_mean_square_ready"), k.sem("g_rms_ready")
    a_ready = [k.sem(f"g_bank_ready{a}") for a in range(A)]
    a_free = [k.sem(f"g_bank_free{a}") for a in range(A)]
    TR, LOW, Z, VG, Q, K_, CORE = 0, 4, 5, 5 + H0, 5 + H0 + TB, 5 + 2 * H0 + TB, 5 + 3 * H0 + TB
    order = [("kt", 0, 0), ("kt", 0, 1)]
    for j in range(1, TB):
        order += [("kt", j, 0), ("kt", j, 1), ("o", j - 1, 0)]
    order += [("o", TB - 1, 0)]
    core_unit = {key: CORE + m for m, key in enumerate(order)}
    assert CORE + len(order) == UNITS
    with ExitStack() as ctx:
        sb, ps = scoped(nc, ctx)
        xn = [sb(f"g_xn{j}", [P, D]) for j in range(2)]
        xT = sb("g_xT", [P, DC, T])
        low = sb("g_low", [LR, T])
        zm = sb("g_zm", [P, H0, T])
        za = sb("g_za", [P, H0, T])
        qp = sb("g_qp", [P, H0, T])
        kp = sb("g_kp", [P, H0, T])
        mid = sb("g_mid", [P, H0, NSUB])
        e_mid = sb("g_e_mid", [P, H0, NSUB])
        e_all = sb("g_e_all", [P, H0, NSUB])
        e_rest = sb("g_e_rest", [P, H0, NSUB])
        v = sb("g_v", [P, TB, H0 * DV])
        gw = sb("g_gw", [P, TB, H0 * DV])
        kT = [sb(f"g_kT{u}", [P, H0, DK]) for u in range(2)]
        atm = [sb(f"g_atm{u}", [P, H0, SUB]) for u in range(2)]
        state = sb("g_state", [P, H0, DV])
        state_mid = [sb(f"g_state_mid{u}", [P, H0, DV]) for u in range(2)]
        kv_dec = sb("g_kv_dec", [P, H0, DV])
        o = [sb(f"g_o{u}", [P, H0, DV]) for u in range(2)]
        sq = sb("g_sq", [P, H0, DV])
        ms = sb("g_ms", [P, H0])
        rms = sb("g_rms", [P, H0])
        on = [sb(f"g_on{u}", [P, H0, DV]) for u in range(2)]
        oT = sb("g_oT", [P, 2, P])
        bank = [ps(f"g_bank{a}", [P, 512]) for a in range(A)]
        ps_at = [ps(f"g_ps_at{u}", [P, H0, SUB]) for u in range(2)]
        ps_kv = ps("g_ps_kv", [P, H0, DV])
        ps_o = ps("g_ps_o", [P, H0, DV])
        ps_out = ps("g_ps_out", [P, D])
        block = ctx.enter_context(nc.Block())

        def chunks(ap):
            return ap.rearrange("p h (c s) -> p h c s", s=SUB)

        def over(ap, m):
            return ap.unsqueeze(len(ap.shape)).to_broadcast(list(ap.shape) + [m])

        def emptied(eng, b, m):
            eng.wait_ge(a_free[m % A], b * QB + (m // A + 2))

        def use(eng, b, m):
            eng.wait_ge(a_ready[m % A], b * QB + (m // A + 1))
            return bank[m % A]

        @block.tensor
        def _(pe):
            pe.wait_ge(k.sem("w0_loaded"), 16 * 12)
            with pe.Fori(0, B) as b:
                def take(m):
                    pe.wait_ge(a_free[m % A], b * QB + (m // A + 1))
                    return bank[m % A]

                for j in range(TB):
                    pe.wait_ge(xn_ready, b * TB + (j + 1))
                    to = take(TR + j)
                    for c in range(DC):
                        ins = pe.transpose(to[:, c * P:(c + 1) * P], xn[j % 2][:, c * P:(c + 1) * P], k.ident[:, :])
                    ins.then_inc(a_ready[(TR + j) % A], 1)
                for j in range(TB):
                    emptied(pe, b, TR + j)
                to = take(LOW)
                for c in range(DC):
                    ins = pe.matmul(to[0:LR, :], k.wgk0[:, c, :], xT[:, c, :], start=(c == 0), stop=(c == DC - 1))
                ins.then_inc(a_ready[LOW % A], 1)
                emptied(pe, b, LOW)
                for h in range(H0):
                    to = take(Z + h)
                    pe.matmul(to[:, :], k.wgk1[:, h * DK:(h + 1) * DK], low[:, :], start=True,
                              stop=True).then_inc(a_ready[(Z + h) % A], 1)
                for j in range(TB):
                    to = take(VG + j)
                    for c in range(DC):
                        ins = pe.matmul(to[:, :], xT[:, c, j * P:(j + 1) * P], k.wvg[:, c, :],
                                        start=(c == 0), stop=(c == DC - 1))
                    ins.then_inc(a_ready[(VG + j) % A], 1)
                for w, first in ((k.wq0, Q), (k.wk0, K_)):
                    for h in range(H0):
                        to = take(first + h)
                        for c in range(DC):
                            ins = pe.matmul(to[:, :], w[:, c, h * DK:(h + 1) * DK], xT[:, c, :],
                                            start=(c == 0), stop=(c == DC - 1))
                        ins.then_inc(a_ready[(first + h) % A], 1)

                def project(j):
                    pe.wait_ge(on_ready, b * TB + (j + 1))
                    m = core_unit[("o", j, 0)]
                    to = take(m)
                    flat = on[j % 2][:, :, :].rearrange("p h v -> p (h v)")
                    for c in range(2):
                        ins = pe.transpose(to[:, c * P:(c + 1) * P], flat[:, c * P:(c + 1) * P], k.ident[:, :])
                    ins.then_inc(a_ready[m % A], 1)
                    emptied(pe, b, m)
                    pe.wait_ge(out_used, b * TB + (j + 1))
                    for c in range(2):
                        ins = pe.matmul(ps_out[:, :], oT[:, c, :], k.wo0[:, c, :], start=(c == 0), stop=(c == 1))
                    ins.then_inc(out_ready, 1)

                for h in range(H0 - A, H0):
                    emptied(pe, b, K_ + h)
                for j in range(TB):
                    t0 = j * P
                    pe.wait_ge(at_masked, b * TB + (j + 1))
                    for s in range(2):
                        for h in range(H0):
                            cols = slice(t0 + s * SUB, t0 + (s + 1) * SUB)
                            ins = pe.matmul(ps_at[j % 2][s * SUB:(s + 1) * SUB, h, :], kp[:, h, cols], qp[:, h, cols],
                                            start=True, stop=True)
                    ins.then_inc(at_ready, 1)
                    for half in range(2):
                        m = core_unit[("kt", j, half)]
                        to = take(m)
                        for h in range(4):
                            ins = pe.transpose(to[:, h * P:(h + 1) * P], kp[:, half * 4 + h, t0:t0 + P], k.ident[:, :])
                        ins.then_inc(a_ready[m % A], 1)
                    emptied(pe, b, core_unit[("kt", j, 0)])
                    emptied(pe, b, core_unit[("kt", j, 1)])
                    for s in range(2):
                        rows = slice(s * SUB, (s + 1) * SUB)
                        pe.wait_ge(kv_used, (b * TB + j) * 2 + (s + 1))
                        for h in range(H0):
                            ins = pe.matmul(ps_kv[:, h, :], kT[j % 2][rows, h, :], v[rows, j, h * DV:(h + 1) * DV],
                                            start=True, stop=True)
                        ins.then_inc(kv_ready, 1)
                        pe.wait_ge(sm_ready, (b * TB + j) * 2 + (s + 1))
                        if s == 0:
                            pe.wait_ge(at_masked, b * TB + (j + 3))
                            pe.wait_ge(o_copied, b * TB + (j + 1))
                        for h in range(H0):
                            cols = slice(t0 + s * SUB, t0 + (s + 1) * SUB)
                            pe.matmul(ps_o[rows, h, :], qp[:, h, cols], state_mid[s][:, h, :], start=True, stop=False)
                            ins = pe.matmul(ps_o[rows, h, :], atm[j % 2][rows, h, :], v[rows, j, h * DV:(h + 1) * DV],
                                            start=False, stop=True)
                    ins.then_inc(o_ready, 1)
                    if j:
                        project(j - 1)
                project(TB - 1)

        @block.scalar
        def _(act):
            act.wait_ge(k.sem("w0_loaded"), 16 * 12)
            row_std(act, k)
            with act.Fori(0, B) as b:
                s = Steps(act, act_steps, b, 4)
                for j in range(TB):
                    src = use(act, b, TR + j)
                    act.activation(xT[:, :, j * P:(j + 1) * P], src[:, 0:D].rearrange("p (c t) -> p c t", c=DC),
                                   ACT.Copy).then_inc(a_free[(TR + j) % A], 1)
                src = use(act, b, LOW)
                act.activation(low[:, :], src[0:LR, :], ACT.Copy).then_inc(a_free[LOW % A], 1)
                for h in range(H0):
                    m = Z + h
                    src = use(act, b, m)
                    act.activation(za[:, h, :], src[:, :], ACT.Identity, bias=k.bgk1[:, h:h + 1])\
                       .then_inc(a_free[m % A], 1)
                for half in range(2):
                    part = za[:, half * HG:(half + 1) * HG, :]
                    act.wait_ge(zmin_ready, b * 2 + (half + 1))
                    s.mark(act.activation(part, part, ACT.Abs))
                for half in range(2):
                    part = za[:, half * HG:(half + 1) * HG, :]
                    s.settle(back=1)
                    s.mark(act.activation(part, part, ACT.Exp, scale=-1.0))
                for half in range(2):
                    part = za[:, half * HG:(half + 1) * HG, :]
                    s.settle(back=1 - half)
                    act.activation(part, part, ACT.Ln, bias=1.0).then_inc(soft_ready, 1)
                for j in range(TB):
                    m = VG + j
                    src = use(act, b, m)
                    act.activation(v[:, j, :], src[:, 0:H0 * DV], ACT.Copy)
                    act.activation(gw[:, j, :], src[:, H0 * DV:2 * H0 * DV], ACT.Silu).then_inc(a_free[m % A], 1)
                for half in range(2):
                    hs = slice(half * HG, (half + 1) * HG)
                    act.wait_ge(cen_ready, b * 2 + (half + 1))
                    act.activation(e_mid[:, hs, :], mid[:, hs, :], ACT.Exp, scale=1.0 / GATE_NORM)
                    act.activation(e_all[:, hs, :], chunks(zm[:, hs, :])[:, :, :, SUB - 1], ACT.Exp,
                                   scale=1.0 / GATE_NORM).then_inc(edge_ready, 1)
                    act.wait_ge(edge_ready, b * 2 + (half + 1))
                    act.activation(zm[:, hs, :], za[:, hs, :], ACT.Exp, scale=1.0 / GATE_NORM).then_inc(up_ready, 1)
                    act.wait_ge(up_ready, b * 2 + (half + 1))
                    act.activation(za[:, hs, :], za[:, hs, :], ACT.Exp, scale=-1.0 / GATE_NORM).then_inc(down_ready, 1)

                def oT_copy(j):
                    m = core_unit[("o", j, 0)]
                    src = use(act, b, m)
                    act.activation(oT[:, :, :], src[:, 0:D].rearrange("p (c t) -> p c t", c=2),
                                   ACT.Copy).then_inc(a_free[m % A], 1)

                for j in range(TB):
                    for half in range(2):
                        m = core_unit[("kt", j, half)]
                        src = use(act, b, m)
                        act.activation(kT[j % 2][:, half * 4:(half + 1) * 4, :],
                                       src[:, :].rearrange("p (h d) -> p h d", h=4), ACT.Copy).then_inc(a_free[m % A], 1)
                    act.wait_ge(o_ready, b * TB + (j + 1))
                    act.activation(o[j % 2][:, :, :], ps_o[:, :, :], ACT.Copy).then_inc(o_copied, 1)
                    if j:
                        oT_copy(j - 1)
                    act.wait_ge(ms_ready, b * TB + (j + 1))
                    act.activation(rms[:, :], ms[:, :], ACT.Sqrt, bias=k.eps[:, 0:1], scale=1.0 / DV).then_inc(rms_ready, 1)
                oT_copy(TB - 1)
                s.close()

        @block.gpsimd
        def _(pool):
            with pool.Fori(0, B) as b:
                for half in range(2):
                    hs = slice(half * HG, (half + 1) * HG)
                    pool.wait_ge(soft_ready, b * 2 + (half + 1))
                    pool.tensor_tensor(zm[:, hs, :], zm[:, hs, :], za[:, hs, :], ALU.subtract).then_inc(gk_ready, 1)
                for j in range(TB):
                    emptied(pool, b, VG + j)
                    g = gw[:, j, :].rearrange("p (h v) -> p h v", h=H0)
                    pool.tensor_tensor(g, g, k.gnorm[:, :].unsqueeze(1).to_broadcast([P, H0, DV]),
                                       ALU.mult).then_inc(gw_ready, 1)
                for j in range(TB):
                    pool.wait_ge(o_copied, b * TB + (j + 2))
                    pool.tensor_tensor(sq[:, :, :], o[j % 2][:, :, :], o[j % 2][:, :, :], ALU.mult).then_inc(sq_ready, 1)

        @block.vector
        def _(dve):
            dve.wait_ge(k.sem("x_loaded"), 16)
            row_stats(dve, k)
            for a in range(A):
                dve.sem_inc(a_free[a], 1)
            dve.sem_inc(at_masked, 2)
            dve.sem_inc(kv_used, 1)
            dve.sem_inc(o_copied, 1)
            dve.sem_inc(out_used, 1)
            row_rstd(dve, k)
            with dve.Fori(0, B) as b:
                s = Steps(dve, dve_steps, b, 2 * 2 + 2 + TB * 6)
                for j in range(TB):
                    if j >= 2:
                        dve.wait_ge(a_ready[(TR + j - 2) % A], b * QB + ((TR + j - 2) // A + 1))
                    layernorm(dve, k, b * TB + j, xn[j % 2][:, :], xn_ready)
                for half in range(2):
                    hs = slice(half * HG, (half + 1) * HG)
                    emptied(dve, b, Z + HG * (half + 1) - 1)
                    dve.tensor_scalar(zm[:, hs, :], za[:, hs, :], 0.0, None, ALU.min).then_inc(zmin_ready, 1)
                for half in range(2):
                    hs = slice(half * HG, (half + 1) * HG)
                    dve.wait_ge(gk_ready, b * 2 + (half + 1))
                    for h in range(half * HG, (half + 1) * HG):
                        ins = dve.tensor_tensor_scan(zm[:, h, :], k.chunk_keep[:, :], zm[:, h, :], 0.0, ALU.mult, ALU.add)
                    s.mark(ins)
                    s.settle()
                    s.mark(dve.tensor_copy(mid[:, hs, :], chunks(zm[:, hs, :])[:, :, :, MID]))
                    s.settle()
                    for h in range(half * HG, (half + 1) * HG):
                        ins = dve.tensor_tensor(za[:, h, :].rearrange("p (c s) -> p c s", s=SUB),
                                                zm[:, h, :].rearrange("p (c s) -> p c s", s=SUB),
                                                over(mid[:, h, :], SUB), ALU.subtract)
                    ins.then_inc(cen_ready, 1)
                for first, dst, dec, scale in ((Q, qp, zm, DK ** -0.5), (K_, kp, za, 1.0)):
                    for h in range(H0):
                        m = first + h
                        if h % HG == 0:
                            dve.wait_ge(up_ready if first == Q else down_ready, b * 2 + (h // HG + 1))
                        src = use(dve, b, m)
                        dve.scalar_tensor_tensor(out=dst[:, h, :], in0=src[:, :], scalar=scale, in1=dec[:, h, :],
                                                 op0=ALU.mult, op1=ALU.mult).then_inc(a_free[m % A], 1)
                s.mark(dve.tensor_copy(e_rest[:, :, :], chunks(zm[:, :, :])[:, :, :, SUB - 1]))
                s.mark(dve.memset(state[:, :, :], 0.0))
                s.settle()

                def add_out(j):
                    dve.wait_ge(out_ready, b * TB + (j + 1))
                    x = k.X[:, b * TB + j, :]
                    dve.tensor_tensor(x, ps_out[:, :], x, ALU.add).then_inc(out_used, 1)

                for j in range(TB):
                    dve.wait_ge(at_ready, b * TB + (j + 1))
                    dve.tensor_tensor(atm[j % 2][:, :, :], ps_at[j % 2][:, :, :],
                                      k.causal[:, :].unsqueeze(1).to_broadcast([P, H0, SUB]),
                                      ALU.mult).then_inc(at_masked, 1)
                    for half in range(2):
                        c = 2 * j + half
                        dve.tensor_tensor(state_mid[half][:, :, :], state[:, :, :], over(e_mid[:, :, c], DV),
                                          ALU.mult).then_inc(sm_ready, 1)
                        s.mark(dve.tensor_tensor(state[:, :, :], state[:, :, :], over(e_all[:, :, c], DV), ALU.mult))
                        dve.wait_ge(kv_ready, (b * TB + j) * 2 + (half + 1))
                        dve.tensor_tensor(kv_dec[:, :, :], ps_kv[:, :, :], over(e_rest[:, :, c], DV),
                                          ALU.mult).then_inc(kv_used, 1)
                        dve.wait_ge(kv_used, (b * TB + j) * 2 + (half + 2))
                        s.settle()
                        s.mark(dve.tensor_tensor(state[:, :, :], state[:, :, :], kv_dec[:, :, :], ALU.add))
                        s.settle()
                    if j:
                        add_out(j - 1)
                    dve.wait_ge(sq_ready, b * TB + (j + 1))
                    dve.tensor_reduce(ms[:, :], sq[:, :, :], AX, ALU.add).then_inc(ms_ready, 1)
                    dve.wait_ge(rms_ready, b * TB + (j + 1))
                    s.mark(dve.reciprocal(rms[:, :], rms[:, :]))
                    s.settle()
                    s.mark(dve.tensor_tensor(on[j % 2][:, :, :], o[j % 2][:, :, :], over(rms[:, :], DV), ALU.mult))
                    s.settle()
                    dve.wait_ge(gw_ready, b * TB + (j + 1))
                    dve.tensor_tensor(on[j % 2][:, :, :], on[j % 2][:, :, :],
                                      gw[:, j, :].rearrange("p (h v) -> p h v", h=H0), ALU.mult).then_inc(on_ready, 1)
                add_out(TB - 1)
                s.close()
    k.norms += 1


def latent_attention(nc, k):
    UP = 2 * TB
    U2 = 2 * UP
    NU = PAIRS * UP
    TLAG = 3
    VLAG = UP + TLAG
    OLAG = VLAG + TB
    LAST = NU - UP + OLAG
    SCALE = DH ** -0.5
    PRE = TB + 2 + PAIRS
    QB = PRE // 2
    assert PRE % 2 == 0 and TB % 2 == 0
    xn_ready = k.sem("m_xn_ready")
    bank_ready = [k.sem(f"m_bank_ready{u}") for u in range(2)]
    bank_free = [k.sem(f"m_bank_free{u}") for u in range(2)]
    high_ready = k.sem("m_high_parts_ready")
    q_staged, s_ready, nmax_ready, p_ready = (k.sem("m_queries_staged"), k.sem("m_scores_ready"),
                                              k.sem("m_neg_max_ready"), k.sem("m_probs_ready"))
    scaled, pT_raw, pT_ready = k.sem("m_normalised"), k.sem("m_pT_psum_ready"), k.sem("m_pT_ready")
    v_ready, o_copied = k.sem("m_values_ready"), k.sem("m_o_copied")
    out_ready, out_used = k.sem("m_out_ready"), k.sem("m_out_used")
    max_steps, inv_steps = k.sem("m_max_steps"), k.sem("m_inverse_steps")
    TR, LATT, LATK, Q = 0, TB, TB + 1, TB + 2
    with ExitStack() as ctx:
        sb, ps = scoped(nc, ctx)
        xn = [sb(f"m_xn{u}", [P, D]) for u in range(2)]
        xT = sb("m_xT", [P, DC, T])
        latT = [sb(f"m_latT_{part}", [P, T], F32R) for part in ("high", "low")]
        lat = sb("m_lat", [P, TB, LAT])
        qa = sb("m_qa", [P, H1, T], F32R)
        qs = [sb(f"m_qs{u}", [P, 2, T], F32R) for u in range(2)]
        raw = sb("m_raw", [P, 2])
        nmax = sb("m_nmax", [P, 2])
        rsum = sb("m_rsum", [P, 4])
        rinv = sb("m_rinv", [P, 2])
        prob = [sb(f"m_prob{u}", [P, T]) for u in range(4)]
        pT = [sb(f"m_pT{u}", [P, 2, TB, T]) for u in range(2)]
        oT = sb("m_oT", [P, PAIRS, T])
        bank = [ps(f"m_bank{u}", [P, 512]) for u in range(2)]
        ps_s = [ps(f"m_ps_s{u}", [P, T]) for u in range(2)]
        ps_p = [ps(f"m_ps_p{u}", [P, TB, P]) for u in range(2)]
        ps_v = [ps(f"m_ps_v{u}", [P, T]) for u in range(2)]
        block = ctx.enter_context(nc.Block())

        def live(m, lag):
            return not isinstance(m, int) or 0 <= m - lag < NU

        def place(u, lag):
            w = (u - lag) % U2
            return w // UP, w % UP // 2, w % 2

        def steps(eng, body):
            for m in range(U2):
                body(m, m, 0)
            with eng.Fori(1, NU // U2) as i:
                for u in range(U2):
                    body(i * U2 + u, u, i)
            for m in range(NU, LAST + 1):
                body(m, m - NU, NU // U2)

        def pair_at(m, u, i, lag):
            w = u - lag
            if w % UP or (isinstance(m, int) and not 0 <= m - lag < NU):
                return None
            return i * 2 + w // UP

        @block.tensor
        def _(pe):
            pe.wait_ge(k.sem("w1_loaded"), 16 * 5)
            with pe.Fori(0, B) as b:
                def take(m):
                    pe.wait_ge(bank_free[m % 2], b * QB + (m // 2 + 1))
                    return bank[m % 2]

                for j in range(TB):
                    pe.wait_ge(xn_ready, b * TB + (j + 1))
                    to = take(TR + j)
                    for c in range(DC):
                        ins = pe.transpose(to[:, c * P:(c + 1) * P], xn[j % 2][:, c * P:(c + 1) * P], k.ident[:, :])
                    ins.then_inc(bank_ready[j % 2], 1)
                for j in range(TB - 2, TB):
                    pe.wait_ge(bank_free[j % 2], b * QB + (j // 2 + 2))
                to = take(LATT)
                for c in range(DC):
                    ins = pe.matmul(to[:, :], k.wkv1[:, c, :], xT[:, c, :], start=(c == 0), stop=(c == DC - 1))
                ins.then_inc(bank_ready[LATT % 2], 1)
                to = take(LATK)
                for j in range(TB):
                    for c in range(DC):
                        ins = pe.matmul(to[:, j * LAT:(j + 1) * LAT], xT[:, c, j * P:(j + 1) * P], k.wkv1[:, c, 0:LAT],
                                        start=(c == 0), stop=(c == DC - 1))
                ins.then_inc(bank_ready[LATK % 2], 1)
                for p in range(PAIRS):
                    to = take(Q + p)
                    for c in range(DC):
                        ins = pe.matmul(to[:, :], k.absorb[:, c, p * P:(p + 1) * P], xT[:, c, :],
                                        start=(c == 0), stop=(c == DC - 1))
                    ins.then_inc(bank_ready[(Q + p) % 2], 1)

                def step(m, u, i):
                    g = b * NU + m
                    if live(m, 0):
                        par, tile, hh = place(u, 0)
                        if u % UP == 0:
                            pe.wait_ge(q_staged, b * PAIRS + i * 2 + (u // UP + 1))
                        pe.wait_ge(p_ready, g + 1)
                        query = qs[par][:, hh, tile * P:(tile + 1) * P]
                        pe.matmul(ps_s[u % 2][:, :], query, latT[0][:, :], start=True, stop=False)
                        pe.matmul(ps_s[u % 2][:, :], query, latT[1][:, :], start=False, stop=True).then_inc(s_ready, 1)
                    if live(m, TLAG):
                        pe.wait_ge(scaled, g - (TLAG - 1))
                        pe.wait_ge(pT_ready, g - (TLAG - 1))
                        for t in range(TB):
                            ins = pe.transpose(ps_p[(u - TLAG) % 2][:, t, :], prob[(u - TLAG) % 4][:, t * P:(t + 1) * P],
                                               k.ident[:, :])
                        ins.then_inc(pT_raw, 1)
                    for t in range(TB):
                        pair = pair_at(m, u, i, VLAG + t)
                        if pair is None:
                            continue
                        par = place(u, VLAG + t)[0]
                        if t == 0:
                            pe.wait_ge(pT_ready, b * NU + pair * UP + (UP + 2))
                            pe.wait_ge(o_copied, b * PAIRS + pair + 1)
                        for hh in range(2):
                            ins = pe.matmul(ps_v[par][hh * LAT:(hh + 1) * LAT, :], lat[:, t, :], pT[par][:, hh, t, :],
                                            start=(t == 0), stop=(t == TB - 1))
                        if t == TB - 1:
                            ins.then_inc(v_ready, 1)

                steps(pe, step)
                pe.wait_ge(o_copied, b * PAIRS + (PAIRS + 2))
                for t in range(TB):
                    if t >= 2:
                        pe.wait_ge(out_used, b * TB + (t - 1))
                    for p in range(PAIRS):
                        ins = pe.matmul(ps_s[t % 2][:, 0:D], oT[:, p, t * P:(t + 1) * P], k.mix[:, p, :],
                                        start=(p == 0), stop=(p == PAIRS - 1))
                    ins.then_inc(out_ready, 1)

        @block.scalar
        def _(act):
            row_std(act, k)
            with act.Fori(0, B) as b:
                def use(m):
                    act.wait_ge(bank_ready[m % 2], b * QB + (m // 2 + 1))
                    return bank[m % 2]

                for j in range(TB):
                    act.activation(xT[:, :, j * P:(j + 1) * P], use(TR + j)[:, 0:D].rearrange("p (c t) -> p c t", c=DC),
                                   ACT.Copy).then_inc(bank_free[j % 2], 1)
                act.activation(latT[0][:, :], use(LATT), ACT.Copy).then_inc(high_ready, 1)
                act.activation(lat[:, :, :], use(LATK)[:, 0:TB * LAT].rearrange("p (t l) -> p t l", l=LAT),
                               ACT.Copy).then_inc(bank_free[LATK % 2], 1)
                for p in range(PAIRS):
                    src = use(Q + p)
                    act.activation(qa[0:LAT, 2 * p, :], src[0:LAT, :], ACT.Copy)
                    act.activation(qa[LAT:P, 2 * p + 1, :], src[LAT:P, :], ACT.Copy).then_inc(high_ready, 1)

                def step(m, u, i):
                    g = b * NU + m
                    if live(m, TLAG):
                        par, tile, hh = place(u, TLAG)
                        act.wait_ge(pT_raw, g - (TLAG - 1))
                        act.activation(pT[par][:, hh, :, tile * P:(tile + 1) * P], ps_p[(u - TLAG) % 2][:, :, :],
                                       ACT.Copy).then_inc(pT_ready, 1)
                    if live(m, 0):
                        act.wait_ge(nmax_ready, g + 1)
                        act.activation(prob[u % 4][:, :], ps_s[u % 2][:, :], ACT.Exp, bias=nmax[:, u % 2:u % 2 + 1],
                                       scale=SCALE, accum_out=rsum[:, u % 4:u % 4 + 1]).then_inc(p_ready, 1)
                    pair = pair_at(m, u, i, OLAG)
                    if pair is not None:
                        act.wait_ge(v_ready, b * PAIRS + pair + 1)
                        act.activation(oT[:, pair, :], ps_v[place(u, OLAG)[0]][:, :], ACT.Copy).then_inc(o_copied, 1)

                steps(act, step)

        @block.gpsimd
        def _(pool):
            for sem in bank_free:
                pool.sem_inc(sem, 1)
            for sem in (p_ready, pT_ready, o_copied):
                pool.sem_inc(sem, 2)
            with pool.Fori(0, B) as b:
                def stage(i, par):
                    pair = i * 2 + par
                    pool_copy(pool, k, qs[par][:, :, :], qa[:, bass.ds(pair * 2, 2), :].bitcast(F32)).then_inc(q_staged, 1)

                for par in range(2):
                    pool.wait_ge(bank_free[(Q + par) % 2], b * QB + ((Q + par) // 2 + 2))
                    pool.sem_inc(k.sem("passed"), 1)
                    stage(0, par)
                for m in range(Q + PAIRS - 2, Q + PAIRS):
                    pool.wait_ge(bank_free[m % 2], b * QB + (m // 2 + 2))
                    pool.sem_inc(k.sem("passed"), 1)
                with pool.Fori(1, PAIRS // 2) as i:
                    for par in range(2):
                        pool.wait_ge(s_ready, b * NU + i * U2 + (par - 1) * UP)
                        pool.sem_inc(k.sem("passed"), 1)
                        stage(i, par)

        @block.vector
        def _(dve):
            row_stats(dve, k)
            row_rstd(dve, k)
            with dve.Fori(0, B) as b:
                for j in range(TB):
                    if j >= 2:
                        dve.wait_ge(bank_ready[j % 2], b * QB + j // 2)
                    layernorm(dve, k, b * TB + j, xn[j % 2][:, :], xn_ready)
                dve.wait_ge(high_ready, b * (PAIRS + 1) + 1)
                dve.tensor_tensor(latT[1][:, :], bank[LATT % 2], latT[0][:, :].bitcast(F32),
                                  ALU.subtract).then_inc(bank_free[LATT % 2], 1)
                for p in range(PAIRS):
                    src = bank[(Q + p) % 2]
                    dve.wait_ge(high_ready, b * (PAIRS + 1) + (p + 2))
                    dve.tensor_tensor(qa[LAT:P, 2 * p, :], src[0:LAT, :], qa[0:LAT, 2 * p, :].bitcast(F32), ALU.subtract)
                    dve.tensor_tensor(qa[0:LAT, 2 * p + 1, :], src[LAT:P, :], qa[LAT:P, 2 * p + 1, :].bitcast(F32),
                                      ALU.subtract).then_inc(bank_free[(Q + p) % 2], 1)

                def step(m, u, i):
                    g = b * NU + m
                    if live(m, 0):
                        v = slice(u % 2, u % 2 + 1)
                        dve.wait_ge(s_ready, g + 1)
                        dve.tensor_reduce(raw[:, v], ps_s[u % 2][:, :], AX, ALU.max, negate=True).then_inc(max_steps, 1)
                        dve.wait_ge(max_steps, g + 1)
                        dve.tensor_scalar(nmax[:, v], raw[:, v], SCALE, None, ALU.mult).then_inc(nmax_ready, 1)
                    if live(m, 1):
                        v, w = (u - 1) % 2, (u - 1) % 4
                        dve.wait_ge(p_ready, g + 2)
                        dve.reciprocal(rinv[:, v:v + 1], rsum[:, w:w + 1]).then_inc(inv_steps, 1)
                        dve.wait_ge(inv_steps, g)
                        dve.tensor_scalar(prob[w][:, :], prob[w][:, :], rinv[:, v:v + 1], None, ALU.mult)\
                           .then_inc(scaled, 1)

                steps(dve, step)
                for t in range(TB):
                    x = k.X[:, b * TB + t, :]
                    dve.wait_ge(out_ready, b * TB + (t + 1))
                    dve.tensor_tensor(x, ps_s[t % 2][:, 0:D], x, ALU.add).then_inc(out_used, 1)
    k.norms += 1


def expert_layer(nc, k, r):
    with ExitStack() as ctx:
        k.xnT = ctx.enter_context(nc.sbuf_tensor(f"xnT{r}", [P, DC, N], F32))
        route(nc, k, r)
        routed_experts(nc, k, r)
        shared_and_combine(nc, k, r)


def macaron(nc, w, out):
    with ExitStack() as ctx:
        k = Kit(nc, ctx)
        Steps.passed = k.sem("passed")
        k.w, k.norms = w, 0
        k.X = k.sb("x", [P, NT, D])
        k.row_raw = k.sb("row_raw", [P, NT, 6])
        k.row_mv = k.sb("row_mv", [P, NT, 2])
        k.row_rstd = k.sb("row_rstd", [P, NT])
        k.gateT = k.sb("gateT", [P, DC, E0])
        k.sguT = k.sb("sguT", [P, DC, 2 * MS])
        k.sdT = k.sb("sdT", [P, 3, D])
        k.wvg = k.sb("wvg", [P, DC, 2 * H0 * DV])
        k.wgk0 = k.sb("wgk0", [P, DC, LR])
        k.wgk1 = k.sb("wgk1", [LR, H0 * DK])
        k.bgk1 = k.sb("bgk1", [P, H0])
        k.wq0 = k.sb("wq0", [P, DC, H0 * DK])
        k.wk0 = k.sb("wk0", [P, DC, H0 * DK])
        k.wo0 = k.sb("wo0", [P, DC, D])
        k.gnorm_row = k.sb("gnorm_row", [1, DV])
        k.gnorm = k.sb("gnorm", [P, DV])
        k.wr1 = k.sb("wr1", [P, DC, E1])
        k.wkv1 = k.sb("wkv1", [P, DC, 2 * LAT])
        k.we1 = k.sb("we1", [P, DC, E1, D])
        k.be1 = k.sb("be1", [E1, D])
        k.absorb = k.sb("absorb", [P, DC, H1 * LAT])
        k.mix = k.sb("mix", [P, PAIRS, D])
        k.ident = k.sb("ident", [P, P])
        k.before_bf = k.sb("before_bf", [P, P], BF16)
        k.ones_bf = k.sb("ones_bf", [P, P], BF16)
        k.causal = k.sb("causal", [P, SUB])
        k.chunk_keep = k.sb("chunk_keep", [P, T])
        k.eps = k.sb("eps", [P, 1])
        k.zeros = k.sb("zeros", [P, P])
        k.last_slot = k.sb("last_slot", [E0, CAP])
        k.iota64 = k.sb("iota64", [P, E0])
        k.iota_slot = k.sb("iota_slot", [P, CAP])
        k.token = k.sb("token", [P, NT])
        k.token1 = k.sb("token1", [P, NT])
        k.member_sum = k.sb("member_sum", [P, 2, E0], BF16)
        k.weight = k.sb("weight", [P, NT, TOPK])
        k.slot = k.sb("slot", [P, NT, TOPK], U32)
        k.table = k.sb("table", [CAP, E0], U32)
        k.xn_rows = nc.dram_tensor("xn_rows", [N, D], F32, kind="Internal").ap()
        k.slot_rows = nc.dram_tensor("slot_rows", [E0 * CAP, D], F32, kind="Internal").ap()
        load_and_prepare(nc, k, w)
        expert_layer(nc, k, 0)
        linear_attention(nc, k)
        expert_layer(nc, k, 1)
        dense_experts(nc, k, 0)
        latent_attention(nc, k)
        dense_experts(nc, k, 1, store=out)


def arrange(a):
    import numpy as np

    c = np.ascontiguousarray
    gu = np.concatenate([a["L0_ffn_Wg"].transpose(0, 2, 1), a["L0_ffn_Wu"].transpose(0, 2, 1)], axis=2)
    return {
        "x": c(a["L0_attn_hidden_states"].reshape(N, D)),
        "wqT1": c(a["L1_attn_W_q"].T), "upT1": c(a["L1_attn_W_kv_up"].T), "wo1": c(a["L1_attn_W_o"]),
        "gateT": c(a["L0_ffn_gate_weight"].T),
        "sguT": c(np.concatenate([a["L0_ffn_Sg"].T, a["L0_ffn_Su"].T], axis=1)),
        "sdT": c(a["L0_ffn_Sd"].T),
        "wvg": c(np.concatenate([a["L0_attn_Wv"], a["L0_attn_Wg"]], axis=1)),
        "wgk0": c(a["L0_attn_Wgk0"]), "wgk1": c(a["L0_attn_Wgk1"]),
        "bgk1": c(a["L0_attn_bgk1"].reshape(H0, DK).T), "gnorm": c(a["L0_attn_g_norm_w"]),
        "wq0": c(a["L0_attn_Wq"]), "wk0": c(a["L0_attn_Wk"]), "wo0": c(a["L0_attn_Wo"]),
        "wr1": c(a["L1_ffn_Wr"]),
        "wkv1": c(np.concatenate([a["L1_attn_W_kv_down"], a["L1_attn_W_kv_down"]], axis=1)),
        "we1": c(a["L1_ffn_We"]), "be1": c(a["L1_ffn_be"]),
        "wgu0": c(gu.reshape(E0, DC, P, 2 * M0).transpose(0, 2, 1, 3)),
        "wdn0": c(a["L0_ffn_Wd"].transpose(0, 2, 1).reshape(E0, 2, MH, D).transpose(0, 2, 1, 3)),
    }


def build(nc, arrays):
    w = {n: nc.dram_tensor(n, a.shape, F32, kind="ExternalInput").ap() for n, a in arrays.items()}
    out = nc.dram_tensor("out", [N, D], F32, kind="ExternalOutput").ap()
    macaron(nc, w, out)


def kernel(**inputs):
    import concourse.bacc as bacc
    import numpy as np
    from concourse.bass_utils import run_bass_kernel_spmd

    arrays = arrange({n: np.asarray(a) for n, a in inputs.items()})
    nc = bacc.Bacc("TRN2", target_bir_lowering=False, num_devices=1)
    build(nc, arrays)
    result = run_bass_kernel_spmd(nc, [arrays], core_ids=[0])
    return result.results[0]["out"].reshape(B, T, D)
```

```python
from contextlib import ExitStack

import concourse.bass as bass
from concourse import mybir

ALU = mybir.AluOpType
ACT = mybir.ActivationFunctionType
AX = mybir.AxisListType.X
F32 = mybir.dt.float32
BF16 = mybir.dt.bfloat16
U32 = mybir.dt.uint32
F32R = mybir.dt.float32r

P = 128
B, T, D = 4, 512, 256
N = B * T
NT = N // P
TB = T // P
DC = D // P
EPS = 1e-5

E0, M0, TOPK, NG, TG, CAP = 64, 176, 6, 8, 3, 96
MH = 96
MHC = (0, M0 - MH)
AHEAD = 8
MS = 352
MSC = [(0, 128), (128, 128), (256, 96)]
H0, DK, DV, LR = 8, 128, 32, 16
GATE_NORM = 16.0
SUB = P
NSUB = T // SUB
E1 = 8
H1, DH, LAT = 16, 128, 64
PAIRS = H1 // 2


class Steps:

    passed = None

    def __init__(self, eng, sem, step, per):
        self.eng, self.sem, self.before, self.per, self.n = eng, sem, step * per, per, 0

    def mark(self, ins):
        ins.then_inc(self.sem, 1)
        self.n += 1

    def settle(self, back=0):
        self.eng.wait_ge(self.sem, self.before + self.n - back)

    def settle_apart(self):
        self.settle()
        self.eng.sem_inc(self.passed, 1)

    def close(self):
        assert self.n == self.per, (self.n, self.per)


class Kit:

    def __init__(self, nc, ctx):
        self.nc, self.ctx, self.sems = nc, ctx, {}

    def sb(self, name, shape, dt=F32):
        return self.ctx.enter_context(self.nc.sbuf_tensor("sb_" + name, shape, dt))

    def sem(self, name):
        if name not in self.sems:
            self.sems[name] = self.ctx.enter_context(self.nc.semaphore(name))
        return self.sems[name]


def scoped(nc, ctx):
    def sb(name, shape, dt=F32):
        return ctx.enter_context(nc.sbuf_tensor("sb_" + name, shape, dt))

    def ps(name, shape):
        width = 1
        for m in shape[1:]:
            width *= m
        bank = ctx.enter_context(nc.psum_tensor(name, [P, 512], F32))[0:shape[0], 0:width]
        if len(shape) == 3:
            return bank.rearrange("p (a b) -> p a b", a=shape[1])
        return bank
    return sb, ps


def row_stats(dve, k):
    done = k.sem("row_stats_steps")
    first = 2 * NT * k.norms
    for n in range(NT):
        dve.bn_stats(k.row_raw[:, n, :], k.X[:, n, :]).then_inc(done, 1)
    for n in range(NT):
        dve.wait_ge(done, first + n + 1)
        dve.bn_aggr(k.row_mv[:, n, :], k.row_raw[:, n, :]).then_inc(done, 1)


def row_std(act, k):
    act.wait_ge(k.sem("row_stats_steps"), 2 * NT * (k.norms + 1))
    act.activation(k.row_rstd[:, :], k.row_mv[:, :, 1], ACT.Sqrt, bias=k.eps[:, 0:1]).then_inc(k.sem("row_std_ready"), 1)


def row_rstd(dve, k):
    dve.wait_ge(k.sem("row_std_ready"), k.norms + 1)
    dve.reciprocal(k.row_rstd[:, :], k.row_rstd[:, :]).then_inc(k.sem("row_rstd_ready"), 1)
    dve.wait_ge(k.sem("row_rstd_ready"), k.norms + 1)


def layernorm(dve, k, n, out, ready):
    dve.tensor_scalar(out, k.X[:, n, :], k.row_mv[:, n, 0:1], k.row_rstd[:, bass.ds(n, 1)],
                      ALU.subtract, ALU.mult).then_inc(ready, 1)


def pool_copy(pool, k, out, in_):
    pool.sem_inc(k.sem("passed"), 1)
    return pool.tensor_copy(out, in_)


def load_and_prepare(nc, k, w):
    loaded_x, loaded_w0, loaded_w1 = k.sem("x_loaded"), k.sem("w0_loaded"), k.sem("w1_loaded")
    prep_loaded, made = k.sem("prep_loaded"), k.sem("constants_made")
    pre_ready, pre_free = k.sem("prep_psum_ready"), k.sem("prep_psum_free")
    with ExitStack() as ctx:
        sb, ps = scoped(nc, ctx)
        wqT = sb("wqT", [P, H1, D])
        upT = sb("upT", [P, H1, LAT])
        wo1 = sb("wo1", [P, H1, D])
        pa = [ps(f"prep_psum{u}", [P, 512]) for u in range(2)]
        block = ctx.enter_context(nc.Block())

        @block.sync
        def _(sp):
            sp.dma_start(k.X[:, :, :], w["x"].rearrange("(n p) d -> p n d", p=P)).then_inc(loaded_x, 16)
            sp.dma_start(wqT[:, :, :], w["wqT1"].rearrange("(h p) d -> p h d", p=DH)).then_inc(prep_loaded, 16)
            sp.dma_start(upT[:, :, :], w["upT1"].rearrange("(h p) d -> p h d", p=DH)).then_inc(prep_loaded, 16)
            sp.dma_start(wo1[:, :, :], w["wo1"].rearrange("(h p) d -> p h d", p=DH)).then_inc(prep_loaded, 16)
            for dst, name in ((k.gateT, "gateT"), (k.sguT, "sguT"), (k.wvg, "wvg"),
                              (k.wq0, "wq0"), (k.wk0, "wk0"), (k.wo0, "wo0")):
                sp.dma_start(dst[:, :, :], w[name].rearrange("(c p) n -> p c n", p=P)).then_inc(loaded_w0, 16)
            for c, (m0, m) in enumerate(MSC):
                sp.dma_start(k.sdT[0:m, c, :], w["sdT"][m0:m0 + m, :]).then_inc(loaded_w0, 16)
            sp.wait_ge(made, 3)
            sp.dma_start(k.wgk0[:, :, 0:LR], w["wgk0"].rearrange("(c p) n -> p c n", p=P)).then_inc(loaded_w0, 16)
            sp.dma_start(k.wgk1[0:LR, :], w["wgk1"]).then_inc(loaded_w0, 16)
            sp.dma_start(k.bgk1[:, :], w["bgk1"]).then_inc(loaded_w0, 16)
            sp.dma_start(k.gnorm_row[:, :], w["gnorm"].rearrange("(a n) -> a n", a=1)).then_inc(k.sem("gnorm_loaded"), 16)
            for dst, name in ((k.wr1, "wr1"), (k.wkv1, "wkv1")):
                sp.dma_start(dst[:, :, :], w[name].rearrange("(c p) n -> p c n", p=P)).then_inc(loaded_w1, 16)
            for c in range(DC):
                sp.dma_start(k.we1[:, c, :, :], w["we1"].rearrange("e (c p) f -> c p e f", p=P)[c]).then_inc(loaded_w1, 16)
            sp.dma_start(k.be1[0:E1, :], w["be1"]).then_inc(loaded_w1, 16)

        @block.gpsimd
        def _(pool):
            s = Steps(pool, made, 0, 23)
            s.mark(pool.memset(k.wgk0[:, :, :], 0.0))
            s.mark(pool.memset(k.wgk1[:, :], 0.0))
            s.mark(pool.memset(k.be1[:, :], 0.0))
            s.mark(pool.memset(k.ident[:, :], 0.0))
            s.mark(pool.memset(k.before_bf[:, :], 1.0))
            s.mark(pool.memset(k.ones_bf[:, :], 1.0))
            s.mark(pool.memset(k.causal[:, :], 1.0))
            s.mark(pool.memset(k.chunk_keep[:, :], 1.0))
            s.mark(pool.memset(k.last_slot[:, :], 0.0))
            s.mark(pool.memset(k.eps[:, :], EPS))
            s.mark(pool.memset(k.zeros[:, :], 0.0))
            s.settle()
            s.mark(pool.affine_select(out=k.ident[:, :], in_=k.ident[:, :], compare_op=ALU.not_equal, fill=1.0,
                                      base=0, pattern=[[-1, P]], channel_multiplier=1))
            s.mark(pool.affine_select(out=k.before_bf[:, :], in_=k.before_bf[:, :], compare_op=ALU.is_gt, fill=0.0,
                                      base=0, pattern=[[1, P]], channel_multiplier=-1))
            s.settle()
            s.mark(pool.affine_select(out=k.causal[:, :], in_=k.causal[:, :], compare_op=ALU.is_ge, fill=0.0,
                                      base=0, pattern=[[1, SUB]], channel_multiplier=-1))
            s.settle()
            s.mark(pool.memset(k.chunk_keep[:, :].rearrange("p (c s) -> p c s", s=SUB)[:, :, 0:1], 0.0))
            s.mark(pool.iota(k.iota64[:, :], pattern=[[1, E0]], base=0, channel_multiplier=0,
                             allow_small_or_imprecise_dtypes=True))
            s.mark(pool.iota(k.iota_slot[:, :], pattern=[[1, CAP]], base=0, channel_multiplier=0,
                             allow_small_or_imprecise_dtypes=True))
            s.mark(pool.iota(k.token_part[:, 0, :], pattern=[[0, NT // 2], [P, 2]], base=0, channel_multiplier=1,
                             allow_small_or_imprecise_dtypes=True))
            s.mark(pool.iota(k.token_part[:, 1, :], pattern=[[2 * P, NT // 2], [0, 2]], base=0, channel_multiplier=0,
                             allow_small_or_imprecise_dtypes=True))
            s.mark(pool.iota(k.token1[:, :], pattern=[[P, NT]], base=1, channel_multiplier=1,
                             allow_small_or_imprecise_dtypes=True))
            s.settle()
            s.mark(pool.memset(k.iota_slot[:, CAP - 1:CAP], -1.0))
            pool.wait_ge(k.sem("gnorm_loaded"), 16)
            s.mark(pool.partition_broadcast(k.gnorm[:, :], k.gnorm_row[:, :], channels=P))
            s.settle()
            s.mark(pool.memset(k.member_sum[:, :, :], 0.0))
            s.settle()
            s.close()

        @block.tensor
        def _(pe):
            pe.wait_ge(prep_loaded, 48)
            n = 0
            for h0 in range(0, H1, 8):
                for c in range(DC):
                    if n >= 2:
                        pe.wait_ge(pre_free, n - 1)
                    for h in range(h0, h0 + 8):
                        last = pe.matmul(pa[n % 2][:, (h - h0) * LAT:(h - h0 + 1) * LAT], wqT[:, h, c * P:(c + 1) * P],
                                         upT[:, h, :], start=True, stop=True)
                    last.then_inc(pre_ready, 1)
                    n += 1
            for p in range(PAIRS):
                pe.wait_ge(pre_free, n - 1)
                for hh in range(2):
                    h = 2 * p + hh
                    last = pe.matmul(pa[n % 2][hh * LAT:(hh + 1) * LAT, 0:D], upT[:, h, :], wo1[:, h, :],
                                     start=True, stop=True)
                last.then_inc(pre_ready, 1)
                n += 1

        @block.vector
        def _(dve):
            n = 0
            for h0 in range(0, H1, 8):
                for c in range(DC):
                    dve.wait_ge(pre_ready, n + 1)
                    dve.tensor_copy(k.absorb[:, c, h0 * LAT:(h0 + 8) * LAT], pa[n % 2][:, :]).then_inc(pre_free, 1)
                    n += 1
            for p in range(PAIRS):
                dve.wait_ge(pre_ready, n + 1)
                dve.tensor_copy(k.mix[:, p, :], pa[n % 2][:, 0:D]).then_inc(pre_free, 1)
                n += 1


def dense_experts(nc, k, r, store=None, combine=None):
    stats_done, rstd_ready = k.sem("d_stats_steps"), k.sem("d_rstd_ready")
    xn_ready, xT_raw, xT_ready = k.sem("d_xn_ready"), k.sem("d_xT_psum_ready"), k.sem("d_xT_ready")
    high_ready, low_ready = k.sem("d_xT_high_ready"), k.sem("d_xT_low_ready")
    we_high, we_low = k.sem("d_we_high_ready"), k.sem("d_we_low_ready")
    logits_ready, gate_ready = k.sem("d_logits_ready"), k.sem("d_gate_ready")
    gap_ready, egap_ready = k.sem("d_logit_gap_ready"), k.sem("d_exp_gap_ready")
    gateT_raw, gateT_ready = k.sem("d_gateT_psum_ready"), k.sem("d_gateT_ready")
    pair_ready, pair_free = k.sem("d_pair_ready"), k.sem("d_pair_free")
    bias_ready, out_ready, stored = k.sem("d_bias_ready"), k.sem("d_out_ready"), k.sem("d_stored")
    rows_got = [k.sem(f"c_rows_got{u}") for u in range(2)]
    NP = E1 // 2
    with ExitStack() as ctx:
        sb, ps = scoped(nc, ctx)
        we = [sb(f"d{r}_we_{part}", [P, DC, E1, D], F32R) for part in ("high", "low")]
        lnv = [sb(f"d{r}_lnv{u}", [P, 1]) for u in range(2)]
        rstd = [sb(f"d{r}_rstd{u}", [P, 1]) for u in range(2)]
        raw = [sb(f"d{r}_raw{u}", [P, 6]) for u in range(2)]
        mv = [sb(f"d{r}_mv{u}", [P, 2]) for u in range(2)]
        xn = [sb(f"d{r}_xn{u}", [P, D]) for u in range(2)]
        xT = [sb(f"d{r}_xT{u}", [P, DC, P]) for u in range(2)]
        xTs = [[sb(f"d{r}_xT_{part}{u}", [P, DC, P], F32R) for part in ("high", "low")] for u in range(2)]
        top = sb(f"d{r}_top", [P, 8])
        top_i = sb(f"d{r}_top_i", [P, 8], U32)
        top_f = sb(f"d{r}_top_f", [P, 2])
        gap = sb(f"d{r}_gap", [P, 1])
        egap = sb(f"d{r}_egap", [P, 1])
        den = sb(f"d{r}_den", [P, 1])
        w1 = sb(f"d{r}_w1", [P, 1])
        w2 = sb(f"d{r}_w2", [P, 1])
        g1 = sb(f"d{r}_g1", [P, E1])
        g2 = sb(f"d{r}_g2", [P, E1])
        gate = [sb(f"d{r}_gate{u}", [P, P]) for u in range(2)]
        gateT = sb(f"d{r}_gateT", [P, P])
        acc = sb(f"d{r}_acc", [P, D])
        if combine is not None:
            rows = [[sb(f"c{combine}_rows{u}_{j}", [P, D]) for j in range(TOPK)] for u in range(2)]
            at = [sb(f"c{combine}_at{u}", [P, TOPK], U32) for u in range(2)]
        ps_x = ps(f"d{r}_ps_x", [P, DC, P])
        ps_r = ps(f"d{r}_ps_r", [P, E1])
        ps_g = ps(f"d{r}_ps_g", [P, P])
        ps_b = ps(f"d{r}_ps_b", [P, D])
        ps_e = [ps(f"d{r}_ps_e{j}", [P, 2, D]) for j in range(NP)]
        block = ctx.enter_context(nc.Block())

        def live(n):
            return not isinstance(n, int) or n < NT

        def tiles(eng, body):
            with eng.Fori(0, NT // 2 - 2) as i:
                for u in range(2):
                    body(i * 2 + u, u)
            for n in range(NT - 4, NT):
                body(n, n % 2)

        @block.tensor
        def _(pe):
            pe.wait_ge(k.sem("w1_loaded"), 16 * 5)

            def transposed(n, u):
                g = n + r * NT
                pe.wait_ge(xn_ready, g + 1)
                pe.wait_ge(xT_ready, g + 1)
                pe.wait_ge(high_ready, g + 1)
                for c in range(DC):
                    ins = pe.transpose(ps_x[:, c, :], xn[u][:, c * P:(c + 1) * P], k.ident[:, :])
                ins.then_inc(xT_raw, 1)

            def logits(n, u):
                g = n + r * NT
                pe.wait_ge(xT_ready, g + 2)
                for c in range(DC):
                    ins = pe.matmul(ps_r[:, :], xT[u][:, c, :], k.wr1[:, c, :], start=(c == 0), stop=(c == DC - 1))
                ins.then_inc(logits_ready, 1)

            def pair(n, u, j):
                g = n + r * NT
                pe.wait_ge(pair_free, g * NP + (j + 1))
                m = 0
                for xpart, wpart in ((0, 0), (0, 1), (1, 0)):
                    for c in range(DC):
                        ins = pe.matmul(ps_e[j][:, :, :], xTs[u][xpart][:, c, :], we[wpart][:, c, 2 * j:2 * j + 2, :],
                                        start=(m == 0), stop=(m == 3 * DC - 1))
                        m += 1
                ins.then_inc(pair_ready, 1)

            def tile(n, u):
                g = n + r * NT
                pe.wait_ge(high_ready, g + 2)
                pe.wait_ge(low_ready, g + 1)
                pair(n, u, 0)
                if live(n + 1):
                    transposed(n + 1, 1 - u)
                pair(n, u, 1)
                pe.wait_ge(gate_ready, g + 1)
                pe.transpose(ps_g[:, :], gate[u][:, :], k.ident[:, :]).then_inc(gateT_raw, 1)
                if live(n + 1):
                    logits(n + 1, 1 - u)
                pair(n, u, 2)
                pe.wait_ge(gateT_ready, g + 1)
                pe.wait_ge(out_ready, g + 1)
                pe.matmul(ps_b[:, :], gateT[:, :], k.be1[:, :], start=True, stop=True).then_inc(bias_ready, 1)
                pair(n, u, 3)

            transposed(0, 0)
            logits(0, 0)
            pe.wait_ge(we_low, (r + 1) * DC)
            tiles(pe, tile)

        @block.scalar
        def _(act):
            def copies(n, u):
                g = n + r * NT
                act.wait_ge(xT_raw, g + 1)
                act.activation(xT[u][:, :, :], ps_x[:, :, :], ACT.Copy).then_inc(xT_ready, 1)
                act.activation(xTs[u][0][:, :, :], ps_x[:, :, :], ACT.Copy).then_inc(high_ready, 1)

            def inverse_deviation(n, u):
                g = n + r * NT
                act.wait_ge(stats_done, (g + 1) * 2)
                s = Steps(act, k.sem("d_ln_steps"), g, 1)
                s.mark(act.activation(lnv[u][:, :], mv[u][:, 1:2], ACT.Ln, bias=k.eps[:, 0:1]))
                s.settle()
                s.close()
                act.activation(rstd[u][:, :], lnv[u][:, :], ACT.Exp, scale=-0.5).then_inc(rstd_ready, 1)

            def gap_exp(n):
                g = n + r * NT
                act.wait_ge(gap_ready, g + 1)
                act.activation(egap[:, :], gap[:, :], ACT.Exp).then_inc(egap_ready, 1)

            def tile(n, u):
                g = n + r * NT
                if live(n + 1):
                    copies(n + 1, 1 - u)
                act.wait_ge(gateT_raw, g + 1)
                act.activation(gateT[:, :], ps_g[:, :], ACT.Copy).then_inc(gateT_ready, 1)
                if live(n + 1):
                    gap_exp(n + 1)
                if live(n + 3):
                    inverse_deviation(n + 3, 1 - u)

            act.preload_act_table_set("natural_log_exp_and_others")
            act.wait_ge(k.sem("w1_loaded"), 16 * 5)
            for c in range(DC):
                act.activation(we[0][:, c, :, :], k.we1[:, c, :, :], ACT.Copy).then_inc(we_high, 1)
            for n in range(3):
                if n == 2:
                    copies(0, 0)
                    gap_exp(0)
                inverse_deviation(n, n % 2)
            tiles(act, tile)

        if combine is not None:
            @block.gpsimd
            def _(pool):
                gather_rows(pool, k, combine, rows, at)

        @block.vector
        def _(dve):
            if r == 0:
                dve.sem_inc(pair_free, NP)
                for sem in (xT_ready, high_ready, out_ready):
                    dve.sem_inc(sem, 1)
            zeroed = k.sem("d_gates_zeroed")
            for u in range(2):
                dve.memset(gate[u][:, :], 0.0).then_inc(zeroed, 1)
            dve.wait_ge(zeroed, 2 * (r + 1))

            def statistics(n, u):
                g = n + r * NT
                x = k.X[:, n, :]
                if combine is not None:
                    add_rows(dve, k, combine, n, rows[u], rows_got[u], u)
                s = Steps(dve, stats_done, g, 2)
                dve.sem_inc(s.passed, 1)
                s.mark(dve.bn_stats(raw[u][:, :], x))
                s.settle_apart()
                s.mark(dve.bn_aggr(mv[u][:, :], raw[u][:, :]))
                s.close()

            def normalise(n, u):
                g = n + r * NT
                dve.wait_ge(rstd_ready, g + 1)
                dve.tensor_scalar(xn[u][:, :], k.X[:, n, :], mv[u][:, 0:1], rstd[u][:, 0:1],
                                  ALU.subtract, ALU.mult).then_inc(xn_ready, 1)

            def leaders(n, u):
                g = n + r * NT
                s = Steps(dve, k.sem("d_leader_steps"), g, 3)
                dve.wait_ge(high_ready, g + 2)
                dve.tensor_tensor(xTs[u][1][:, :, :], xT[u][:, :, :], xTs[u][0][:, :, :].bitcast(F32),
                                  ALU.subtract).then_inc(low_ready, 1)
                dve.wait_ge(logits_ready, g + 1)
                dve.sem_inc(s.passed, 1)
                s.mark(dve.max(top[:, :], ps_r[:, :]))
                s.settle_apart()
                s.mark(dve.max_index(top_i[:, :], top[:, :], ps_r[:, :]))
                dve.tensor_tensor(gap[:, :], top[:, 1:2], top[:, 0:1], ALU.subtract).then_inc(gap_ready, 1)
                s.settle()
                s.mark(dve.tensor_copy(top_f[:, :], top_i[:, 0:2]))
                s.settle()
                s.close()

            def gates(n, u, between):
                g = n + r * NT
                s = Steps(dve, k.sem("d_gate_steps"), g, 5)
                dve.wait_ge(egap_ready, g + 1)
                s.mark(dve.tensor_scalar(den[:, :], egap[:, :], 2.0, 2.0, ALU.mult, ALU.add))
                between[0]()
                s.settle()
                s.mark(dve.reciprocal(w1[:, :], den[:, :]))
                between[1]()
                s.settle()
                s.mark(dve.tensor_scalar(w2[:, :], egap[:, :], w1[:, 0:1], None, ALU.mult))
                s.mark(dve.tensor_scalar(g1[:, :], k.iota64[:, 0:E1], top_f[:, 0:1], w1[:, 0:1], ALU.is_equal, ALU.mult))
                between[2]()
                s.settle()
                s.mark(dve.tensor_scalar(g2[:, :], k.iota64[:, 0:E1], top_f[:, 1:2], w2[:, 0:1], ALU.is_equal, ALU.mult))
                between[3]()
                s.settle()
                s.close()
                dve.tensor_tensor(gate[u][:, 0:E1], g1[:, :], g2[:, :], ALU.add).then_inc(gate_ready, 1)

            even_added = k.sem("d_even_steps")

            def weigh_even(n, u, j):
                g = n + r * NT
                x = k.X[:, n, :]
                dve.wait_ge(pair_ready, g * NP + (j + 1))
                if j:
                    dve.wait_ge(even_added, g * NP + j)
                dve.scalar_tensor_tensor(out=x, in0=ps_e[j][:, 0, :], scalar=gate[u][:, 2 * j:2 * j + 1], in1=x,
                                         op0=ALU.mult, op1=ALU.add).then_inc(even_added, 1)

            def weigh_odd(n, u, j):
                g = n + r * NT
                src, w = ps_e[j][:, 1, :], gate[u][:, 2 * j + 1:2 * j + 2]
                if j == 0:
                    ins = dve.tensor_scalar(acc[:, :], src, w, None, ALU.mult)
                else:
                    dve.wait_ge(pair_free, g * NP + (NP + j))
                    ins = dve.scalar_tensor_tensor(out=acc[:, :], in0=src, scalar=w, in1=acc[:, :],
                                                   op0=ALU.mult, op1=ALU.add)
                ins.then_inc(pair_free, 1)

            def tile(n, u):
                g = n + r * NT
                x = k.X[:, n, :]
                dve.wait_ge(gate_ready, g + 1)
                weigh_even(n, u, 0)
                weigh_odd(n, u, 0)
                if live(n + 2):
                    normalise(n + 2, u)
                weigh_even(n, u, 1)
                weigh_odd(n, u, 1)
                if live(n + 1):
                    leaders(n + 1, 1 - u)
                weigh_even(n, u, 2)
                if live(n + 3):
                    statistics(n + 3, 1 - u)
                rest = [lambda: weigh_odd(n, u, 2), lambda: weigh_even(n, u, 3), lambda: weigh_odd(n, u, 3)]

                def add_up():
                    dve.wait_ge(k.sem("d_even_steps"), g * NP + NP)
                    dve.wait_ge(pair_free, g * NP + 2 * NP)
                    dve.tensor_tensor(x, acc[:, :], x, ALU.add).then_inc(k.sem("d_sum_steps"), 1)

                if live(n + 1):
                    gates(n + 1, 1 - u, rest + [add_up])
                else:
                    for part in rest + [add_up]:
                        part()
                dve.wait_ge(bias_ready, g + 1)
                dve.wait_ge(k.sem("d_sum_steps"), g + 1)
                dve.tensor_tensor(x, ps_b[:, :], x, ALU.add).then_inc(out_ready, 1)

            statistics(0, 0)
            statistics(1, 1)
            normalise(0, 0)
            normalise(1, 1)
            for c in range(DC):
                dve.wait_ge(we_high, r * DC + c + 1)
                dve.tensor_tensor(we[1][:, c, :, :], k.we1[:, c, :, :], we[0][:, c, :, :].bitcast(F32),
                                  ALU.subtract).then_inc(we_low, 1)
            leaders(0, 0)
            statistics(2, 0)
            gates(0, 0, [lambda: None] * 4)
            tiles(dve, tile)

        if store is not None:
            @block.sync
            def _(sp):
                with sp.Fori(0, NT) as n:
                    sp.wait_ge(out_ready, n + (r * NT + 2))
                    sp.dma_start(store.rearrange("(n p) d -> n p d", p=P)[n], k.X[:, n, :]).then_inc(stored, 16)
                sp.wait_ge(stored, 16 * NT)


def route(nc, k, r):
    xn_ready, xT_raw, xT_ready = k.sem("r_xn_ready"), k.sem("r_xT_psum_ready"), k.sem("r_xT_ready")
    xn_stored = [k.sem(f"r_xn_stored{u}") for u in range(2)]
    xnT_ready = k.sem("r_xnT_ready")
    logits_ready, nmax_ready, exp_ready = k.sem("r_logits_ready"), k.sem("r_neg_max_ready"), k.sem("r_exp_ready")
    member_ready, pos_ready = k.sem("r_member_ready"), k.sem("r_positions_ready")
    posf_ready, onehot_ready, onehot_free = k.sem("r_position_k_ready"), k.sem("r_onehots_ready"), k.sem("r_onehots_free")
    slots_ready, table_done = k.sem("r_slots_ready"), k.sem("r_table_done")
    begin_ready, lastT_ready, last_ready = k.sem("r_begin_ready"), k.sem("r_lastT_ready"), k.sem("r_last_ready")
    gu_ready, gu_copied, silu_ready = k.sem("s_gate_up_ready"), k.sem("s_gate_up_copied"), k.sem("s_silu_ready")
    hid_ready, down_ready, down_used = k.sem("s_hidden_ready"), k.sem("s_down_ready"), k.sem("s_down_used")
    G = 4
    GN = NT // G
    GT = G * P
    with ExitStack() as ctx:
        sb, ps = scoped(nc, ctx)
        xn = [sb(f"r{r}_xn{u}", [P, D]) for u in range(2)]
        xT = [sb(f"r{r}_xT{u}", [P, DC, P]) for u in range(2)]
        xnT = sb(f"r{r}_xnT", [P, DC, N])
        nmax = sb(f"r{r}_nmax", [P, 1])
        ex = sb(f"r{r}_ex", [P, E0])
        esum = sb(f"r{r}_esum", [P, 1])
        rsum = sb(f"r{r}_rsum", [P, 1])
        score = sb(f"r{r}_score", [P, E0])
        gmax = sb(f"r{r}_gmax", [P, NG])
        gtop = sb(f"r{r}_gtop", [P, 8])
        gtop_i = sb(f"r{r}_gtop_i", [P, 8], U32)
        gtop_f = sb(f"r{r}_gtop_f", [P, TG])
        ghot = sb(f"r{r}_ghot", [P, TG, NG])
        gmask = sb(f"r{r}_gmask", [P, NG])
        masked = sb(f"r{r}_masked", [P, E0])
        top = sb(f"r{r}_top", [P, 8])
        top_i = sb(f"r{r}_top_i", [P, 8], U32)
        top_f = sb(f"r{r}_top_f", [P, TOPK])
        hot = [sb(f"r{r}_hot{u}", [P, TOPK, E0]) for u in range(2)]
        hot_tok = [sb(f"r{r}_hot_tok{u}", [P, TOPK, 2, E0], BF16) for u in range(2)]
        hot_pos = [sb(f"r{r}_hot_pos{u}", [P, TOPK, CAP], BF16) for u in range(2)]
        member = [sb(f"r{r}_member{u}", [P, E0], BF16) for u in range(2)]
        last = sb(f"r{r}_last", [P, E0])
        picked = sb(f"r{r}_picked", [P, TOPK, E0])
        posf = [sb(f"r{r}_posf{u}", [P, TOPK]) for u in range(2)]
        slot_c = sb(f"r{r}_slot_c", [P, TOPK])
        high = sb(f"r{r}_high", [CAP, E0])
        last_col = sb(f"r{r}_last_col", [E0, 1])
        sgate = sb(f"s{r}_gate", [P, 3, GT])
        sup = sb(f"s{r}_up", [P, 3, GT])
        ps_x = ps(f"r{r}_ps_x", [P, DC, P])
        ps_r = [ps(f"r{r}_ps_r{u}", [P, E0]) for u in range(2)]
        ps_p = [ps(f"r{r}_ps_p{u}", [P, E0]) for u in range(2)]
        ps_t = ps(f"r{r}_ps_t", [P, 2 * E0])
        ps_s = [ps(f"s{r}_ps{which}", [P, GT]) for which in range(2)]
        block = ctx.enter_context(nc.Block())
        kept_table = ps_t[0:CAP, :]
        LAST = NT + G
        PEEL = 2

        def spread(ap, n, m):
            return ap.unsqueeze(2).to_broadcast([P, n, m])

        def repeat(ap, n, m):
            return ap.unsqueeze(1).to_broadcast([P, n, m])

        def live(m, lag):
            return not isinstance(m, int) or 0 <= m - lag < NT

        def steps(eng, body):
            for m in range(PEEL * G):
                body(m, m % G, m // G - 1)
            with eng.Fori(PEEL, GN) as i:
                for t in range(G):
                    body(i * G + t, t, i - 1)
            for m in range(NT, LAST + 1):
                body(m, m % G, m // G - 1)

        def group(q, lag=0):
            return not isinstance(q, int) or 0 <= q - lag < GN

        @block.sync
        def _(sp):
            if r == 0:
                for u in range(2):
                    sp.sem_inc(xn_stored[u], 16)
            for e in range(AHEAD):
                sp.dma_start(k.wgu[e][:, :, :], k.w["wgu0"][e]).then_inc(k.sem(f"e_gate_up_got{e}"), 16)
                sp.dma_start(k.wdn[e][:, :, :], k.w["wdn0"][e]).then_inc(k.sem(f"e_down_got{e}"), 16)
            with sp.Fori(0, NT // 2) as i:
                for u in range(2):
                    n = i * 2 + u
                    sp.wait_ge(xn_ready, n + (r * NT + 1))
                    sp.dma_start(k.xn_rows.rearrange("(n p) d -> n p d", p=P)[n], xn[u][:, :]).then_inc(xn_stored[u], 16)

        @block.tensor
        def _(pe):
            pe.wait_ge(k.sem("w0_loaded"), 16 * 12)
            if r == 0:
                pe.sem_inc(onehot_free, 2)
                pe.sem_inc(gu_copied, 1)
                pe.sem_inc(down_ready, 1)
                pe.sem_inc(down_used, 1)
            pe.wait_ge(begin_ready, 2 * r + 2)
            pe.matmul(kept_table, k.zeros[:, 0:CAP], k.zeros[:, :], start=True, stop=False)

            def shared(t, q):
                qq = q + r * GN
                if group(q) and t < len(MSC):
                    m0, rows = MSC[t]
                    if t == 0:
                        pe.wait_ge(down_used, qq + 1)
                        pe.wait_ge(xnT_ready, (qq + 1) * G)
                    pe.wait_ge(gu_copied, qq * 3 + (t + 1))
                    for which in range(2):
                        for d in range(DC):
                            ins = pe.matmul(ps_s[which][0:rows, :], k.sguT[:, d, which * MS + m0:which * MS + m0 + rows],
                                            xnT[:, d, bass.ds(q * GT, GT)], start=(d == 0), stop=(d == DC - 1))
                    ins.then_inc(gu_ready, 1)
                elif group(q):
                    pe.wait_ge(gu_copied, qq * 3 + 4)
                    pe.wait_ge(hid_ready, qq + 1)
                    for tile in range(G):
                        to = ps_s[tile // 2][:, (tile % 2) * D:(tile % 2 + 1) * D]
                        for c, (m0, rows) in enumerate(MSC):
                            ins = pe.matmul(to, sgate[0:rows, c, tile * P:(tile + 1) * P], k.sdT[0:rows, c, :],
                                            start=(c == 0), stop=(c == 2))
                    ins.then_inc(down_ready, 1)

            def step(m, t, q):
                gm = m + r * NT
                qq = q + r * GN
                if live(m, 1):
                    g, u = gm - 1, (t - 1) % 2
                    pe.wait_ge(xn_ready, g + 1)
                    if not isinstance(m, int) or m > 1 or r > 0:
                        pe.wait_ge(xnT_ready, g)
                    for c in range(DC):
                        ins = pe.transpose(ps_x[:, c, :], xn[u][:, c * P:(c + 1) * P], k.ident[:, :])
                    ins.then_inc(xT_raw, 1)
                    pe.wait_ge(xT_ready, g + 1)
                    for c in range(DC):
                        ins = pe.matmul(ps_r[u][:, :], xT[u][:, c, :], k.gateT[:, c, :], start=(c == 0), stop=(c == DC - 1))
                    ins.then_inc(logits_ready, 1)
                if live(m, 3):
                    g, u = gm - 3, (t - 1) % 2
                    pe.wait_ge(member_ready, g + 1)
                    pe.matmul(ps_p[u][:, :], k.before_bf[:, :], member[u][:, :], start=True, stop=False)
                    pe.matmul(ps_p[u][:, :], k.ones_bf[:, :], k.member_sum[:, 1 - u, :], start=False,
                              stop=True).then_inc(pos_ready, 1)
                if live(m, 4):
                    g, u = gm - 4, t % 2
                    pe.wait_ge(onehot_ready, g + 1)
                    for j in range(TOPK):
                        ins = pe.matmul(kept_table, hot_pos[u][:, j, :], hot_tok[u][:, j, :, :], start=False, stop=False)
                    ins.then_inc(onehot_free, 1)
                if isinstance(m, int) and m - 3 == NT:
                    pe.wait_ge(slots_ready, (r + 1) * NT)
                    pe.wait_ge(xnT_ready, (r + 1) * NT)
                    pe.transpose(ps_x[0:E0, 0, :], last[:, :], k.ident[:, :]).then_inc(lastT_ready, 1)
                    pe.wait_ge(last_ready, r + 1)
                    pe.matmul(kept_table, k.last_slot[:, :], k.ident[0:E0, :], start=False, stop=True).then_inc(table_done, 1)
                shared(t, q)

            steps(pe, step)

        @block.scalar
        def _(act):
            row_std(act, k)

            def step(m, t, q):
                gm = m + r * NT
                qq = q + r * GN
                if live(m, 1):
                    g, u = gm - 1, (t - 1) % 2
                    act.wait_ge(xT_raw, g + 1)
                    act.activation(xT[u][:, :, :], ps_x[:, :, :], ACT.Copy).then_inc(xT_ready, 1)
                    act.activation(xnT[:, :, bass.ds((m - 1) * P, P)], ps_x[:, :, :], ACT.Copy).then_inc(xnT_ready, 1)
                if live(m, 2):
                    g, u = gm - 2, t % 2
                    act.wait_ge(nmax_ready, g + 1)
                    act.activation(ex[:, :], ps_r[u][:, :], ACT.Exp, bias=nmax[:, 0:1],
                                   accum_out=esum[:, 0:1]).then_inc(exp_ready, 1)
                if group(q) and t < len(MSC):
                    rows = MSC[t][1]
                    act.wait_ge(gu_ready, qq * 3 + (t + 1))
                    if t == 0:
                        act.wait_ge(down_ready, qq + 1)
                    act.activation(sgate[0:rows, t, :], ps_s[0][0:rows, :], ACT.Copy)
                    act.activation(sup[0:rows, t, :], ps_s[1][0:rows, :], ACT.Copy).then_inc(gu_copied, 1)
                    if t == 2:
                        act.wait_ge(gu_copied, qq * 3 + 4)
                        act.activation(sgate[:, 0:2, :], sgate[:, 0:2, :], ACT.Silu)
                        act.activation(sgate[0:rows, 2, :], sgate[0:rows, 2, :], ACT.Silu).then_inc(silu_ready, 1)

            steps(act, step)

        @block.gpsimd
        def _(pool):
            def step(m, t, q):
                gm = m + r * NT
                qq = q + r * GN
                if live(m, 4):
                    g, u = gm - 4, t % 2
                    pool.wait_ge(onehot_free, g + 1)
                    pool.wait_ge(posf_ready, g + 1)
                    for part in range(2):
                        pool.tensor_tensor(hot_tok[u][:, :, part, :], hot[u][:, :, :],
                                           spread(k.token_part[:, part, bass.ds(m - 4, 1)], 1, E0)
                                           .to_broadcast([P, TOPK, E0]), ALU.mult)
                    for j in range(TOPK):
                        ins = pool.tensor_scalar(hot_pos[u][:, j, :], k.iota_slot[:, :], posf[u][:, j:j + 1], None,
                                                 ALU.is_equal)
                    ins.then_inc(onehot_ready, 1)

            steps(pool, step)

        @block.vector
        def _(dve):
            dve.wait_ge(k.sem("x_loaded"), 16)
            row_stats(dve, k)
            dve.memset(last[:, :], 0.0).then_inc(begin_ready, 1)
            dve.memset(k.member_sum[:, 1, :], 0.0).then_inc(begin_ready, 1)
            dve.wait_ge(begin_ready, 2 * r + 2)

            def step(m, t, q):
                gm = m + r * NT
                qq = q + r * GN

                def normalised():
                    if live(m, 0):
                        dve.wait_ge(xn_stored[t % 2], (gm + (2 - t % 2)) * 8)
                        if not isinstance(m, int) or m > 1 or r > 0:
                            dve.wait_ge(xT_raw, gm - 1)
                        layernorm(dve, k, m, xn[t % 2][:, :], xn_ready)

                def row_max():
                    if live(m, 2):
                        dve.wait_ge(logits_ready, gm - 1)
                        dve.tensor_reduce(nmax[:, :], ps_r[t % 2][:, :], AX, ALU.max, negate=True)\
                           .then_inc(nmax_ready, 1)

                slot_steps = k.sem("r_slot_steps")

                def positions():
                    g, u = gm - 4, t % 2
                    dve.wait_ge(pos_ready, g + 1)
                    dve.tensor_tensor(picked[:, :, :], hot[u][:, :, :], repeat(ps_p[u][:, :], TOPK, E0),
                                      ALU.mult).then_inc(slot_steps, 1)

                def positions_k():
                    g, u = gm - 4, t % 2
                    dve.wait_ge(slot_steps, g * 2 + 1)
                    dve.tensor_reduce(posf[u][:, :], picked[:, :, :], AX, ALU.add).then_inc(posf_ready, 1)

                def slots_capped():
                    g, u = gm - 4, t % 2
                    dve.wait_ge(posf_ready, g + 1)
                    dve.tensor_scalar(slot_c[:, :], posf[u][:, :], float(CAP - 1), None, ALU.min).then_inc(slot_steps, 1)

                def slots():
                    g = gm - 4
                    dve.wait_ge(slot_steps, g * 2 + 2)
                    dve.scalar_tensor_tensor(out=k.slot[:, m - 4, :], in0=top_f[:, :], scalar=float(CAP), in1=slot_c[:, :],
                                             op0=ALU.mult, op1=ALU.add).then_inc(slots_ready, 1)

                def shared_added():
                    if group(q, 1) and t == 0:
                        dve.wait_ge(down_ready, qq + 1)
                        for half in range(2):
                            x = k.X[:, bass.ds((q - 1) * G + half * 2, 2), :]
                            ins = dve.scalar_tensor_tensor(out=x, in0=ps_s[half][:, :].rearrange("p (n d) -> p n d", d=D),
                                                           scalar=0.5, in1=x, op0=ALU.mult, op1=ALU.add)
                        ins.then_inc(down_used, 1)

                def hidden():
                    if group(q) and t == 3:
                        rows = MSC[2][1]
                        dve.wait_ge(silu_ready, qq + 1)
                        dve.tensor_tensor(sgate[:, 0:2, :], sgate[:, 0:2, :], sup[:, 0:2, :], ALU.mult)
                        dve.tensor_tensor(sgate[0:rows, 2, :], sgate[0:rows, 2, :], sup[0:rows, 2, :],
                                          ALU.mult).then_inc(hid_ready, 1)

                if not live(m, 3):
                    normalised()
                    row_max()
                    if live(m, 4):
                        positions()
                        positions_k()
                        slots_capped()
                        slots()
                    hidden()
                    shared_added()
                    return
                u = (t - 1) % 2
                g = gm - 3
                s = Steps(dve, k.sem("r_steps"), g, 15)
                before = live(m, 4)
                dve.wait_ge(exp_ready, g + 1)
                s.mark(dve.reciprocal(rsum[:, :], esum[:, :]))
                if before:
                    positions()
                s.settle()
                s.mark(dve.tensor_scalar(score[:, :], ex[:, :], rsum[:, 0:1], None, ALU.mult))
                if before:
                    positions_k()
                s.settle()
                s.mark(dve.tensor_reduce(gmax[:, :], score[:, :].rearrange("p (g e) -> p g e", g=NG), AX, ALU.max))
                if before:
                    slots_capped()
                s.settle_apart()
                s.mark(dve.max(gtop[:, :], gmax[:, :]))
                if before:
                    slots()
                s.settle_apart()
                s.mark(dve.max_index(gtop_i[:, :], gtop[:, :], gmax[:, :]))
                normalised()
                s.settle()
                s.mark(dve.tensor_copy(gtop_f[:, :], gtop_i[:, 0:TG]))
                s.settle()
                s.mark(dve.tensor_tensor(ghot[:, :, :], repeat(k.iota64[:, 0:NG], TG, NG),
                                         spread(gtop_f[:, :], TG, NG), ALU.is_equal))
                s.settle()
                s.mark(dve.tensor_reduce(gmask[:, :], ghot[:, :, :].rearrange("p k g -> p g k"), AX, ALU.add))
                s.settle()
                s.mark(dve.tensor_tensor(masked[:, :].rearrange("p (g e) -> p g e", g=NG),
                                         score[:, :].rearrange("p (g e) -> p g e", g=NG),
                                         spread(gmask[:, :], NG, E0 // NG), ALU.mult))
                s.settle_apart()
                s.mark(dve.max(top[:, :], masked[:, :]))
                row_max()
                s.settle_apart()
                s.mark(dve.max_index(top_i[:, :], top[:, :], masked[:, :]))
                dve.tensor_scalar(k.weight[:, m - 3, :], top[:, 0:TOPK], 0.5, None, ALU.mult)
                if before:
                    dve.wait_ge(slots_ready, g)
                dve.wait_ge(onehot_free, g + 1)
                s.settle()
                s.mark(dve.tensor_copy(top_f[:, :], top_i[:, 0:TOPK]))
                s.settle()
                s.mark(dve.tensor_tensor(hot[u][:, :, :], repeat(k.iota64[:, :], TOPK, E0),
                                         spread(top_f[:, :], TOPK, E0), ALU.is_equal))
                s.settle()
                with nc.allow_low_precision(reason="sums of zeros and ones up to 16 are exact"):
                    dve.tensor_reduce(member[u][:, :], hot[u][:, :, :].rearrange("p k e -> p e k"), AX,
                                      ALU.add).then_inc(member_ready, 1)
                    dve.wait_ge(member_ready, g + 1)
                    s.mark(dve.tensor_tensor(k.member_sum[:, u, :], k.member_sum[:, 1 - u, :], member[u][:, :], ALU.add))
                s.mark(dve.scalar_tensor_tensor(out=last[:, :], in0=member[u][:, :], scalar=k.token1[:, bass.ds(m - 3, 1)],
                                                in1=last[:, :], op0=ALU.mult, op1=ALU.max))
                hidden()
                shared_added()
                s.settle()
                s.close()

            row_rstd(dve, k)
            for m in range(PEEL * G):
                step(m, m % G, m // G - 1)
            with dve.Fori(PEEL, GN) as i:
                for t in range(G):
                    step(i * G + t, t, i - 1)
            for m in range(NT, LAST + 1):
                step(m, m % G, m // G - 1)
                if m - 3 == NT:
                    dve.wait_ge(lastT_ready, r + 1)
                    f = k.sem("r_last_steps")
                    dve.tensor_reduce(last_col[:, :], ps_x[0:E0, 0, :], AX, ALU.max).then_inc(f, 1)
                    dve.wait_ge(f, 2 * r + 1)
                    dve.tensor_scalar(k.last_slot[:, CAP - 1:CAP], last_col[:, :], -1.0, 0.0, ALU.add,
                                      ALU.max).then_inc(last_ready, 1)
                    dve.wait_ge(table_done, r + 1)
                    dve.tensor_copy(high[:, :], kept_table[:, E0:2 * E0]).then_inc(f, 1)
                    dve.wait_ge(f, 2 * r + 2)
                    dve.tensor_tensor(k.table[:, :], high[:, :], kept_table[:, 0:E0], ALU.add)
    k.norms += 1


def pipelined(eng, body, first, last, unroll):
    rounds = (last + 1 - first) // unroll
    for s in range(first):
        body(s, s % unroll)
    assert first % unroll == 0
    with eng.Fori(0, rounds) as i:
        for u in range(unroll):
            body(i * unroll + (first + u), u)
    for s in range(first + rounds * unroll, last + 1):
        body(s, s % unroll)


def routed_experts(nc, k, r):
    U, GA, LAG = AHEAD, 4, 3
    staged = k.sem("e_index_staged")
    got = [k.sem(f"e_tokens_got{u}") for u in range(GA)]
    gu_got = [k.sem(f"e_gate_up_got{u}") for u in range(U)]
    dn_got = [k.sem(f"e_down_got{u}") for u in range(U)]
    xT_raw, xT_ready = k.sem("e_xT_psum_ready"), k.sem("e_xT_ready")
    gu_ready, act_ready, h_ready = k.sem("e_gate_up_ready"), k.sem("e_silu_ready"), k.sem("e_hidden_ready")
    hT_raw, hT_ready = k.sem("e_hT_psum_ready"), k.sem("e_hT_ready")
    dn_ready, y_ready = k.sem("e_down_ready"), k.sem("e_y_ready")
    y_stored = [k.sem(f"e_y_stored{u}") for u in range(2)]
    with ExitStack() as ctx:
        sb, ps = scoped(nc, ctx)
        index = [sb(f"e{r}_index{u}", [CAP, 1], U32) for u in range(GA)]
        x = [sb(f"e{r}_x{u}", [CAP, D]) for u in range(GA)]
        xT = [sb(f"e{r}_xT{u}", [P, DC, CAP]) for u in range(2)]
        wgu, wdn = k.wgu, k.wdn
        sg = [sb(f"e{r}_sg{u}", [CAP, M0]) for u in range(2)]
        h = [sb(f"e{r}_h{u}", [CAP, M0]) for u in range(2)]
        hT = [sb(f"e{r}_hT{u}", [MH, 2, CAP]) for u in range(2)]
        y = [sb(f"e{r}_y{u}", [CAP, D]) for u in range(2)]
        ps_x = [ps(f"e{r}_ps_x{u}", [P, DC, CAP]) for u in range(2)]
        ps_gu = [ps(f"e{r}_ps_gu{u}", [CAP, 2 * M0]) for u in range(2)]
        ps_h = [ps(f"e{r}_ps_h{u}", [MH, 2, CAP]) for u in range(2)]
        ps_y = [ps(f"e{r}_ps_y{u}", [CAP, D]) for u in range(2)]
        block = ctx.enter_context(nc.Block())
        last = E0 - 1 + LAG

        def later(s, n):
            return not isinstance(s, int) or s >= n or r > 0

        def live(s, lag):
            return not isinstance(s, int) or 0 <= s - lag < E0

        @block.sync
        def _(sp):
            def load(e, u):
                g = e + r * E0
                sp.wait_ge(gu_ready, g - (U - 1))
                sp.dma_start(wgu[u][:, :, :], k.w["wgu0"][e]).then_inc(gu_got[u], 16)
                sp.wait_ge(dn_ready, g - (U - 1))
                sp.dma_start(wdn[u][:, :, :], k.w["wdn0"][e]).then_inc(dn_got[u], 16)

            with sp.Fori(1, E0 // U) as i:
                for u in range(U):
                    load(i * U + u, u)

        @block.gpsimd
        def _(pool):
            for u in range(2):
                pool.wait_ge(k.sem(f"r_xn_stored{u}"), 16 * ((r + 1) * NT // 2 + 1))

            def gather(e, u):
                g = e + r * E0
                if later(e, GA):
                    pool.wait_ge(xT_raw, g - (GA - 1))
                pool_copy(pool, k, index[u][:, :], k.table[:, bass.ds(e, 1)]).then_inc(staged, 1)
                pool.wait_ge(staged, g + 1)
                pool.sem_inc(k.sem("passed"), 1)
                pool.indirect_dma_start(x[u][:, :], None, k.xn_rows[:, :],
                                        bass.IndirectOffsetOnAxis(ap=index[u][:, 0:1], axis=0)).then_inc(got[u], 16)

            pipelined(pool, gather, GA, E0 - 1, GA)

        @block.tensor
        def _(pe):
            def step(s, u):
                g = s + r * E0
                if live(s, 0):
                    v = u % 2
                    a = u % GA
                    pe.wait_ge(got[a], (g + (GA - a)) * (16 // GA))
                    if later(s, 2):
                        pe.wait_ge(xT_ready, g - 1)
                    for c in range(DC):
                        ins = pe.transpose(ps_x[v][:, c, :], x[a][:, c * P:(c + 1) * P], k.ident[0:CAP, 0:CAP])
                    ins.then_inc(xT_raw, 1)
                if live(s, 1):
                    v = (u - 1) % 2
                    pe.wait_ge(xT_ready, g)
                    pe.wait_ge(gu_got[(u - 1) % U], (g - 1 + (U - (u - 1) % U)) * (16 // U))
                    if later(s, 3):
                        pe.wait_ge(h_ready, g - 2)
                    for c in range(DC):
                        ins = pe.matmul(ps_gu[v][:, :], xT[v][:, c, :], wgu[(u - 1) % U][:, c, :],
                                        start=(c == 0), stop=(c == DC - 1))
                    ins.then_inc(gu_ready, 1)
                if live(s, 2):
                    v = u % 2
                    pe.wait_ge(h_ready, g - 1)
                    if later(s, 4):
                        pe.wait_ge(hT_ready, g - 3)
                    for c in range(2):
                        ins = pe.transpose(ps_h[v][:, c, :], h[v][:, MHC[c]:MHC[c] + MH], k.ident[0:CAP, 0:CAP])
                    ins.then_inc(hT_raw, 1)
                if live(s, 3):
                    v = (u - 1) % 2
                    pe.wait_ge(hT_ready, g - 2)
                    pe.wait_ge(dn_got[(u - 3) % U], (g - 3 + (U - (u - 3) % U)) * (16 // U))
                    if later(s, 5):
                        pe.wait_ge(y_ready, g - 4)
                    for c in range(2):
                        ins = pe.matmul(ps_y[v][:, :], hT[v][:, c, :], wdn[(u - 3) % U][:, c, :],
                                        start=(c == 0), stop=(c == 1))
                    ins.then_inc(dn_ready, 1)

            pipelined(pe, step, U, last, U)

        @block.scalar
        def _(act):
            def step(s, u):
                g = s + r * E0
                if live(s, 0):
                    v = u % 2
                    act.wait_ge(xT_raw, g + 1)
                    if later(s, 2):
                        act.wait_ge(gu_ready, g - 1)
                    act.activation(xT[v][:, :, :], ps_x[v][:, :, :], ACT.Copy).then_inc(xT_ready, 1)
                if live(s, 1):
                    v = (u - 1) % 2
                    act.wait_ge(gu_ready, g)
                    if later(s, 3):
                        act.wait_ge(h_ready, g - 2)
                    act.activation(sg[v][:, :], ps_gu[v][:, 0:M0], ACT.Silu).then_inc(act_ready, 1)
                if live(s, 3):
                    v = (u - 1) % 2
                    act.wait_ge(dn_ready, g - 2)
                    if later(s, 5):
                        act.wait_ge(y_stored[v], (g - (3 + v)) * 8)
                    act.activation(y[v][:, :], ps_y[v][:, :], ACT.Copy).then_inc(y_ready, 1)
                    act.wait_ge(y_ready, g - 2)
                    act.dma_start(k.slot_rows.rearrange("(e c) d -> e c d", c=CAP)[s - 3], y[v][:, :])\
                       .then_inc(y_stored[v], 16)

            pipelined(act, step, U, last, U)
            for v in range(2):
                act.wait_ge(y_stored[v], 16 * ((r + 1) * E0 // 2))

        @block.vector
        def _(dve):
            def step(s, u):
                g = s + r * E0
                if live(s, 1):
                    v = (u - 1) % 2
                    dve.wait_ge(act_ready, g)
                    if later(s, 3):
                        dve.wait_ge(hT_raw, g - 2)
                    dve.tensor_tensor(h[v][:, :], sg[v][:, :], ps_gu[v][:, M0:2 * M0], ALU.mult).then_inc(h_ready, 1)
                if live(s, 2):
                    v = u % 2
                    dve.wait_ge(hT_raw, g - 1)
                    if later(s, 4):
                        dve.wait_ge(dn_ready, g - 3)
                    dve.tensor_copy(hT[v][:, :, :], ps_h[v][:, :, :]).then_inc(hT_ready, 1)

            pipelined(dve, step, U, last, U)


def combine_experts(nc, k, r):
    rows_got = [k.sem(f"c_rows_got{u}") for u in range(2)]
    with ExitStack() as ctx:
        sb, ps = scoped(nc, ctx)
        rows = [[sb(f"c{r}_rows{u}_{j}", [P, D]) for j in range(TOPK)] for u in range(2)]
        at = [sb(f"c{r}_at{u}", [P, TOPK], U32) for u in range(2)]
        block = ctx.enter_context(nc.Block())

        @block.gpsimd
        def _(pool):
            gather_rows(pool, k, r, rows, at)

        @block.vector
        def _(dve):
            with dve.Fori(0, NT // 2) as i:
                for u in range(2):
                    add_rows(dve, k, r, i * 2 + u, rows[u], rows_got[u], u)


def gather_rows(pool, k, r, rows, at):
    staged, rows_used = k.sem("c_slots_staged"), k.sem("c_rows_used")
    if r == 0:
        pool.sem_inc(rows_used, 2)
    with pool.Fori(0, NT // 2) as i:
        for u in range(2):
            g = i * 2 + (r * NT + u)
            pool.wait_ge(rows_used, g + 1)
            pool_copy(pool, k, at[u][:, :], k.slot[:, i * 2 + u, :]).then_inc(staged, 1)
            pool.wait_ge(staged, g + 1)
            pool.sem_inc(k.sem("passed"), 1)
            for j in range(TOPK):
                pool.indirect_dma_start(rows[u][j][:, :], None, k.slot_rows[:, :],
                                        bass.IndirectOffsetOnAxis(ap=at[u][:, j:j + 1], axis=0))\
                    .then_inc(k.sem(f"c_rows_got{u}"), 16)


def add_rows(dve, k, r, n, rows, got, u):
    g = n + r * NT
    x = k.X[:, n, :]
    s = Steps(dve, k.sem("c_sum_steps"), g, TOPK)
    dve.wait_ge(got, (g + (2 - u)) * (8 * TOPK))
    for j in range(TOPK):
        s.mark(dve.scalar_tensor_tensor(out=x, in0=rows[j][:, :], scalar=k.weight[:, n, j:j + 1],
                                        in1=x, op0=ALU.mult, op1=ALU.add))
        s.settle()
    s.close()
    dve.sem_inc(k.sem("c_rows_used"), 1)


def linear_attention(nc, k):
    A = 3
    UNITS = 4 + 1 + H0 + TB + 2 * H0 + 3 * TB
    QB = UNITS // A
    assert UNITS % A == 0
    HG = H0 // 2
    MID = SUB // 2 - 1
    xn_ready, zmin_ready, soft_ready = k.sem("g_xn_ready"), k.sem("g_zmin_ready"), k.sem("g_softplus_ready")
    gk_ready, cen_ready = k.sem("g_log_gate_ready"), k.sem("g_centred_ready")
    edge_ready = k.sem("g_edges_ready")
    up_ready, down_ready, gw_ready = k.sem("g_exp_up_ready"), k.sem("g_exp_down_ready"), k.sem("g_gate_ready")
    act_steps, dve_steps = k.sem("g_act_steps"), k.sem("g_dve_steps")
    at_ready, at_masked = k.sem("g_scores_ready"), k.sem("g_scores_masked")
    sm_ready, kv_ready, kv_used = k.sem("g_state_ready"), k.sem("g_kv_ready"), k.sem("g_kv_used")
    o_ready, o_copied, sq_ready, on_ready = (k.sem("g_o_ready"), k.sem("g_o_copied"), k.sem("g_squares_ready"),
                                             k.sem("g_normed_ready"))
    out_ready, out_used = k.sem("g_out_ready"), k.sem("g_out_used")
    ms_ready, rms_ready = k.sem("g_mean_square_ready"), k.sem("g_rms_ready")
    a_ready = [k.sem(f"g_bank_ready{a}") for a in range(A)]
    a_free = [k.sem(f"g_bank_free{a}") for a in range(A)]
    TR, LOW, Z, VG, Q, K_, CORE = 0, 4, 5, 5 + H0, 5 + H0 + TB, 5 + 2 * H0 + TB, 5 + 3 * H0 + TB
    order = [("kt", 0, 0), ("kt", 0, 1)]
    for j in range(1, TB):
        order += [("kt", j, 0), ("kt", j, 1), ("o", j - 1, 0)]
    order += [("o", TB - 1, 0)]
    core_unit = {key: CORE + m for m, key in enumerate(order)}
    assert CORE + len(order) == UNITS
    with ExitStack() as ctx:
        sb, ps = scoped(nc, ctx)
        xn = [sb(f"g_xn{j}", [P, D]) for j in range(2)]
        xT = sb("g_xT", [P, DC, T])
        low = sb("g_low", [P, T])
        zm = sb("g_zm", [P, H0, T])
        za = sb("g_za", [P, H0, T])
        qp = sb("g_qp", [P, H0, T])
        kp = sb("g_kp", [P, H0, T])
        mid = sb("g_mid", [P, H0, NSUB])
        e_mid = sb("g_e_mid", [P, H0, NSUB])
        e_all = sb("g_e_all", [P, H0, NSUB])
        e_rest = sb("g_e_rest", [P, H0, NSUB])
        v = sb("g_v", [P, TB, H0 * DV])
        gw = sb("g_gw", [P, TB, H0 * DV])
        kT = [sb(f"g_kT{u}", [P, H0, DK]) for u in range(2)]
        atm = [sb(f"g_atm{u}", [P, H0, SUB]) for u in range(2)]
        state = sb("g_state", [P, H0, DV])
        state_mid = [sb(f"g_state_mid{u}", [P, H0, DV]) for u in range(2)]
        kv_dec = sb("g_kv_dec", [P, H0, DV])
        o = [sb(f"g_o{u}", [P, H0, DV]) for u in range(2)]
        sq = sb("g_sq", [P, H0, DV])
        ms = sb("g_ms", [P, H0])
        rms = sb("g_rms", [P, H0])
        on = [sb(f"g_on{u}", [P, H0, DV]) for u in range(2)]
        oT = sb("g_oT", [P, 2, P])
        bank = [ps(f"g_bank{a}", [P, 512]) for a in range(A)]
        ps_at = [ps(f"g_ps_at{half}", [P, HG, SUB]) for half in range(2)]
        ps_kv = ps("g_ps_kv", [P, H0, DV])
        ps_o = ps("g_ps_o", [P, H0, DV])
        ps_out = ps("g_ps_out", [P, D])
        block = ctx.enter_context(nc.Block())

        def chunks(ap):
            return ap.rearrange("p h (c s) -> p h c s", s=SUB)

        def over(ap, m):
            return ap.unsqueeze(len(ap.shape)).to_broadcast(list(ap.shape) + [m])

        def emptied(eng, b, m):
            eng.wait_ge(a_free[m % A], b * QB + (m // A + 2))

        def use(eng, b, m):
            eng.wait_ge(a_ready[m % A], b * QB + (m // A + 1))
            return bank[m % A]

        @block.tensor
        def _(pe):
            pe.wait_ge(k.sem("w0_loaded"), 16 * 12)
            with pe.Fori(0, B) as b:
                def take(m):
                    pe.wait_ge(a_free[m % A], b * QB + (m // A + 1))
                    return bank[m % A]

                for j in range(TB):
                    pe.wait_ge(xn_ready, b * TB + (j + 1))
                    to = take(TR + j)
                    for c in range(DC):
                        ins = pe.transpose(to[:, c * P:(c + 1) * P], xn[j % 2][:, c * P:(c + 1) * P], k.ident[:, :])
                    ins.then_inc(a_ready[(TR + j) % A], 1)
                for j in range(TB):
                    emptied(pe, b, TR + j)
                to = take(LOW)
                for c in range(DC):
                    ins = pe.matmul(to[:, :], k.wgk0[:, c, :], xT[:, c, :], start=(c == 0), stop=(c == DC - 1))
                ins.then_inc(a_ready[LOW % A], 1)
                emptied(pe, b, LOW)
                for h in range(H0):
                    to = take(Z + h)
                    pe.matmul(to[:, :], k.wgk1[:, h * DK:(h + 1) * DK], low[:, :], start=True,
                              stop=True).then_inc(a_ready[(Z + h) % A], 1)
                for j in range(TB):
                    to = take(VG + j)
                    for c in range(DC):
                        ins = pe.matmul(to[:, :], xT[:, c, j * P:(j + 1) * P], k.wvg[:, c, :],
                                        start=(c == 0), stop=(c == DC - 1))
                    ins.then_inc(a_ready[(VG + j) % A], 1)
                for w, first in ((k.wq0, Q), (k.wk0, K_)):
                    for h in range(H0):
                        to = take(first + h)
                        for c in range(DC):
                            ins = pe.matmul(to[:, :], w[:, c, h * DK:(h + 1) * DK], xT[:, c, :],
                                            start=(c == 0), stop=(c == DC - 1))
                        ins.then_inc(a_ready[(first + h) % A], 1)

                def project(j):
                    pe.wait_ge(on_ready, b * TB + (j + 1))
                    m = core_unit[("o", j, 0)]
                    to = take(m)
                    flat = on[j % 2][:, :, :].rearrange("p h v -> p (h v)")
                    for c in range(2):
                        ins = pe.transpose(to[:, c * P:(c + 1) * P], flat[:, c * P:(c + 1) * P], k.ident[:, :])
                    ins.then_inc(a_ready[m % A], 1)
                    emptied(pe, b, m)
                    pe.wait_ge(out_used, b * TB + (j + 1))
                    for c in range(2):
                        ins = pe.matmul(ps_out[:, :], oT[:, c, :], k.wo0[:, c, :], start=(c == 0), stop=(c == 1))
                    ins.then_inc(out_ready, 1)

                for h in range(H0 - A, H0):
                    emptied(pe, b, K_ + h)
                for j in range(TB):
                    tokens = slice(j * P, (j + 1) * P)
                    for half in range(2):
                        pe.wait_ge(at_masked, (b * TB + j) * 2 + (half + 1))
                        for h in range(HG):
                            hh = half * HG + h
                            ins = pe.matmul(ps_at[half][:, h, :], kp[:, hh, tokens], qp[:, hh, tokens],
                                            start=True, stop=True)
                        ins.then_inc(at_ready, 1)
                    for half in range(2):
                        m = core_unit[("kt", j, half)]
                        to = take(m)
                        for h in range(HG):
                            ins = pe.transpose(to[:, h * P:(h + 1) * P], kp[:, half * HG + h, tokens], k.ident[:, :])
                        ins.then_inc(a_ready[m % A], 1)
                    emptied(pe, b, core_unit[("kt", j, 0)])
                    emptied(pe, b, core_unit[("kt", j, 1)])
                    pe.wait_ge(kv_used, b * TB + (j + 1))
                    for h in range(H0):
                        ins = pe.matmul(ps_kv[:, h, :], kT[j % 2][:, h, :], v[:, j, h * DV:(h + 1) * DV],
                                        start=True, stop=True)
                    ins.then_inc(kv_ready, 1)
                    pe.wait_ge(sm_ready, b * TB + (j + 1))
                    pe.wait_ge(at_masked, (b * TB + j) * 2 + 4)
                    pe.wait_ge(o_copied, b * TB + (j + 1))
                    for h in range(H0):
                        pe.matmul(ps_o[:, h, :], qp[:, h, tokens], state_mid[j % 2][:, h, :], start=True, stop=False)
                        ins = pe.matmul(ps_o[:, h, :], atm[j % 2][:, h, :], v[:, j, h * DV:(h + 1) * DV],
                                        start=False, stop=True)
                    ins.then_inc(o_ready, 1)
                    if j:
                        project(j - 1)
                project(TB - 1)

        @block.scalar
        def _(act):
            act.wait_ge(k.sem("w0_loaded"), 16 * 12)
            row_std(act, k)
            with act.Fori(0, B) as b:
                s = Steps(act, act_steps, b, 4)
                for j in range(TB):
                    src = use(act, b, TR + j)
                    act.activation(xT[:, :, j * P:(j + 1) * P], src[:, 0:D].rearrange("p (c t) -> p c t", c=DC),
                                   ACT.Copy).then_inc(a_free[(TR + j) % A], 1)
                src = use(act, b, LOW)
                act.activation(low[:, :], src[:, :], ACT.Copy).then_inc(a_free[LOW % A], 1)
                for h in range(H0):
                    m = Z + h
                    src = use(act, b, m)
                    act.activation(za[:, h, :], src[:, :], ACT.Identity, bias=k.bgk1[:, h:h + 1])\
                       .then_inc(a_free[m % A], 1)
                for half in range(2):
                    part = za[:, half * HG:(half + 1) * HG, :]
                    act.wait_ge(zmin_ready, b * 2 + (half + 1))
                    s.mark(act.activation(part, part, ACT.Abs))
                for half in range(2):
                    part = za[:, half * HG:(half + 1) * HG, :]
                    s.settle(back=1)
                    s.mark(act.activation(part, part, ACT.Exp, scale=-1.0))
                for half in range(2):
                    part = za[:, half * HG:(half + 1) * HG, :]
                    s.settle(back=1 - half)
                    act.activation(part, part, ACT.Ln, bias=1.0).then_inc(soft_ready, 1)
                for j in range(TB):
                    m = VG + j
                    src = use(act, b, m)
                    act.activation(v[:, j, :], src[:, 0:H0 * DV], ACT.Copy)
                    act.activation(gw[:, j, :], src[:, H0 * DV:2 * H0 * DV], ACT.Silu).then_inc(a_free[m % A], 1)
                for half in range(2):
                    hs = slice(half * HG, (half + 1) * HG)
                    act.wait_ge(cen_ready, b * 2 + (half + 1))
                    act.activation(e_mid[:, hs, :], mid[:, hs, :], ACT.Exp, scale=1.0 / GATE_NORM)
                    act.activation(e_all[:, hs, :], chunks(zm[:, hs, :])[:, :, :, SUB - 1], ACT.Exp,
                                   scale=1.0 / GATE_NORM).then_inc(edge_ready, 1)
                    act.wait_ge(edge_ready, b * 2 + (half + 1))
                    act.activation(zm[:, hs, :], za[:, hs, :], ACT.Exp, scale=1.0 / GATE_NORM).then_inc(up_ready, 1)
                    act.wait_ge(up_ready, b * 2 + (half + 1))
                    act.activation(za[:, hs, :], za[:, hs, :], ACT.Exp, scale=-1.0 / GATE_NORM).then_inc(down_ready, 1)

                def oT_copy(j):
                    m = core_unit[("o", j, 0)]
                    src = use(act, b, m)
                    act.activation(oT[:, :, :], src[:, 0:D].rearrange("p (c t) -> p c t", c=2),
                                   ACT.Copy).then_inc(a_free[m % A], 1)

                for j in range(TB):
                    for half in range(2):
                        m = core_unit[("kt", j, half)]
                        src = use(act, b, m)
                        act.activation(kT[j % 2][:, half * 4:(half + 1) * 4, :],
                                       src[:, :].rearrange("p (h d) -> p h d", h=4), ACT.Copy).then_inc(a_free[m % A], 1)
                    act.wait_ge(o_ready, b * TB + (j + 1))
                    act.activation(o[j % 2][:, :, :], ps_o[:, :, :], ACT.Copy).then_inc(o_copied, 1)
                    if j:
                        oT_copy(j - 1)
                    act.wait_ge(ms_ready, b * TB + (j + 1))
                    act.activation(rms[:, :], ms[:, :], ACT.Sqrt, bias=k.eps[:, 0:1], scale=1.0 / DV).then_inc(rms_ready, 1)
                oT_copy(TB - 1)
                s.close()

        @block.gpsimd
        def _(pool):
            with pool.Fori(0, B) as b:
                for half in range(2):
                    hs = slice(half * HG, (half + 1) * HG)
                    pool.wait_ge(soft_ready, b * 2 + (half + 1))
                    pool.tensor_tensor(zm[:, hs, :], zm[:, hs, :], za[:, hs, :], ALU.subtract).then_inc(gk_ready, 1)
                for j in range(TB):
                    emptied(pool, b, VG + j)
                    g = gw[:, j, :].rearrange("p (h v) -> p h v", h=H0)
                    pool.tensor_tensor(g, g, k.gnorm[:, :].unsqueeze(1).to_broadcast([P, H0, DV]),
                                       ALU.mult).then_inc(gw_ready, 1)
                for j in range(TB):
                    pool.wait_ge(o_copied, b * TB + (j + 2))
                    pool.tensor_tensor(sq[:, :, :], o[j % 2][:, :, :], o[j % 2][:, :, :], ALU.mult).then_inc(sq_ready, 1)

        @block.vector
        def _(dve):
            dve.wait_ge(k.sem("x_loaded"), 16)
            row_stats(dve, k)
            for a in range(A):
                dve.sem_inc(a_free[a], 1)
            dve.sem_inc(at_masked, 2)
            dve.sem_inc(kv_used, 1)
            dve.sem_inc(o_copied, 1)
            dve.sem_inc(out_used, 1)
            row_rstd(dve, k)
            with dve.Fori(0, B) as b:
                s = Steps(dve, dve_steps, b, 2 * 2 + 2 + TB * 4)
                for j in range(TB):
                    if j >= 2:
                        dve.wait_ge(a_ready[(TR + j - 2) % A], b * QB + ((TR + j - 2) // A + 1))
                    layernorm(dve, k, b * TB + j, xn[j % 2][:, :], xn_ready)
                for half in range(2):
                    hs = slice(half * HG, (half + 1) * HG)
                    emptied(dve, b, Z + HG * (half + 1) - 1)
                    dve.tensor_scalar(zm[:, hs, :], za[:, hs, :], 0.0, None, ALU.min).then_inc(zmin_ready, 1)
                for half in range(2):
                    hs = slice(half * HG, (half + 1) * HG)
                    dve.wait_ge(gk_ready, b * 2 + (half + 1))
                    for h in range(half * HG, (half + 1) * HG):
                        ins = dve.tensor_tensor_scan(zm[:, h, :], k.chunk_keep[:, :], zm[:, h, :], 0.0, ALU.mult, ALU.add)
                    s.mark(ins)
                    s.settle()
                    s.mark(dve.tensor_copy(mid[:, hs, :], chunks(zm[:, hs, :])[:, :, :, MID]))
                    s.settle()
                    for h in range(half * HG, (half + 1) * HG):
                        ins = dve.tensor_tensor(za[:, h, :].rearrange("p (c s) -> p c s", s=SUB),
                                                zm[:, h, :].rearrange("p (c s) -> p c s", s=SUB),
                                                over(mid[:, h, :], SUB), ALU.subtract)
                    ins.then_inc(cen_ready, 1)
                for first, dst, dec, scale in ((Q, qp, zm, DK ** -0.5), (K_, kp, za, 1.0)):
                    for h in range(H0):
                        m = first + h
                        if h % HG == 0:
                            dve.wait_ge(up_ready if first == Q else down_ready, b * 2 + (h // HG + 1))
                        src = use(dve, b, m)
                        dve.scalar_tensor_tensor(out=dst[:, h, :], in0=src[:, :], scalar=scale, in1=dec[:, h, :],
                                                 op0=ALU.mult, op1=ALU.mult).then_inc(a_free[m % A], 1)
                s.mark(dve.tensor_copy(e_rest[:, :, :], chunks(zm[:, :, :])[:, :, :, SUB - 1]))
                s.mark(dve.memset(state[:, :, :], 0.0))
                s.settle()

                def add_out(j):
                    dve.wait_ge(out_ready, b * TB + (j + 1))
                    x = k.X[:, b * TB + j, :]
                    dve.tensor_tensor(x, ps_out[:, :], x, ALU.add).then_inc(out_used, 1)

                for j in range(TB):
                    for half in range(2):
                        dve.wait_ge(at_ready, (b * TB + j) * 2 + (half + 1))
                        dve.tensor_tensor(atm[j % 2][:, half * HG:(half + 1) * HG, :], ps_at[half][:, :, :],
                                          k.causal[:, :].unsqueeze(1).to_broadcast([P, HG, SUB]),
                                          ALU.mult).then_inc(at_masked, 1)
                    dve.tensor_tensor(state_mid[j % 2][:, :, :], state[:, :, :], over(e_mid[:, :, j], DV),
                                      ALU.mult).then_inc(sm_ready, 1)
                    s.mark(dve.tensor_tensor(state[:, :, :], state[:, :, :], over(e_all[:, :, j], DV), ALU.mult))
                    dve.wait_ge(kv_ready, b * TB + (j + 1))
                    dve.tensor_tensor(kv_dec[:, :, :], ps_kv[:, :, :], over(e_rest[:, :, j], DV),
                                      ALU.mult).then_inc(kv_used, 1)
                    dve.wait_ge(kv_used, b * TB + (j + 2))
                    s.settle()
                    s.mark(dve.tensor_tensor(state[:, :, :], state[:, :, :], kv_dec[:, :, :], ALU.add))
                    s.settle()
                    if j:
                        add_out(j - 1)
                    dve.wait_ge(sq_ready, b * TB + (j + 1))
                    dve.tensor_reduce(ms[:, :], sq[:, :, :], AX, ALU.add).then_inc(ms_ready, 1)
                    dve.wait_ge(rms_ready, b * TB + (j + 1))
                    s.mark(dve.reciprocal(rms[:, :], rms[:, :]))
                    s.settle()
                    s.mark(dve.tensor_tensor(on[j % 2][:, :, :], o[j % 2][:, :, :], over(rms[:, :], DV), ALU.mult))
                    s.settle()
                    dve.wait_ge(gw_ready, b * TB + (j + 1))
                    dve.tensor_tensor(on[j % 2][:, :, :], on[j % 2][:, :, :],
                                      gw[:, j, :].rearrange("p (h v) -> p h v", h=H0), ALU.mult).then_inc(on_ready, 1)
                add_out(TB - 1)
                s.close()
    k.norms += 1


def latent_attention(nc, k):
    UP = 2 * TB
    U2 = 2 * UP
    NU = PAIRS * UP
    TLAG = 3
    VLAG = UP + TLAG
    OLAG = VLAG + TB
    LAST = NU - UP + OLAG
    SCALE = DH ** -0.5
    PRE = TB + 2 + PAIRS
    QB = PRE // 2
    assert PRE % 2 == 0 and TB % 2 == 0
    xn_ready = k.sem("m_xn_ready")
    bank_ready = [k.sem(f"m_bank_ready{u}") for u in range(2)]
    bank_free = [k.sem(f"m_bank_free{u}") for u in range(2)]
    high_ready = k.sem("m_high_parts_ready")
    q_staged, s_ready, nmax_ready, p_ready = (k.sem("m_queries_staged"), k.sem("m_scores_ready"),
                                              k.sem("m_neg_max_ready"), k.sem("m_probs_ready"))
    scaled, pT_raw, pT_ready = k.sem("m_normalised"), k.sem("m_pT_psum_ready"), k.sem("m_pT_ready")
    v_ready, o_copied = k.sem("m_values_ready"), k.sem("m_o_copied")
    out_ready, out_used = k.sem("m_out_ready"), k.sem("m_out_used")
    max_steps, inv_steps = k.sem("m_max_steps"), k.sem("m_inverse_steps")
    TR, LATT, LATK, Q = 0, TB, TB + 1, TB + 2
    with ExitStack() as ctx:
        sb, ps = scoped(nc, ctx)
        xn = [sb(f"m_xn{u}", [P, D]) for u in range(2)]
        xT = sb("m_xT", [P, DC, T])
        latT = [sb(f"m_latT_{part}", [P, T], F32R) for part in ("high", "low")]
        lat = sb("m_lat", [P, TB, LAT])
        qa = sb("m_qa", [P, H1, T], F32R)
        qs = [sb(f"m_qs{u}", [P, 2, T], F32R) for u in range(2)]
        raw = sb("m_raw", [P, 2])
        nmax = sb("m_nmax", [P, 2])
        rsum = sb("m_rsum", [P, 4])
        rinv = sb("m_rinv", [P, 2])
        prob = [sb(f"m_prob{u}", [P, T]) for u in range(4)]
        pT = [sb(f"m_pT{u}", [P, 2, TB, T]) for u in range(2)]
        oT = sb("m_oT", [P, PAIRS, T])
        bank = [ps(f"m_bank{u}", [P, 512]) for u in range(2)]
        ps_s = [ps(f"m_ps_s{u}", [P, T]) for u in range(2)]
        ps_p = [ps(f"m_ps_p{u}", [P, TB, P]) for u in range(2)]
        ps_v = [ps(f"m_ps_v{u}", [P, T]) for u in range(2)]
        block = ctx.enter_context(nc.Block())

        def live(m, lag):
            return not isinstance(m, int) or 0 <= m - lag < NU

        def place(u, lag):
            w = (u - lag) % U2
            return w // UP, w % UP // 2, w % 2

        def steps(eng, body):
            for m in range(U2):
                body(m, m, 0)
            with eng.Fori(1, NU // U2) as i:
                for u in range(U2):
                    body(i * U2 + u, u, i)
            for m in range(NU, LAST + 1):
                body(m, m - NU, NU // U2)

        def pair_at(m, u, i, lag):
            w = u - lag
            if w % UP or (isinstance(m, int) and not 0 <= m - lag < NU):
                return None
            return i * 2 + w // UP

        @block.tensor
        def _(pe):
            pe.wait_ge(k.sem("w1_loaded"), 16 * 5)
            with pe.Fori(0, B) as b:
                def take(m):
                    pe.wait_ge(bank_free[m % 2], b * QB + (m // 2 + 1))
                    return bank[m % 2]

                for j in range(TB):
                    pe.wait_ge(xn_ready, b * TB + (j + 1))
                    to = take(TR + j)
                    for c in range(DC):
                        ins = pe.transpose(to[:, c * P:(c + 1) * P], xn[j % 2][:, c * P:(c + 1) * P], k.ident[:, :])
                    ins.then_inc(bank_ready[j % 2], 1)
                for j in range(TB - 2, TB):
                    pe.wait_ge(bank_free[j % 2], b * QB + (j // 2 + 2))
                to = take(LATT)
                for c in range(DC):
                    ins = pe.matmul(to[:, :], k.wkv1[:, c, :], xT[:, c, :], start=(c == 0), stop=(c == DC - 1))
                ins.then_inc(bank_ready[LATT % 2], 1)
                to = take(LATK)
                for j in range(TB):
                    for c in range(DC):
                        ins = pe.matmul(to[:, j * LAT:(j + 1) * LAT], xT[:, c, j * P:(j + 1) * P], k.wkv1[:, c, 0:LAT],
                                        start=(c == 0), stop=(c == DC - 1))
                ins.then_inc(bank_ready[LATK % 2], 1)
                for p in range(PAIRS):
                    to = take(Q + p)
                    for c in range(DC):
                        ins = pe.matmul(to[:, :], k.absorb[:, c, p * P:(p + 1) * P], xT[:, c, :],
                                        start=(c == 0), stop=(c == DC - 1))
                    ins.then_inc(bank_ready[(Q + p) % 2], 1)

                def step(m, u, i):
                    g = b * NU + m
                    if live(m, 0):
                        par, tile, hh = place(u, 0)
                        if u % UP == 0:
                            pe.wait_ge(q_staged, b * PAIRS + i * 2 + (u // UP + 1))
                        pe.wait_ge(p_ready, g + 1)
                        query = qs[par][:, hh, tile * P:(tile + 1) * P]
                        pe.matmul(ps_s[u % 2][:, :], query, latT[0][:, :], start=True, stop=False)
                        pe.matmul(ps_s[u % 2][:, :], query, latT[1][:, :], start=False, stop=True).then_inc(s_ready, 1)
                    if live(m, TLAG):
                        pe.wait_ge(scaled, g - (TLAG - 1))
                        pe.wait_ge(pT_ready, g - (TLAG - 1))
                        for t in range(TB):
                            ins = pe.transpose(ps_p[(u - TLAG) % 2][:, t, :], prob[(u - TLAG) % 4][:, t * P:(t + 1) * P],
                                               k.ident[:, :])
                        ins.then_inc(pT_raw, 1)
                    for t in range(TB):
                        pair = pair_at(m, u, i, VLAG + t)
                        if pair is None:
                            continue
                        par = place(u, VLAG + t)[0]
                        if t == 0:
                            pe.wait_ge(pT_ready, b * NU + pair * UP + (UP + 2))
                            pe.wait_ge(o_copied, b * PAIRS + pair + 1)
                        for hh in range(2):
                            ins = pe.matmul(ps_v[par][hh * LAT:(hh + 1) * LAT, :], lat[:, t, :], pT[par][:, hh, t, :],
                                            start=(t == 0), stop=(t == TB - 1))
                        if t == TB - 1:
                            ins.then_inc(v_ready, 1)

                steps(pe, step)
                pe.wait_ge(o_copied, b * PAIRS + (PAIRS + 2))
                for t in range(TB):
                    if t >= 2:
                        pe.wait_ge(out_used, b * TB + (t - 1))
                    for p in range(PAIRS):
                        ins = pe.matmul(ps_s[t % 2][:, 0:D], oT[:, p, t * P:(t + 1) * P], k.mix[:, p, :],
                                        start=(p == 0), stop=(p == PAIRS - 1))
                    ins.then_inc(out_ready, 1)

        @block.scalar
        def _(act):
            row_std(act, k)
            with act.Fori(0, B) as b:
                def use(m):
                    act.wait_ge(bank_ready[m % 2], b * QB + (m // 2 + 1))
                    return bank[m % 2]

                for j in range(TB):
                    act.activation(xT[:, :, j * P:(j + 1) * P], use(TR + j)[:, 0:D].rearrange("p (c t) -> p c t", c=DC),
                                   ACT.Copy).then_inc(bank_free[j % 2], 1)
                act.activation(latT[0][:, :], use(LATT), ACT.Copy).then_inc(high_ready, 1)
                act.activation(lat[:, :, :], use(LATK)[:, 0:TB * LAT].rearrange("p (t l) -> p t l", l=LAT),
                               ACT.Copy).then_inc(bank_free[LATK % 2], 1)
                for p in range(PAIRS):
                    src = use(Q + p)
                    act.activation(qa[0:LAT, 2 * p, :], src[0:LAT, :], ACT.Copy)
                    act.activation(qa[LAT:P, 2 * p + 1, :], src[LAT:P, :], ACT.Copy).then_inc(high_ready, 1)

                def step(m, u, i):
                    g = b * NU + m
                    if live(m, TLAG):
                        par, tile, hh = place(u, TLAG)
                        act.wait_ge(pT_raw, g - (TLAG - 1))
                        act.activation(pT[par][:, hh, :, tile * P:(tile + 1) * P], ps_p[(u - TLAG) % 2][:, :, :],
                                       ACT.Copy).then_inc(pT_ready, 1)
                    if live(m, 0):
                        act.wait_ge(nmax_ready, g + 1)
                        act.activation(prob[u % 4][:, :], ps_s[u % 2][:, :], ACT.Exp, bias=nmax[:, u % 2:u % 2 + 1],
                                       scale=SCALE, accum_out=rsum[:, u % 4:u % 4 + 1]).then_inc(p_ready, 1)
                    pair = pair_at(m, u, i, OLAG)
                    if pair is not None:
                        act.wait_ge(v_ready, b * PAIRS + pair + 1)
                        act.activation(oT[:, pair, :], ps_v[place(u, OLAG)[0]][:, :], ACT.Copy).then_inc(o_copied, 1)

                steps(act, step)

        @block.gpsimd
        def _(pool):
            for sem in bank_free:
                pool.sem_inc(sem, 1)
            for sem in (p_ready, pT_ready, o_copied):
                pool.sem_inc(sem, 2)
            with pool.Fori(0, B) as b:
                def stage(i, par):
                    pair = i * 2 + par
                    pool_copy(pool, k, qs[par][:, :, :], qa[:, bass.ds(pair * 2, 2), :].bitcast(F32)).then_inc(q_staged, 1)

                for par in range(2):
                    pool.wait_ge(bank_free[(Q + par) % 2], b * QB + ((Q + par) // 2 + 2))
                    pool.sem_inc(k.sem("passed"), 1)
                    stage(0, par)
                for m in range(Q + PAIRS - 2, Q + PAIRS):
                    pool.wait_ge(bank_free[m % 2], b * QB + (m // 2 + 2))
                    pool.sem_inc(k.sem("passed"), 1)
                with pool.Fori(1, PAIRS // 2) as i:
                    for par in range(2):
                        pool.wait_ge(s_ready, b * NU + i * U2 + (par - 1) * UP)
                        pool.sem_inc(k.sem("passed"), 1)
                        stage(i, par)

        @block.vector
        def _(dve):
            row_stats(dve, k)
            row_rstd(dve, k)
            with dve.Fori(0, B) as b:
                for j in range(TB):
                    if j >= 2:
                        dve.wait_ge(bank_ready[j % 2], b * QB + j // 2)
                    layernorm(dve, k, b * TB + j, xn[j % 2][:, :], xn_ready)
                dve.wait_ge(high_ready, b * (PAIRS + 1) + 1)
                dve.tensor_tensor(latT[1][:, :], bank[LATT % 2], latT[0][:, :].bitcast(F32),
                                  ALU.subtract).then_inc(bank_free[LATT % 2], 1)
                for p in range(PAIRS):
                    src = bank[(Q + p) % 2]
                    dve.wait_ge(high_ready, b * (PAIRS + 1) + (p + 2))
                    dve.tensor_tensor(qa[LAT:P, 2 * p, :], src[0:LAT, :], qa[0:LAT, 2 * p, :].bitcast(F32), ALU.subtract)
                    dve.tensor_tensor(qa[0:LAT, 2 * p + 1, :], src[LAT:P, :], qa[LAT:P, 2 * p + 1, :].bitcast(F32),
                                      ALU.subtract).then_inc(bank_free[(Q + p) % 2], 1)

                def step(m, u, i):
                    g = b * NU + m
                    if live(m, 0):
                        v = slice(u % 2, u % 2 + 1)
                        dve.wait_ge(s_ready, g + 1)
                        dve.tensor_reduce(raw[:, v], ps_s[u % 2][:, :], AX, ALU.max, negate=True).then_inc(max_steps, 1)
                        dve.wait_ge(max_steps, g + 1)
                        dve.tensor_scalar(nmax[:, v], raw[:, v], SCALE, None, ALU.mult).then_inc(nmax_ready, 1)
                    if live(m, 1):
                        v, w = (u - 1) % 2, (u - 1) % 4
                        dve.wait_ge(p_ready, g + 2)
                        dve.reciprocal(rinv[:, v:v + 1], rsum[:, w:w + 1]).then_inc(inv_steps, 1)
                        dve.wait_ge(inv_steps, g)
                        dve.tensor_scalar(prob[w][:, :], prob[w][:, :], rinv[:, v:v + 1], None, ALU.mult)\
                           .then_inc(scaled, 1)

                steps(dve, step)
                for t in range(TB):
                    x = k.X[:, b * TB + t, :]
                    dve.wait_ge(out_ready, b * TB + (t + 1))
                    dve.tensor_tensor(x, ps_s[t % 2][:, 0:D], x, ALU.add).then_inc(out_used, 1)
    k.norms += 1


def expert_layer(nc, k, r):
    with ExitStack() as ctx:
        k.wgu = [ctx.enter_context(nc.sbuf_tensor(f"e{r}_wgu{u}", [P, DC, 2 * M0], F32)) for u in range(AHEAD)]
        k.wdn = [ctx.enter_context(nc.sbuf_tensor(f"e{r}_wdn{u}", [MH, 2, D], F32)) for u in range(AHEAD)]
        route(nc, k, r)
        routed_experts(nc, k, r)


def macaron(nc, w, out):
    with ExitStack() as ctx:
        k = Kit(nc, ctx)
        Steps.passed = k.sem("passed")
        k.w, k.norms = w, 0
        k.X = k.sb("x", [P, NT, D])
        k.row_raw = k.sb("row_raw", [P, NT, 6])
        k.row_mv = k.sb("row_mv", [P, NT, 2])
        k.row_rstd = k.sb("row_rstd", [P, NT])
        k.gateT = k.sb("gateT", [P, DC, E0])
        k.sguT = k.sb("sguT", [P, DC, 2 * MS])
        k.sdT = k.sb("sdT", [P, 3, D])
        k.wvg = k.sb("wvg", [P, DC, 2 * H0 * DV])
        k.wgk0 = k.sb("wgk0", [P, DC, P])
        k.wgk1 = k.sb("wgk1", [P, H0 * DK])
        k.bgk1 = k.sb("bgk1", [P, H0])
        k.wq0 = k.sb("wq0", [P, DC, H0 * DK])
        k.wk0 = k.sb("wk0", [P, DC, H0 * DK])
        k.wo0 = k.sb("wo0", [P, DC, D])
        k.gnorm_row = k.sb("gnorm_row", [1, DV])
        k.gnorm = k.sb("gnorm", [P, DV])
        k.wr1 = k.sb("wr1", [P, DC, E1])
        k.wkv1 = k.sb("wkv1", [P, DC, 2 * LAT])
        k.we1 = k.sb("we1", [P, DC, E1, D])
        k.be1 = k.sb("be1", [P, D])
        k.absorb = k.sb("absorb", [P, DC, H1 * LAT])
        k.mix = k.sb("mix", [P, PAIRS, D])
        k.ident = k.sb("ident", [P, P])
        k.before_bf = k.sb("before_bf", [P, P], BF16)
        k.ones_bf = k.sb("ones_bf", [P, P], BF16)
        k.causal = k.sb("causal", [P, SUB])
        k.chunk_keep = k.sb("chunk_keep", [P, T])
        k.eps = k.sb("eps", [P, 1])
        k.zeros = k.sb("zeros", [P, P])
        k.last_slot = k.sb("last_slot", [E0, CAP])
        k.iota64 = k.sb("iota64", [P, E0])
        k.iota_slot = k.sb("iota_slot", [P, CAP])
        k.token_part = k.sb("token_part", [P, 2, NT])
        k.token1 = k.sb("token1", [P, NT])
        k.member_sum = k.sb("member_sum", [P, 2, E0], BF16)
        k.weight = k.sb("weight", [P, NT, TOPK])
        k.slot = k.sb("slot", [P, NT, TOPK], U32)
        k.table = k.sb("table", [CAP, E0], U32)
        k.xn_rows = nc.dram_tensor("xn_rows", [N, D], F32, kind="Internal").ap()
        k.slot_rows = nc.dram_tensor("slot_rows", [E0 * CAP, D], F32, kind="Internal").ap()
        load_and_prepare(nc, k, w)
        expert_layer(nc, k, 0)
        combine_experts(nc, k, 0)
        linear_attention(nc, k)
        expert_layer(nc, k, 1)
        dense_experts(nc, k, 0, combine=1)
        latent_attention(nc, k)
        dense_experts(nc, k, 1, store=out)


def arrange(a):
    import numpy as np

    c = np.ascontiguousarray
    down = a["L0_ffn_Wd"].transpose(0, 2, 1)
    down_chunks = np.zeros((E0, MH, 2, D), down.dtype)
    down_chunks[:, :, 0] = down[:, 0:MH]
    down_chunks[:, 2 * MH - M0:, 1] = down[:, MH:M0]
    gu = np.concatenate([a["L0_ffn_Wg"].transpose(0, 2, 1), a["L0_ffn_Wu"].transpose(0, 2, 1)], axis=2)
    return {
        "x": c(a["L0_attn_hidden_states"].reshape(N, D)),
        "wqT1": c(a["L1_attn_W_q"].T), "upT1": c(a["L1_attn_W_kv_up"].T), "wo1": c(a["L1_attn_W_o"]),
        "gateT": c(a["L0_ffn_gate_weight"].T),
        "sguT": c(np.concatenate([a["L0_ffn_Sg"].T, a["L0_ffn_Su"].T], axis=1)),
        "sdT": c(a["L0_ffn_Sd"].T),
        "wvg": c(np.concatenate([a["L0_attn_Wv"], a["L0_attn_Wg"]], axis=1)),
        "wgk0": c(a["L0_attn_Wgk0"]), "wgk1": c(a["L0_attn_Wgk1"]),
        "bgk1": c(a["L0_attn_bgk1"].reshape(H0, DK).T), "gnorm": c(a["L0_attn_g_norm_w"]),
        "wq0": c(a["L0_attn_Wq"]), "wk0": c(a["L0_attn_Wk"]), "wo0": c(a["L0_attn_Wo"]),
        "wr1": c(a["L1_ffn_Wr"]),
        "wkv1": c(np.concatenate([a["L1_attn_W_kv_down"], a["L1_attn_W_kv_down"]], axis=1)),
        "we1": c(a["L1_ffn_We"]), "be1": c(a["L1_ffn_be"]),
        "wgu0": c(gu.reshape(E0, DC, P, 2 * M0).transpose(0, 2, 1, 3)),
        "wdn0": c(down_chunks),
    }


def build(nc, arrays):
    w = {n: nc.dram_tensor(n, a.shape, F32, kind="ExternalInput").ap() for n, a in arrays.items()}
    out = nc.dram_tensor("out", [N, D], F32, kind="ExternalOutput").ap()
    macaron(nc, w, out)


def kernel(**inputs):
    import concourse.bacc as bacc
    import numpy as np
    from concourse.bass_utils import run_bass_kernel_spmd

    arrays = arrange({n: np.asarray(a) for n, a in inputs.items()})
    nc = bacc.Bacc("TRN2", target_bir_lowering=False, num_devices=1)
    build(nc, arrays)
    result = run_bass_kernel_spmd(nc, [arrays], core_ids=[0])
    return result.results[0]["out"].reshape(B, T, D)
```

```python
from contextlib import ExitStack

import concourse.bass as bass
from concourse import mybir

ALU = mybir.AluOpType
ACT = mybir.ActivationFunctionType
AX = mybir.AxisListType.X
F32 = mybir.dt.float32
BF16 = mybir.dt.bfloat16
U32 = mybir.dt.uint32
F32R = mybir.dt.float32r

P = 128
B, T, D = 4, 512, 256
N = B * T
NT = N // P
TB = T // P
DC = D // P
EPS = 1e-5

E0, M0, TOPK, NG, TG, CAP = 64, 176, 6, 8, 3, 96
MH = 96
MHC = (0, M0 - MH)
AHEAD = 8
MS = 352
MSC = [(0, 128), (128, 128), (256, 96)]
H0, DK, DV, LR = 8, 128, 32, 16
GATE_NORM = 16.0
SUB = P
NSUB = T // SUB
E1 = 8
H1, DH, LAT = 16, 128, 64
PAIRS = H1 // 2


class Steps:

    passed = None

    def __init__(self, eng, sem, step, per):
        self.eng, self.sem, self.before, self.per, self.n = eng, sem, step * per, per, 0

    def mark(self, ins):
        ins.then_inc(self.sem, 1)
        self.n += 1

    def settle(self, back=0):
        self.eng.wait_ge(self.sem, self.before + self.n - back)

    def settle_apart(self):
        self.settle()
        self.eng.sem_inc(self.passed, 1)

    def close(self):
        assert self.n == self.per, (self.n, self.per)


class Kit:

    def __init__(self, nc, ctx):
        self.nc, self.ctx, self.sems = nc, ctx, {}

    def sb(self, name, shape, dt=F32):
        return self.ctx.enter_context(self.nc.sbuf_tensor("sb_" + name, shape, dt))

    def sem(self, name):
        if name not in self.sems:
            self.sems[name] = self.ctx.enter_context(self.nc.semaphore(name))
        return self.sems[name]


def scoped(nc, ctx):
    def sb(name, shape, dt=F32):
        return ctx.enter_context(nc.sbuf_tensor("sb_" + name, shape, dt))

    def ps(name, shape):
        width = 1
        for m in shape[1:]:
            width *= m
        bank = ctx.enter_context(nc.psum_tensor(name, [P, 512], F32))[0:shape[0], 0:width]
        if len(shape) == 3:
            return bank.rearrange("p (a b) -> p a b", a=shape[1])
        return bank
    return sb, ps


def row_stats(dve, k):
    done = k.sem("row_stats_steps")
    first = 2 * NT * k.norms
    for n in range(NT):
        dve.bn_stats(k.row_raw[:, n, :], k.X[:, n, :]).then_inc(done, 1)
    for n in range(NT):
        dve.wait_ge(done, first + n + 1)
        dve.bn_aggr(k.row_mv[:, n, :], k.row_raw[:, n, :]).then_inc(done, 1)


def row_std(act, k):
    act.wait_ge(k.sem("row_stats_steps"), 2 * NT * (k.norms + 1))
    act.activation(k.row_rstd[:, :], k.row_mv[:, :, 1], ACT.Sqrt, bias=k.eps[:, 0:1]).then_inc(k.sem("row_std_ready"), 1)


def row_rstd(dve, k):
    dve.wait_ge(k.sem("row_std_ready"), k.norms + 1)
    dve.reciprocal(k.row_rstd[:, :], k.row_rstd[:, :]).then_inc(k.sem("row_rstd_ready"), 1)
    dve.wait_ge(k.sem("row_rstd_ready"), k.norms + 1)


def layernorm(dve, k, n, out, ready):
    dve.tensor_scalar(out, k.X[:, n, :], k.row_mv[:, n, 0:1], k.row_rstd[:, bass.ds(n, 1)],
                      ALU.subtract, ALU.mult).then_inc(ready, 1)


def pool_copy(pool, k, out, in_):
    pool.sem_inc(k.sem("passed"), 1)
    return pool.tensor_copy(out, in_)


def load_and_prepare(nc, k, w):
    loaded_x, loaded_ffn = k.sem("x_loaded"), k.sem("w0_ffn_loaded")
    made = k.sem("constants_made")
    with ExitStack() as ctx:
        block = ctx.enter_context(nc.Block())

        @block.sync
        def _(sp):
            sp.dma_start(k.X[:, :, :], w["x"].rearrange("(n p) d -> p n d", p=P)).then_inc(loaded_x, 16)
            for dst, name in ((k.gateT, "gateT"), (k.sguT, "sguT")):
                sp.dma_start(dst[:, :, :], w[name].rearrange("(c p) n -> p c n", p=P)).then_inc(loaded_ffn, 16)
            for c, (m0, m) in enumerate(MSC):
                sp.dma_start(k.sdT[0:m, c, :], w["sdT"][m0:m0 + m, :]).then_inc(loaded_ffn, 16)
            sp.dma_start(k.gnorm_row[:, :], w["gnorm"].rearrange("(a n) -> a n", a=1)).then_inc(k.sem("gnorm_loaded"), 16)

        @block.gpsimd
        def _(pool):
            s = Steps(pool, made, 0, 23)
            s.mark(pool.memset(k.wgk0[:, :, :], 0.0))
            s.mark(pool.memset(k.wgk1[:, :], 0.0))
            s.mark(pool.memset(k.be1[:, :], 0.0))
            s.mark(pool.memset(k.ident[:, :], 0.0))
            s.mark(pool.memset(k.before_bf[:, :], 1.0))
            s.mark(pool.memset(k.ones_bf[:, :], 1.0))
            s.mark(pool.memset(k.causal[:, :], 1.0))
            s.mark(pool.memset(k.chunk_keep[:, :], 1.0))
            s.mark(pool.memset(k.last_slot[:, :], 0.0))
            s.mark(pool.memset(k.eps[:, :], EPS))
            s.mark(pool.memset(k.zeros[:, :], 0.0))
            s.settle()
            s.mark(pool.affine_select(out=k.ident[:, :], in_=k.ident[:, :], compare_op=ALU.not_equal, fill=1.0,
                                      base=0, pattern=[[-1, P]], channel_multiplier=1))
            s.mark(pool.affine_select(out=k.before_bf[:, :], in_=k.before_bf[:, :], compare_op=ALU.is_gt, fill=0.0,
                                      base=0, pattern=[[1, P]], channel_multiplier=-1))
            s.settle()
            s.mark(pool.affine_select(out=k.causal[:, :], in_=k.causal[:, :], compare_op=ALU.is_ge, fill=0.0,
                                      base=0, pattern=[[1, SUB]], channel_multiplier=-1))
            s.settle()
            s.mark(pool.memset(k.chunk_keep[:, :].rearrange("p (c s) -> p c s", s=SUB)[:, :, 0:1], 0.0))
            s.mark(pool.iota(k.iota64[:, :], pattern=[[1, E0]], base=0, channel_multiplier=0,
                             allow_small_or_imprecise_dtypes=True))
            s.mark(pool.iota(k.iota_slot[:, :], pattern=[[1, CAP]], base=0, channel_multiplier=0,
                             allow_small_or_imprecise_dtypes=True))
            s.mark(pool.iota(k.token_part[:, 0, :], pattern=[[0, NT // 2], [P, 2]], base=0, channel_multiplier=1,
                             allow_small_or_imprecise_dtypes=True))
            s.mark(pool.iota(k.token_part[:, 1, :], pattern=[[2 * P, NT // 2], [0, 2]], base=0, channel_multiplier=0,
                             allow_small_or_imprecise_dtypes=True))
            s.mark(pool.iota(k.token1[:, :], pattern=[[P, NT]], base=1, channel_multiplier=1,
                             allow_small_or_imprecise_dtypes=True))
            s.settle()
            s.mark(pool.memset(k.iota_slot[:, CAP - 1:CAP], -1.0))
            pool.wait_ge(k.sem("gnorm_loaded"), 16)
            s.mark(pool.partition_broadcast(k.gnorm[:, :], k.gnorm_row[:, :], channels=P))
            s.settle()
            s.mark(pool.memset(k.member_sum[:, :, :], 0.0))
            s.settle()
            s.close()


def load_attention_weights(sp, k):
    w, made, loaded_w0, loaded_w1 = k.w, k.sem("constants_made"), k.sem("w0_loaded"), k.sem("w1_loaded")
    for dst, name in ((k.wvg, "wvg"), (k.wq0, "wq0"), (k.wk0, "wk0"), (k.wo0, "wo0")):
        sp.dma_start(dst[:, :, :], w[name].rearrange("(c p) n -> p c n", p=P)).then_inc(loaded_w0, 16)
    sp.wait_ge(made, 3)
    sp.dma_start(k.wgk0[:, :, 0:LR], w["wgk0"].rearrange("(c p) n -> p c n", p=P)).then_inc(loaded_w0, 16)
    sp.dma_start(k.wgk1[0:LR, :], w["wgk1"]).then_inc(loaded_w0, 16)
    sp.dma_start(k.bgk1[:, :], w["bgk1"]).then_inc(loaded_w0, 16)
    for dst, name in ((k.wr1, "wr1"), (k.wkv1, "wkv1")):
        sp.dma_start(dst[:, :, :], w[name].rearrange("(c p) n -> p c n", p=P)).then_inc(loaded_w1, 16)
    sp.dma_start(k.be1[0:E1, :], w["be1"]).then_inc(loaded_w1, 16)


def load_dense_experts(sp, k):
    for c in range(DC):
        sp.dma_start(k.we1[:, c, :, :], k.w["we1"].rearrange("e (c p) f -> c p e f", p=P)[c])\
            .then_inc(k.sem("we1_loaded"), 16)


def dense_experts(nc, k, r, store=None, combine=None):
    stats_done, rstd_ready = k.sem("d_stats_steps"), k.sem("d_rstd_ready")
    xn_ready, xT_raw, xT_ready = k.sem("d_xn_ready"), k.sem("d_xT_psum_ready"), k.sem("d_xT_ready")
    high_ready, low_ready = k.sem("d_xT_high_ready"), k.sem("d_xT_low_ready")
    we_high, we_low = k.sem("d_we_high_ready"), k.sem("d_we_low_ready")
    logits_ready, gate_ready = k.sem("d_logits_ready"), k.sem("d_gate_ready")
    gap_ready, egap_ready = k.sem("d_logit_gap_ready"), k.sem("d_exp_gap_ready")
    gateT_raw, gateT_ready = k.sem("d_gateT_psum_ready"), k.sem("d_gateT_ready")
    pair_ready, pair_free = k.sem("d_pair_ready"), k.sem("d_pair_free")
    bias_ready, out_ready, stored = k.sem("d_bias_ready"), k.sem("d_out_ready"), k.sem("d_stored")
    NP = E1 // 2
    with ExitStack() as ctx:
        sb, ps = scoped(nc, ctx)
        we = [sb(f"d{r}_we_{part}", [P, DC, E1, D], F32R) for part in ("high", "low")]
        lnv = [sb(f"d{r}_lnv{u}", [P, 1]) for u in range(2)]
        rstd = [sb(f"d{r}_rstd{u}", [P, 1]) for u in range(2)]
        raw = [sb(f"d{r}_raw{u}", [P, 6]) for u in range(2)]
        mv = [sb(f"d{r}_mv{u}", [P, 2]) for u in range(2)]
        xn = [sb(f"d{r}_xn{u}", [P, D]) for u in range(2)]
        xT = [sb(f"d{r}_xT{u}", [P, DC, P]) for u in range(2)]
        xTs = [[sb(f"d{r}_xT_{part}{u}", [P, DC, P], F32R) for part in ("high", "low")] for u in range(2)]
        top = sb(f"d{r}_top", [P, 8])
        top_i = sb(f"d{r}_top_i", [P, 8], U32)
        top_f = sb(f"d{r}_top_f", [P, 2])
        gap = sb(f"d{r}_gap", [P, 1])
        egap = sb(f"d{r}_egap", [P, 1])
        den = sb(f"d{r}_den", [P, 1])
        w1 = sb(f"d{r}_w1", [P, 1])
        w2 = sb(f"d{r}_w2", [P, 1])
        g1 = sb(f"d{r}_g1", [P, E1])
        g2 = sb(f"d{r}_g2", [P, E1])
        gate = [sb(f"d{r}_gate{u}", [P, P]) for u in range(2)]
        gateT = sb(f"d{r}_gateT", [P, P])
        acc = sb(f"d{r}_acc", [P, D])
        if combine is not None:
            rows = [[sb(f"c{combine}_rows{u}_{j}", [P, D]) for j in range(TOPK)] for u in range(2)]
            at = [sb(f"c{combine}_at{u}", [P, TOPK], U32) for u in range(2)]
        ps_x = ps(f"d{r}_ps_x", [P, DC, P])
        ps_r = ps(f"d{r}_ps_r", [P, E1])
        ps_g = ps(f"d{r}_ps_g", [P, P])
        ps_b = ps(f"d{r}_ps_b", [P, D])
        ps_e = [ps(f"d{r}_ps_e{j}", [P, 2, D]) for j in range(NP)]
        block = ctx.enter_context(nc.Block())

        def live(n):
            return not isinstance(n, int) or n < NT

        def tiles(eng, body):
            with eng.Fori(0, NT // 2 - 2) as i:
                for u in range(2):
                    body(i * 2 + u, u)
            for n in range(NT - 4, NT):
                body(n, n % 2)

        @block.tensor
        def _(pe):
            pe.wait_ge(k.sem("w1_loaded"), 16 * 3)

            def transposed(n, u):
                g = n + r * NT
                pe.wait_ge(xn_ready, g + 1)
                pe.wait_ge(xT_ready, g + 1)
                pe.wait_ge(high_ready, g + 1)
                for c in range(DC):
                    ins = pe.transpose(ps_x[:, c, :], xn[u][:, c * P:(c + 1) * P], k.ident[:, :])
                ins.then_inc(xT_raw, 1)

            def logits(n, u):
                g = n + r * NT
                pe.wait_ge(xT_ready, g + 2)
                for c in range(DC):
                    ins = pe.matmul(ps_r[:, :], xT[u][:, c, :], k.wr1[:, c, :], start=(c == 0), stop=(c == DC - 1))
                ins.then_inc(logits_ready, 1)

            def pair(n, u, j):
                g = n + r * NT
                pe.wait_ge(pair_free, g * NP + (j + 1))
                m = 0
                for xpart, wpart in ((0, 0), (0, 1), (1, 0)):
                    for c in range(DC):
                        ins = pe.matmul(ps_e[j][:, :, :], xTs[u][xpart][:, c, :], we[wpart][:, c, 2 * j:2 * j + 2, :],
                                        start=(m == 0), stop=(m == 3 * DC - 1))
                        m += 1
                ins.then_inc(pair_ready, 1)

            def tile(n, u):
                g = n + r * NT
                pe.wait_ge(high_ready, g + 2)
                pe.wait_ge(low_ready, g + 1)
                pair(n, u, 0)
                if live(n + 1):
                    transposed(n + 1, 1 - u)
                pair(n, u, 1)
                pe.wait_ge(gate_ready, g + 1)
                pe.transpose(ps_g[:, :], gate[u][:, :], k.ident[:, :]).then_inc(gateT_raw, 1)
                if live(n + 1):
                    logits(n + 1, 1 - u)
                pair(n, u, 2)
                pe.wait_ge(gateT_ready, g + 1)
                pe.wait_ge(out_ready, g + 1)
                pe.matmul(ps_b[:, :], gateT[:, :], k.be1[:, :], start=True, stop=True).then_inc(bias_ready, 1)
                pair(n, u, 3)

            transposed(0, 0)
            logits(0, 0)
            pe.wait_ge(we_low, (r + 1) * DC)
            tiles(pe, tile)

        @block.scalar
        def _(act):
            def copies(n, u):
                g = n + r * NT
                act.wait_ge(xT_raw, g + 1)
                act.activation(xT[u][:, :, :], ps_x[:, :, :], ACT.Copy).then_inc(xT_ready, 1)
                act.activation(xTs[u][0][:, :, :], ps_x[:, :, :], ACT.Copy).then_inc(high_ready, 1)

            def inverse_deviation(n, u):
                g = n + r * NT
                act.wait_ge(stats_done, (g + 1) * 2)
                s = Steps(act, k.sem("d_ln_steps"), g, 1)
                s.mark(act.activation(lnv[u][:, :], mv[u][:, 1:2], ACT.Ln, bias=k.eps[:, 0:1]))
                s.settle()
                s.close()
                act.activation(rstd[u][:, :], lnv[u][:, :], ACT.Exp, scale=-0.5).then_inc(rstd_ready, 1)

            def gap_exp(n):
                g = n + r * NT
                act.wait_ge(gap_ready, g + 1)
                act.activation(egap[:, :], gap[:, :], ACT.Exp).then_inc(egap_ready, 1)

            def tile(n, u):
                g = n + r * NT
                if live(n + 1):
                    copies(n + 1, 1 - u)
                act.wait_ge(gateT_raw, g + 1)
                act.activation(gateT[:, :], ps_g[:, :], ACT.Copy).then_inc(gateT_ready, 1)
                if live(n + 1):
                    gap_exp(n + 1)
                if live(n + 3):
                    inverse_deviation(n + 3, 1 - u)

            act.preload_act_table_set("natural_log_exp_and_others")
            act.wait_ge(k.sem("we1_loaded"), 16 * DC)
            for c in range(DC):
                act.activation(we[0][:, c, :, :], k.we1[:, c, :, :], ACT.Copy).then_inc(we_high, 1)
            for n in range(3):
                if n == 2:
                    copies(0, 0)
                    gap_exp(0)
                inverse_deviation(n, n % 2)
            tiles(act, tile)

        if combine is not None:
            @block.gpsimd
            def _(pool):
                with pool.Fori(0, NT // 2) as i:
                    for u in range(2):
                        gather_tile(pool, k, combine, i * 2 + u, u, rows, at)

        @block.vector
        def _(dve):
            if r == 0:
                dve.sem_inc(pair_free, NP)
                for sem in (xT_ready, high_ready, out_ready):
                    dve.sem_inc(sem, 1)
            zeroed = k.sem("d_gates_zeroed")
            for u in range(2):
                dve.memset(gate[u][:, :], 0.0).then_inc(zeroed, 1)
            dve.wait_ge(zeroed, 2 * (r + 1))

            def statistics(n, u):
                g = n + r * NT
                x = k.X[:, n, :]
                if combine is not None:
                    rows_all_added(dve, k, combine, n)
                s = Steps(dve, stats_done, g, 2)
                dve.sem_inc(s.passed, 1)
                s.mark(dve.bn_stats(raw[u][:, :], x))
                s.settle_apart()
                s.mark(dve.bn_aggr(mv[u][:, :], raw[u][:, :]))
                s.close()

            def add(n, u, *which):
                if combine is not None and live(n):
                    for j in which:
                        add_row(dve, k, combine, n, u, rows, j)

            def normalise(n, u):
                g = n + r * NT
                dve.wait_ge(rstd_ready, g + 1)
                dve.tensor_scalar(xn[u][:, :], k.X[:, n, :], mv[u][:, 0:1], rstd[u][:, 0:1],
                                  ALU.subtract, ALU.mult).then_inc(xn_ready, 1)

            def leaders(n, u):
                g = n + r * NT
                s = Steps(dve, k.sem("d_leader_steps"), g, 3)
                dve.wait_ge(high_ready, g + 2)
                dve.tensor_tensor(xTs[u][1][:, :, :], xT[u][:, :, :], xTs[u][0][:, :, :].bitcast(F32),
                                  ALU.subtract).then_inc(low_ready, 1)
                dve.wait_ge(logits_ready, g + 1)
                dve.sem_inc(s.passed, 1)
                s.mark(dve.max(top[:, :], ps_r[:, :]))
                s.settle_apart()
                s.mark(dve.max_index(top_i[:, :], top[:, :], ps_r[:, :]))
                dve.tensor_tensor(gap[:, :], top[:, 1:2], top[:, 0:1], ALU.subtract).then_inc(gap_ready, 1)
                s.settle()
                s.mark(dve.tensor_copy(top_f[:, :], top_i[:, 0:2]))
                s.settle()
                s.close()

            def gates(n, u, between):
                g = n + r * NT
                s = Steps(dve, k.sem("d_gate_steps"), g, 5)
                dve.wait_ge(egap_ready, g + 1)
                s.mark(dve.tensor_scalar(den[:, :], egap[:, :], 2.0, 2.0, ALU.mult, ALU.add))
                between[0]()
                s.settle()
                s.mark(dve.reciprocal(w1[:, :], den[:, :]))
                between[1]()
                s.settle()
                s.mark(dve.tensor_scalar(w2[:, :], egap[:, :], w1[:, 0:1], None, ALU.mult))
                s.mark(dve.tensor_scalar(g1[:, :], k.iota64[:, 0:E1], top_f[:, 0:1], w1[:, 0:1], ALU.is_equal, ALU.mult))
                between[2]()
                s.settle()
                s.mark(dve.tensor_scalar(g2[:, :], k.iota64[:, 0:E1], top_f[:, 1:2], w2[:, 0:1], ALU.is_equal, ALU.mult))
                between[3]()
                s.settle()
                s.close()
                dve.tensor_tensor(gate[u][:, 0:E1], g1[:, :], g2[:, :], ALU.add).then_inc(gate_ready, 1)

            even_added = k.sem("d_even_steps")

            def weigh_even(n, u, j):
                g = n + r * NT
                x = k.X[:, n, :]
                dve.wait_ge(pair_ready, g * NP + (j + 1))
                if j:
                    dve.wait_ge(even_added, g * NP + j)
                dve.scalar_tensor_tensor(out=x, in0=ps_e[j][:, 0, :], scalar=gate[u][:, 2 * j:2 * j + 1], in1=x,
                                         op0=ALU.mult, op1=ALU.add).then_inc(even_added, 1)

            def weigh_odd(n, u, j):
                g = n + r * NT
                src, w = ps_e[j][:, 1, :], gate[u][:, 2 * j + 1:2 * j + 2]
                if j == 0:
                    ins = dve.tensor_scalar(acc[:, :], src, w, None, ALU.mult)
                else:
                    dve.wait_ge(pair_free, g * NP + (NP + j))
                    ins = dve.scalar_tensor_tensor(out=acc[:, :], in0=src, scalar=w, in1=acc[:, :],
                                                   op0=ALU.mult, op1=ALU.add)
                ins.then_inc(pair_free, 1)

            def tile(n, u):
                g = n + r * NT
                x = k.X[:, n, :]
                dve.wait_ge(gate_ready, g + 1)
                weigh_even(n, u, 0)
                add(n + 3, 1 - u, 0)
                weigh_odd(n, u, 0)
                if live(n + 2):
                    normalise(n + 2, u)
                weigh_even(n, u, 1)
                add(n + 3, 1 - u, 1)
                weigh_odd(n, u, 1)
                add(n + 3, 1 - u, 2)
                if live(n + 1):
                    leaders(n + 1, 1 - u)
                weigh_even(n, u, 2)
                add(n + 3, 1 - u, 3)

                def last_even():
                    weigh_even(n, u, 3)
                    add(n + 3, 1 - u, 4)

                def add_up():
                    dve.wait_ge(k.sem("d_even_steps"), g * NP + NP)
                    dve.wait_ge(pair_free, g * NP + 2 * NP)
                    dve.tensor_tensor(x, acc[:, :], x, ALU.add).then_inc(k.sem("d_sum_steps"), 1)
                    add(n + 3, 1 - u, 5)

                rest = [lambda: weigh_odd(n, u, 2), last_even, lambda: weigh_odd(n, u, 3), add_up]
                if live(n + 1):
                    gates(n + 1, 1 - u, rest)
                else:
                    for part in rest:
                        part()
                if live(n + 3):
                    statistics(n + 3, 1 - u)
                dve.wait_ge(bias_ready, g + 1)
                dve.wait_ge(k.sem("d_sum_steps"), g + 1)
                dve.tensor_tensor(x, ps_b[:, :], x, ALU.add).then_inc(out_ready, 1)

            for n in range(2):
                add(n, n, *range(TOPK))
                statistics(n, n)
            normalise(0, 0)
            normalise(1, 1)
            for c in range(DC):
                dve.wait_ge(we_high, r * DC + c + 1)
                dve.tensor_tensor(we[1][:, c, :, :], k.we1[:, c, :, :], we[0][:, c, :, :].bitcast(F32),
                                  ALU.subtract).then_inc(we_low, 1)
            leaders(0, 0)
            add(2, 0, *range(TOPK))
            statistics(2, 0)
            gates(0, 0, [lambda: None] * 4)
            tiles(dve, tile)

        if store is not None:
            @block.sync
            def _(sp):
                with sp.Fori(0, NT) as n:
                    sp.wait_ge(out_ready, n + (r * NT + 2))
                    sp.dma_start(store.rearrange("(n p) d -> n p d", p=P)[n], k.X[:, n, :]).then_inc(stored, 16)
                sp.wait_ge(stored, 16 * NT)


def route(nc, k, r):
    raw_loaded, fold_ready, fold_free = k.sem("w_fold_loaded"), k.sem("w_fold_ready"), k.sem("w_fold_free")
    xn_ready, xT_raw, xT_ready = k.sem("r_xn_ready"), k.sem("r_xT_psum_ready"), k.sem("r_xT_ready")
    xn_stored = [k.sem(f"r_xn_stored{u}") for u in range(4)]
    xnT_ready = k.sem("r_xnT_ready")
    logits_ready, nmax_ready, exp_ready = k.sem("r_logits_ready"), k.sem("r_neg_max_ready"), k.sem("r_exp_ready")
    member_ready, pos_ready = k.sem("r_member_ready"), k.sem("r_positions_ready")
    posf_ready, onehot_ready, onehot_free = k.sem("r_position_k_ready"), k.sem("r_onehots_ready"), k.sem("r_onehots_free")
    slots_ready, table_done = k.sem("r_slots_ready"), k.sem("r_table_done")
    begin_ready, lastT_ready, last_ready = k.sem("r_begin_ready"), k.sem("r_lastT_ready"), k.sem("r_last_ready")
    gu_ready, gu_copied, silu_ready = k.sem("s_gate_up_ready"), k.sem("s_gate_up_copied"), k.sem("s_silu_ready")
    hid_ready, down_ready, down_used = k.sem("s_hidden_ready"), k.sem("s_down_ready"), k.sem("s_down_used")
    G = 4
    GN = NT // G
    GT = G * P
    with ExitStack() as ctx:
        sb, ps = scoped(nc, ctx)
        xn = [sb(f"r{r}_xn{u}", [P, D]) for u in range(4)]
        xT = [sb(f"r{r}_xT{u}", [P, DC, P]) for u in range(2)]
        xnT = sb(f"r{r}_xnT", [P, DC, N])
        nmax = sb(f"r{r}_nmax", [P, 1])
        ex = sb(f"r{r}_ex", [P, E0])
        esum = sb(f"r{r}_esum", [P, 1])
        rsum = sb(f"r{r}_rsum", [P, 1])
        score = sb(f"r{r}_score", [P, E0])
        gmax = sb(f"r{r}_gmax", [P, NG])
        gtop = sb(f"r{r}_gtop", [P, 8])
        gtop_i = sb(f"r{r}_gtop_i", [P, 8], U32)
        gtop_f = sb(f"r{r}_gtop_f", [P, TG])
        ghot = sb(f"r{r}_ghot", [P, TG, NG])
        gmask = sb(f"r{r}_gmask", [P, NG])
        masked = sb(f"r{r}_masked", [P, E0])
        top = sb(f"r{r}_top", [P, 8])
        top_i = sb(f"r{r}_top_i", [P, 8], U32)
        top_f = sb(f"r{r}_top_f", [P, TOPK])
        hot = [sb(f"r{r}_hot{u}", [P, TOPK, E0]) for u in range(2)]
        hot_tok = [sb(f"r{r}_hot_tok{u}", [P, TOPK, 2, E0], BF16) for u in range(2)]
        hot_pos = [sb(f"r{r}_hot_pos{u}", [P, TOPK, CAP], BF16) for u in range(2)]
        member = [sb(f"r{r}_member{u}", [P, E0], BF16) for u in range(2)]
        last = sb(f"r{r}_last", [P, E0])
        picked = sb(f"r{r}_picked", [P, TOPK, E0])
        posf = [sb(f"r{r}_posf{u}", [P, TOPK]) for u in range(2)]
        slot_c = sb(f"r{r}_slot_c", [P, TOPK])
        high = sb(f"r{r}_high", [CAP, E0])
        last_col = sb(f"r{r}_last_col", [E0, 1])
        sgate = sb(f"s{r}_gate", [P, 3, GT])
        sup = sb(f"s{r}_up", [P, 3, GT])
        ps_x = ps(f"r{r}_ps_x", [P, DC, P])
        ps_r = [ps(f"r{r}_ps_r{u}", [P, E0]) for u in range(2)]
        ps_pp = ps(f"r{r}_ps_p", [P, 2, E0])
        ps_p = [ps_pp[:, u, :] for u in range(2)]
        ps_t = ps(f"r{r}_ps_t", [P, 2 * E0])
        ps_s = [ps(f"s{r}_ps{which}", [P, GT]) for which in range(2)]
        ps_f = ps(f"r{r}_ps_f", [P, 512])
        if r == 0:
            wqT = sb("wqT", [P, H1, D])
            upT = sb("upT", [P, H1, LAT])
            wo1 = sb("wo1", [P, H1, D])
        absorb_at = {m: (n % DC, n // DC * 8) for n, m in enumerate((5, 6, 7, NT))}
        mix_at = {NT + 1 + n: 2 * n for n in range(PAIRS // 2)}
        fold_at = {m: n for n, m in enumerate(sorted(list(absorb_at) + list(mix_at)))}
        block = ctx.enter_context(nc.Block())
        kept_table = ps_t[0:CAP, :]
        LAST = NT + G
        PEEL = 2

        def spread(ap, n, m):
            return ap.unsqueeze(2).to_broadcast([P, n, m])

        def folds(m):
            return r == 0 and isinstance(m, int) and m in fold_at

        def repeat(ap, n, m):
            return ap.unsqueeze(1).to_broadcast([P, n, m])

        def live(m, lag):
            return not isinstance(m, int) or 0 <= m - lag < NT

        def steps(eng, body):
            for m in range(PEEL * G):
                body(m, m % G, m // G - 1)
            with eng.Fori(PEEL, GN) as i:
                for t in range(G):
                    body(i * G + t, t, i - 1)
            for m in range(NT, LAST + 1):
                body(m, m % G, m // G - 1)

        def group(q, lag=0):
            return not isinstance(q, int) or 0 <= q - lag < GN

        @block.sync
        def _(sp):
            def store(group):
                for u in range(4):
                    n = group * 4 + u
                    sp.wait_ge(xn_ready, n + (r * NT + 1))
                    sp.dma_start(k.xn_rows.rearrange("(n p) d -> n p d", p=P)[n], xn[u][:, :]).then_inc(xn_stored[u], 16)

            def load_experts(first, last):
                for e in range(first, last):
                    sp.dma_start(k.wgu[e][:, :, :], k.w["wgu0"][e]).then_inc(k.sem(f"e_weights_got{e}"), 16)
                    sp.dma_start(k.wdn[e][:, :, :], k.w["wdn0"][e]).then_inc(k.sem(f"e_weights_got{e}"), 16)

            if r == 0:
                for u in range(4):
                    sp.sem_inc(xn_stored[u], 16)
            if r == 0:
                for dst, name in ((wqT, "wqT1"), (upT, "upT1"), (wo1, "wo1")):
                    sp.dma_start(dst[:, :, :], k.w[name].rearrange("(h p) d -> p h d", p=DH)).then_inc(raw_loaded, 16)
            else:
                load_dense_experts(sp, k)
            store(0)
            if r == 0:
                load_attention_weights(sp, k)
            store(1)
            load_experts(0, AHEAD // 2)
            store(2)
            load_experts(AHEAD // 2, AHEAD)
            store(3)

        @block.tensor
        def _(pe):
            pe.wait_ge(k.sem("w0_ffn_loaded"), 16 * 5)
            if r == 0:
                pe.sem_inc(onehot_free, 2)
                pe.sem_inc(gu_copied, 1)
                pe.sem_inc(down_ready, 1)
                pe.sem_inc(down_used, 1)
            pe.wait_ge(begin_ready, 2 * r + 2)
            pe.matmul(kept_table, k.zeros[:, 0:CAP], k.zeros[:, :], start=True, stop=False)

            def shared(t, q):
                qq = q + r * GN
                if group(q) and t < len(MSC):
                    m0, rows = MSC[t]
                    if t == 0:
                        pe.wait_ge(down_used, qq + 1)
                        pe.wait_ge(xnT_ready, (qq + 1) * G)
                    pe.wait_ge(gu_copied, qq * 3 + (t + 1))
                    for which in range(2):
                        for d in range(DC):
                            ins = pe.matmul(ps_s[which][0:rows, :], k.sguT[:, d, which * MS + m0:which * MS + m0 + rows],
                                            xnT[:, d, bass.ds(q * GT, GT)], start=(d == 0), stop=(d == DC - 1))
                    ins.then_inc(gu_ready, 1)
                elif group(q):
                    pe.wait_ge(gu_copied, qq * 3 + 4)
                    pe.wait_ge(hid_ready, qq + 1)
                    for tile in range(G):
                        to = ps_s[tile // 2][:, (tile % 2) * D:(tile % 2 + 1) * D]
                        for c, (m0, rows) in enumerate(MSC):
                            ins = pe.matmul(to, sgate[0:rows, c, tile * P:(tile + 1) * P], k.sdT[0:rows, c, :],
                                            start=(c == 0), stop=(c == 2))
                    ins.then_inc(down_ready, 1)

            def step(m, t, q):
                gm = m + r * NT
                qq = q + r * GN
                if live(m, 1):
                    g, u = gm - 1, (t - 1) % 2
                    pe.wait_ge(xn_ready, g + 1)
                    if not isinstance(m, int) or m > 1 or r > 0:
                        pe.wait_ge(xnT_ready, g)
                    for c in range(DC):
                        ins = pe.transpose(ps_x[:, c, :], xn[(t - 1) % 4][:, c * P:(c + 1) * P], k.ident[:, :])
                    ins.then_inc(xT_raw, 1)
                    pe.wait_ge(xT_ready, g + 1)
                    for c in range(DC):
                        ins = pe.matmul(ps_r[u][:, :], xT[u][:, c, :], k.gateT[:, c, :], start=(c == 0), stop=(c == DC - 1))
                    ins.then_inc(logits_ready, 1)
                if live(m, 3):
                    g, u = gm - 3, (t - 1) % 2
                    pe.wait_ge(member_ready, g + 1)
                    pe.matmul(ps_p[u][:, :], k.before_bf[:, :], member[u][:, :], start=True, stop=False)
                    pe.matmul(ps_p[u][:, :], k.ones_bf[:, :], k.member_sum[:, 1 - u, :], start=False,
                              stop=True).then_inc(pos_ready, 1)
                if live(m, 4):
                    g, u = gm - 4, t % 2
                    pe.wait_ge(onehot_ready, g + 1)
                    for j in range(TOPK):
                        ins = pe.matmul(kept_table, hot_pos[u][:, j, :], hot_tok[u][:, j, :, :], start=False, stop=False)
                    ins.then_inc(onehot_free, 1)
                if isinstance(m, int) and m - 3 == NT:
                    pe.wait_ge(slots_ready, (r + 1) * NT)
                    pe.wait_ge(xnT_ready, (r + 1) * NT)
                    pe.transpose(ps_x[0:E0, 0, :], last[:, :], k.ident[:, :]).then_inc(lastT_ready, 1)
                    pe.wait_ge(last_ready, r + 1)
                    pe.matmul(kept_table, k.last_slot[:, :], k.ident[0:E0, :], start=False, stop=True).then_inc(table_done, 1)
                shared(t, q)
                if folds(m):
                    pe.wait_ge(raw_loaded, 48)
                    if fold_at[m] > 0:
                        pe.wait_ge(fold_free, fold_at[m])
                    if m in absorb_at:
                        c, h0 = absorb_at[m]
                        for h in range(h0, h0 + 8):
                            ins = pe.matmul(ps_f[:, (h - h0) * LAT:(h - h0 + 1) * LAT], wqT[:, h, c * P:(c + 1) * P],
                                            upT[:, h, :], start=True, stop=True)
                    else:
                        for pair in range(2):
                            for hh in range(2):
                                h = 2 * (mix_at[m] + pair) + hh
                                ins = pe.matmul(ps_f[hh * LAT:(hh + 1) * LAT, pair * D:(pair + 1) * D], upT[:, h, :],
                                                wo1[:, h, :], start=True, stop=True)
                    ins.then_inc(fold_ready, 1)

            steps(pe, step)

        @block.scalar
        def _(act):
            row_std(act, k)

            def step(m, t, q):
                gm = m + r * NT
                qq = q + r * GN
                if live(m, 1):
                    g, u = gm - 1, (t - 1) % 2
                    act.wait_ge(xT_raw, g + 1)
                    act.activation(xT[u][:, :, :], ps_x[:, :, :], ACT.Copy).then_inc(xT_ready, 1)
                    act.activation(xnT[:, :, bass.ds((m - 1) * P, P)], ps_x[:, :, :], ACT.Copy).then_inc(xnT_ready, 1)
                if live(m, 2):
                    g, u = gm - 2, t % 2
                    act.wait_ge(nmax_ready, g + 1)
                    act.activation(ex[:, :], ps_r[u][:, :], ACT.Exp, bias=nmax[:, 0:1],
                                   accum_out=esum[:, 0:1]).then_inc(exp_ready, 1)
                if group(q) and t < len(MSC):
                    rows = MSC[t][1]
                    act.wait_ge(gu_ready, qq * 3 + (t + 1))
                    if t == 0:
                        act.wait_ge(down_ready, qq + 1)
                    act.activation(sgate[0:rows, t, :], ps_s[0][0:rows, :], ACT.Copy)
                    act.activation(sup[0:rows, t, :], ps_s[1][0:rows, :], ACT.Copy).then_inc(gu_copied, 1)
                    if t == 2:
                        act.wait_ge(gu_copied, qq * 3 + 4)
                        act.activation(sgate[:, 0:2, :], sgate[:, 0:2, :], ACT.Silu)
                        act.activation(sgate[0:rows, 2, :], sgate[0:rows, 2, :], ACT.Silu).then_inc(silu_ready, 1)

                if folds(m):
                    act.wait_ge(fold_ready, fold_at[m] + 1)
                    if m in absorb_at:
                        c, h0 = absorb_at[m]
                        act.activation(k.absorb[:, c, h0 * LAT:(h0 + 8) * LAT], ps_f[:, :], ACT.Copy,
                                       scale=DH ** -0.5).then_inc(fold_free, 1)
                    else:
                        act.activation(k.mix[:, mix_at[m]:mix_at[m] + 2, :], ps_f[:, :].rearrange("p (a d) -> p a d", d=D),
                                       ACT.Copy).then_inc(fold_free, 1)

            steps(act, step)

        @block.gpsimd
        def _(pool):
            def step(m, t, q):
                gm = m + r * NT
                qq = q + r * GN
                if live(m, 4):
                    g, u = gm - 4, t % 2
                    pool.wait_ge(onehot_free, g + 1)
                    pool.wait_ge(posf_ready, g + 1)
                    for part in range(2):
                        pool.tensor_tensor(hot_tok[u][:, :, part, :], hot[u][:, :, :],
                                           spread(k.token_part[:, part, bass.ds(m - 4, 1)], 1, E0)
                                           .to_broadcast([P, TOPK, E0]), ALU.mult)
                    for j in range(TOPK):
                        ins = pool.tensor_scalar(hot_pos[u][:, j, :], k.iota_slot[:, :], posf[u][:, j:j + 1], None,
                                                 ALU.is_equal)
                    ins.then_inc(onehot_ready, 1)

            steps(pool, step)

        @block.vector
        def _(dve):
            dve.wait_ge(k.sem("x_loaded"), 16)
            row_stats(dve, k)
            dve.memset(last[:, :], 0.0).then_inc(begin_ready, 1)
            dve.memset(k.member_sum[:, 1, :], 0.0).then_inc(begin_ready, 1)
            dve.wait_ge(begin_ready, 2 * r + 2)

            def step(m, t, q):
                gm = m + r * NT
                qq = q + r * GN

                def normalised():
                    if live(m, 0):
                        dve.wait_ge(xn_stored[t], (gm + (4 - t)) * 4)
                        if not isinstance(m, int) or m > 3 or r > 0:
                            dve.wait_ge(xT_raw, gm - 3)
                        layernorm(dve, k, m, xn[t][:, :], xn_ready)

                def row_max():
                    if live(m, 2):
                        dve.wait_ge(logits_ready, gm - 1)
                        dve.tensor_reduce(nmax[:, :], ps_r[t % 2][:, :], AX, ALU.max, negate=True)\
                           .then_inc(nmax_ready, 1)

                slot_steps = k.sem("r_slot_steps")

                def positions():
                    g, u = gm - 4, t % 2
                    dve.wait_ge(pos_ready, g + 1)
                    dve.tensor_tensor(picked[:, :, :], hot[u][:, :, :], repeat(ps_p[u][:, :], TOPK, E0),
                                      ALU.mult).then_inc(slot_steps, 1)

                def positions_k():
                    g, u = gm - 4, t % 2
                    dve.wait_ge(slot_steps, g * 2 + 1)
                    dve.tensor_reduce(posf[u][:, :], picked[:, :, :], AX, ALU.add).then_inc(posf_ready, 1)

                def slots_capped():
                    g, u = gm - 4, t % 2
                    dve.wait_ge(posf_ready, g + 1)
                    dve.tensor_scalar(slot_c[:, :], posf[u][:, :], float(CAP - 1), None, ALU.min).then_inc(slot_steps, 1)

                def slots():
                    g = gm - 4
                    dve.wait_ge(slot_steps, g * 2 + 2)
                    dve.scalar_tensor_tensor(out=k.slot[:, m - 4, :], in0=top_f[:, :], scalar=float(CAP), in1=slot_c[:, :],
                                             op0=ALU.mult, op1=ALU.add).then_inc(slots_ready, 1)

                def shared_added():
                    if group(q, 1) and t == 0:
                        dve.wait_ge(down_ready, qq + 1)
                        for half in range(2):
                            x = k.X[:, bass.ds((q - 1) * G + half * 2, 2), :]
                            ins = dve.scalar_tensor_tensor(out=x, in0=ps_s[half][:, :].rearrange("p (n d) -> p n d", d=D),
                                                           scalar=0.5, in1=x, op0=ALU.mult, op1=ALU.add)
                        ins.then_inc(down_used, 1)

                def hidden():
                    if group(q) and t == 3:
                        rows = MSC[2][1]
                        dve.wait_ge(silu_ready, qq + 1)
                        dve.tensor_tensor(sgate[:, 0:2, :], sgate[:, 0:2, :], sup[:, 0:2, :], ALU.mult)
                        dve.tensor_tensor(sgate[0:rows, 2, :], sgate[0:rows, 2, :], sup[0:rows, 2, :],
                                          ALU.mult).then_inc(hid_ready, 1)

                if not live(m, 3):
                    normalised()
                    row_max()
                    if live(m, 4):
                        positions()
                        positions_k()
                        slots_capped()
                        slots()
                    hidden()
                    shared_added()
                    return
                u = (t - 1) % 2
                g = gm - 3
                s = Steps(dve, k.sem("r_steps"), g, 15)
                before = live(m, 4)
                dve.wait_ge(exp_ready, g + 1)
                s.mark(dve.reciprocal(rsum[:, :], esum[:, :]))
                if before:
                    positions()
                s.settle()
                s.mark(dve.tensor_scalar(score[:, :], ex[:, :], rsum[:, 0:1], None, ALU.mult))
                if before:
                    positions_k()
                s.settle()
                s.mark(dve.tensor_reduce(gmax[:, :], score[:, :].rearrange("p (g e) -> p g e", g=NG), AX, ALU.max))
                if before:
                    slots_capped()
                s.settle_apart()
                s.mark(dve.max(gtop[:, :], gmax[:, :]))
                if before:
                    slots()
                s.settle_apart()
                s.mark(dve.max_index(gtop_i[:, :], gtop[:, :], gmax[:, :]))
                normalised()
                s.settle()
                s.mark(dve.tensor_copy(gtop_f[:, :], gtop_i[:, 0:TG]))
                s.settle()
                s.mark(dve.tensor_tensor(ghot[:, :, :], repeat(k.iota64[:, 0:NG], TG, NG),
                                         spread(gtop_f[:, :], TG, NG), ALU.is_equal))
                s.settle()
                s.mark(dve.tensor_reduce(gmask[:, :], ghot[:, :, :].rearrange("p k g -> p g k"), AX, ALU.add))
                s.settle()
                s.mark(dve.tensor_tensor(masked[:, :].rearrange("p (g e) -> p g e", g=NG),
                                         score[:, :].rearrange("p (g e) -> p g e", g=NG),
                                         spread(gmask[:, :], NG, E0 // NG), ALU.mult))
                s.settle_apart()
                s.mark(dve.max(top[:, :], masked[:, :]))
                row_max()
                s.settle_apart()
                s.mark(dve.max_index(top_i[:, :], top[:, :], masked[:, :]))
                dve.tensor_scalar(k.weight[:, m - 3, :], top[:, 0:TOPK], 0.5, None, ALU.mult)
                if before:
                    dve.wait_ge(slots_ready, g)
                dve.wait_ge(onehot_free, g + 1)
                s.settle()
                s.mark(dve.tensor_copy(top_f[:, :], top_i[:, 0:TOPK]))
                s.settle()
                s.mark(dve.tensor_tensor(hot[u][:, :, :], repeat(k.iota64[:, :], TOPK, E0),
                                         spread(top_f[:, :], TOPK, E0), ALU.is_equal))
                s.settle()
                with nc.allow_low_precision(reason="sums of zeros and ones up to 16 are exact"):
                    dve.tensor_reduce(member[u][:, :], hot[u][:, :, :].rearrange("p k e -> p e k"), AX,
                                      ALU.add).then_inc(member_ready, 1)
                    dve.wait_ge(member_ready, g + 1)
                    s.mark(dve.tensor_tensor(k.member_sum[:, u, :], k.member_sum[:, 1 - u, :], member[u][:, :], ALU.add))
                s.mark(dve.scalar_tensor_tensor(out=last[:, :], in0=member[u][:, :], scalar=k.token1[:, bass.ds(m - 3, 1)],
                                                in1=last[:, :], op0=ALU.mult, op1=ALU.max))
                hidden()
                shared_added()
                s.settle()
                s.close()

            row_rstd(dve, k)
            for m in range(PEEL * G):
                step(m, m % G, m // G - 1)
            with dve.Fori(PEEL, GN) as i:
                for t in range(G):
                    step(i * G + t, t, i - 1)
            for m in range(NT, LAST + 1):
                step(m, m % G, m // G - 1)
                if m - 3 == NT:
                    dve.wait_ge(lastT_ready, r + 1)
                    f = k.sem("r_last_steps")
                    dve.tensor_reduce(last_col[:, :], ps_x[0:E0, 0, :], AX, ALU.max).then_inc(f, 1)
                    dve.wait_ge(f, 2 * r + 1)
                    dve.tensor_scalar(k.last_slot[:, CAP - 1:CAP], last_col[:, :], -1.0, 0.0, ALU.add,
                                      ALU.max).then_inc(last_ready, 1)
                    dve.wait_ge(table_done, r + 1)
                    dve.tensor_copy(high[:, :], kept_table[:, E0:2 * E0]).then_inc(f, 1)
                    dve.wait_ge(f, 2 * r + 2)
                    dve.tensor_tensor(k.table[:, :], high[:, :], kept_table[:, 0:E0], ALU.add)
    k.norms += 1


def pipelined(eng, body, first, last, unroll):
    rounds = (last + 1 - first) // unroll
    for s in range(first):
        body(s, s % unroll)
    assert first % unroll == 0
    with eng.Fori(0, rounds) as i:
        for u in range(unroll):
            body(i * unroll + (first + u), u)
    for s in range(first + rounds * unroll, last + 1):
        body(s, s % unroll)


def routed_experts(nc, k, r):
    U, GA, LAG = AHEAD, 4, 3
    staged = k.sem("e_index_staged")
    got = [k.sem(f"e_tokens_got{u}") for u in range(GA)]
    w_got = [k.sem(f"e_weights_got{u}") for u in range(U)]
    xT_raw, xT_ready = k.sem("e_xT_psum_ready"), k.sem("e_xT_ready")
    gu_ready, act_ready, h_ready = k.sem("e_gate_up_ready"), k.sem("e_silu_ready"), k.sem("e_hidden_ready")
    hT_raw, hT_ready = k.sem("e_hT_psum_ready"), k.sem("e_hT_ready")
    dn_ready, y_ready = k.sem("e_down_ready"), k.sem("e_y_ready")
    y_stored = [k.sem(f"e_y_stored{u}") for u in range(2)]
    with ExitStack() as ctx:
        sb, ps = scoped(nc, ctx)
        index = [sb(f"e{r}_index{u}", [CAP, 1], U32) for u in range(GA)]
        x = [sb(f"e{r}_x{u}", [CAP, D]) for u in range(GA)]
        xT = [sb(f"e{r}_xT{u}", [P, DC, CAP]) for u in range(2)]
        wgu, wdn = k.wgu, k.wdn
        sg = [sb(f"e{r}_sg{u}", [CAP, M0]) for u in range(2)]
        h = [sb(f"e{r}_h{u}", [CAP, M0]) for u in range(2)]
        hT = [sb(f"e{r}_hT{u}", [MH, 2, CAP]) for u in range(2)]
        y = [sb(f"e{r}_y{u}", [CAP, D]) for u in range(2)]
        ps_x = [ps(f"e{r}_ps_x{u}", [P, DC, CAP]) for u in range(2)]
        ps_gu = [ps(f"e{r}_ps_gu{u}", [CAP, 2 * M0]) for u in range(2)]
        ps_h = [ps(f"e{r}_ps_h{u}", [MH, 2, CAP]) for u in range(2)]
        ps_y = [ps(f"e{r}_ps_y{u}", [CAP, D]) for u in range(2)]
        block = ctx.enter_context(nc.Block())
        last = E0 - 1 + LAG

        def later(s, n):
            return not isinstance(s, int) or s >= n or r > 0

        def live(s, lag):
            return not isinstance(s, int) or 0 <= s - lag < E0

        @block.sync
        def _(sp):
            def load(e, u):
                g = e + r * E0
                sp.wait_ge(gu_ready, g - (U - 1))
                sp.dma_start(wgu[u][:, :, :], k.w["wgu0"][e]).then_inc(w_got[u], 16)
                sp.wait_ge(dn_ready, g - (U - 1))
                sp.dma_start(wdn[u][:, :, :], k.w["wdn0"][e]).then_inc(w_got[u], 16)

            with sp.Fori(1, E0 // U) as i:
                for u in range(U):
                    load(i * U + u, u)

        @block.gpsimd
        def _(pool):
            for u in range(4):
                pool.wait_ge(k.sem(f"r_xn_stored{u}"), 16 * ((r + 1) * NT // 4 + 1))

            def gather(e, u):
                g = e + r * E0
                if later(e, GA):
                    pool.wait_ge(xT_raw, g - (GA - 1))
                pool_copy(pool, k, index[u][:, :], k.table[:, bass.ds(e, 1)]).then_inc(staged, 1)
                pool.wait_ge(staged, g + 1)
                pool.sem_inc(k.sem("passed"), 1)
                pool.indirect_dma_start(x[u][:, :], None, k.xn_rows[:, :],
                                        bass.IndirectOffsetOnAxis(ap=index[u][:, 0:1], axis=0)).then_inc(got[u], 16)

            pipelined(pool, gather, GA, E0 - 1, GA)

        @block.tensor
        def _(pe):
            def step(s, u):
                g = s + r * E0
                if live(s, 0):
                    v = u % 2
                    a = u % GA
                    pe.wait_ge(got[a], (g + (GA - a)) * (16 // GA))
                    if later(s, 2):
                        pe.wait_ge(xT_ready, g - 1)
                    for c in range(DC):
                        ins = pe.transpose(ps_x[v][:, c, :], x[a][:, c * P:(c + 1) * P], k.ident[0:CAP, 0:CAP])
                    ins.then_inc(xT_raw, 1)
                if live(s, 1):
                    v = (u - 1) % 2
                    pe.wait_ge(xT_ready, g)
                    pe.wait_ge(w_got[(u - 1) % U], (g - 1 + (U - (u - 1) % U)) * (32 // U))
                    if later(s, 3):
                        pe.wait_ge(h_ready, g - 2)
                    for c in range(DC):
                        ins = pe.matmul(ps_gu[v][:, :], xT[v][:, c, :], wgu[(u - 1) % U][:, c, :],
                                        start=(c == 0), stop=(c == DC - 1))
                    ins.then_inc(gu_ready, 1)
                if live(s, 2):
                    v = u % 2
                    pe.wait_ge(h_ready, g - 1)
                    if later(s, 4):
                        pe.wait_ge(hT_ready, g - 3)
                    for c in range(2):
                        ins = pe.transpose(ps_h[v][:, c, :], h[v][:, MHC[c]:MHC[c] + MH], k.ident[0:CAP, 0:CAP])
                    ins.then_inc(hT_raw, 1)
                if live(s, 3):
                    v = (u - 1) % 2
                    pe.wait_ge(hT_ready, g - 2)
                    if later(s, 5):
                        pe.wait_ge(y_ready, g - 4)
                    for c in range(2):
                        ins = pe.matmul(ps_y[v][:, :], hT[v][:, c, :], wdn[(u - 3) % U][:, c, :],
                                        start=(c == 0), stop=(c == 1))
                    ins.then_inc(dn_ready, 1)

            pipelined(pe, step, U, last, U)

        @block.scalar
        def _(act):
            def step(s, u):
                g = s + r * E0
                if live(s, 0):
                    v = u % 2
                    act.wait_ge(xT_raw, g + 1)
                    if later(s, 2):
                        act.wait_ge(gu_ready, g - 1)
                    act.activation(xT[v][:, :, :], ps_x[v][:, :, :], ACT.Copy).then_inc(xT_ready, 1)
                if live(s, 1):
                    v = (u - 1) % 2
                    act.wait_ge(gu_ready, g)
                    if later(s, 3):
                        act.wait_ge(h_ready, g - 2)
                    act.activation(sg[v][:, :], ps_gu[v][:, 0:M0], ACT.Silu).then_inc(act_ready, 1)
                if live(s, 3):
                    v = (u - 1) % 2
                    act.wait_ge(dn_ready, g - 2)
                    if later(s, 5):
                        act.wait_ge(y_stored[v], (g - (3 + v)) * 8)
                    act.activation(y[v][:, :], ps_y[v][:, :], ACT.Copy).then_inc(y_ready, 1)
                    act.wait_ge(y_ready, g - 2)
                    act.dma_start(k.slot_rows.rearrange("(e c) d -> e c d", c=CAP)[s - 3], y[v][:, :])\
                       .then_inc(y_stored[v], 16)

            pipelined(act, step, U, last, U)
            for v in range(2):
                act.wait_ge(y_stored[v], 16 * ((r + 1) * E0 // 2))

        @block.vector
        def _(dve):
            def step(s, u):
                g = s + r * E0
                if live(s, 1):
                    v = (u - 1) % 2
                    dve.wait_ge(act_ready, g)
                    if later(s, 3):
                        dve.wait_ge(hT_raw, g - 2)
                    dve.tensor_tensor(h[v][:, :], sg[v][:, :], ps_gu[v][:, M0:2 * M0], ALU.mult).then_inc(h_ready, 1)
                if live(s, 2):
                    v = u % 2
                    dve.wait_ge(hT_raw, g - 1)
                    if later(s, 4):
                        dve.wait_ge(dn_ready, g - 3)
                    dve.tensor_copy(hT[v][:, :, :], ps_h[v][:, :, :]).then_inc(hT_ready, 1)

            pipelined(dve, step, U, last, U)


def gather_tile(pool, k, r, n, u, rows, at):
    staged = k.sem("c_slots_staged")
    g = n + r * NT
    pool.wait_ge(k.sem("c_rows_used"), g + 1)
    pool_copy(pool, k, at[u][:, :], k.slot[:, n, :]).then_inc(staged, 1)
    pool.wait_ge(staged, g + 1)
    pool.sem_inc(k.sem("passed"), 1)
    for j in range(TOPK):
        pool.indirect_dma_start(rows[u][j][:, :], None, k.slot_rows[:, :],
                                bass.IndirectOffsetOnAxis(ap=at[u][:, j:j + 1], axis=0))\
            .then_inc(k.sem(f"c_rows_got{u}"), 16)


def add_row(dve, k, r, n, u, rows, j):
    g = n + r * NT
    x = k.X[:, n, :]
    added = k.sem("c_rows_added")
    if j == 0:
        dve.wait_ge(k.sem(f"c_rows_got{u}"), (g + (2 - u)) * (8 * TOPK))
    else:
        dve.wait_ge(added, g * TOPK + j)
    dve.scalar_tensor_tensor(out=x, in0=rows[u][j][:, :], scalar=k.weight[:, n, j:j + 1],
                             in1=x, op0=ALU.mult, op1=ALU.add).then_inc(added, 1)


def rows_all_added(dve, k, r, n):
    dve.wait_ge(k.sem("c_rows_added"), (n + r * NT) * TOPK + TOPK)
    dve.sem_inc(k.sem("c_rows_used"), 1)


def linear_attention(nc, k):
    stats_done, lnv_ready, rstd_ready = k.sem("g_stats_steps"), k.sem("g_ln_var_ready"), k.sem("g_rstd_ready")
    A = 3
    HG = H0 // 2
    MID = SUB // 2 - 1
    VW = H0 * DV
    xn_ready, abs_ready, soft_ready = k.sem("g_xn_ready"), k.sem("g_abs_ready"), k.sem("g_softplus_ready")
    cen_ready, edge_ready = k.sem("g_centred_ready"), k.sem("g_edges_ready")
    up_ready, down_ready = k.sem("g_exp_up_ready"), k.sem("g_exp_down_ready")
    sig_ready, v_ready, gw_ready = k.sem("g_sigmoid_ready"), k.sem("g_values_ready"), k.sem("g_gate_ready")
    act_steps, ln_steps, dve_steps, gate_steps, pool_steps = (k.sem("g_exp_steps"), k.sem("g_ln_steps"),
                                                              k.sem("g_state_steps"), k.sem("g_gate_steps"),
                                                              k.sem("g_gw_steps"))
    at_ready, at_masked = k.sem("g_scores_ready"), k.sem("g_scores_masked")
    sm_ready, kv_ready, kv_used = k.sem("g_state_ready"), k.sem("g_kv_ready"), k.sem("g_kv_used")
    o_ready, o_copied, sq_ready, on_ready = (k.sem("g_o_ready"), k.sem("g_o_copied"), k.sem("g_squares_ready"),
                                             k.sem("g_normed_ready"))
    out_ready, out_used = k.sem("g_out_ready"), k.sem("g_out_used")
    ms_ready, rms_ready = k.sem("g_mean_square_ready"), k.sem("g_rms_ready")
    edges_taken = k.sem("g_edges_taken")
    a_ready = [k.sem(f"g_bank_ready{a}") for a in range(A)]
    a_free = [k.sem(f"g_bank_free{a}") for a in range(A)]

    tr, low_unit, vg_units = [("tr", j) for j in range(TB)], [("low", 0)], [("vg", j) for j in range(TB)]
    z, qu, ku = ([(name, h) for h in range(H0)] for name in ("z", "q", "k"))
    kt = [[("kt", j, half) for half in range(2)] for j in range(TB)]
    oo = [("o", j) for j in range(TB)]
    stage_first = tr + low_unit + z + vg_units + qu + ku
    stage_round = (kt[0] + tr + low_unit + z[0:HG] + kt[1] + z[HG:] + oo[0:1] + vg_units[0:2] + kt[2] + vg_units[2:]
                   + oo[1:2] + kt[3] + oo[2:3] + qu[0:3] + oo[3:4] + qu[3:] + ku)
    stage_last = kt[0] + kt[1] + oo[0:1] + kt[2] + oo[1:2] + kt[3] + oo[2:4]
    for stage in (stage_first, stage_round, stage_last):
        assert len(stage) % A == 0

    def stage_at(order, base):
        return {key: m for m, key in enumerate(order)}, base

    first_uses, round_uses = len(stage_first) // A, len(stage_round) // A
    FIRST = stage_at(stage_first, 0)
    FINAL = stage_at(stage_last, first_uses + (B - 1) * round_uses)

    with ExitStack() as ctx:
        sb, ps = scoped(nc, ctx)
        xn = [sb(f"g_xn{j}", [P, D]) for j in range(TB)]
        xT = sb("g_xT", [P, DC, T])
        low = sb("g_low", [P, T])
        zm = sb("g_zm", [P, H0, T])
        za = sb("g_za", [P, H0, T])
        qp = sb("g_qp", [P, H0, T])
        kp = sb("g_kp", [P, H0, T])
        mid = sb("g_mid", [P, H0, NSUB])
        e_mid, e_all, e_mid_next, e_all_next, e_rest = (sb(f"g_e_{n}", [P, H0, NSUB])
                                                        for n in ("mid", "all", "mid_next", "all_next", "rest"))
        vg = sb("g_vg", [P, TB, 2 * VW])
        sig = sb("g_sig", [P, TB, VW])
        v = sb("g_v", [P, TB, VW])
        gw = sb("g_gw", [P, TB, VW])
        rows = [[sb(f"c0_rows{u}_{j}", [P, D]) for j in range(TOPK)] for u in range(2)]
        at = [sb(f"c0_at{u}", [P, TOPK], U32) for u in range(2)]
        raw = sb("g_raw", [P, TB, 6])
        mv = sb("g_mv", [P, TB, 2])
        ln_var = sb("g_ln_var", [P, TB])
        rstd = sb("g_rstd", [P, TB])
        kT = sb("g_kT", [P, H0, DK])
        atm = sb("g_atm", [P, H0, SUB])
        state = sb("g_state", [P, H0, DV])
        state_mid = [sb(f"g_state_mid{u}", [P, H0, DV]) for u in range(2)]
        kv_dec = sb("g_kv_dec", [P, H0, DV])
        o = [sb(f"g_o{u}", [P, H0, DV]) for u in range(2)]
        sq = sb("g_sq", [P, H0, DV])
        ms = sb("g_ms", [P, H0])
        ln_ms = sb("g_ln_ms", [P, H0])
        rms = sb("g_rms", [P, H0])
        on = [sb(f"g_on{u}", [P, H0, DV]) for u in range(2)]
        oT = sb("g_oT", [P, 2, P])
        bank = [ps(f"g_bank{a}", [P, 512]) for a in range(A)]
        ps_at = [ps(f"g_ps_at{half}", [P, HG, SUB]) for half in range(2)]
        ps_kv = ps("g_ps_kv", [P, H0, DV])
        ps_o = ps("g_ps_o", [P, H0, DV])
        ps_out = ps("g_ps_out", [P, D])
        block = ctx.enter_context(nc.Block())

        def chunks(ap):
            return ap.rearrange("p h (c s) -> p h c s", s=SUB)

        def over(ap, m):
            return ap.unsqueeze(len(ap.shape)).to_broadcast(list(ap.shape) + [m])

        def emptied(eng, stage, key):
            m = stage[0][key]
            eng.wait_ge(a_free[m % A], stage[1] + (m // A + 2))

        def use(eng, stage, key):
            m = stage[0][key]
            eng.wait_ge(a_ready[m % A], stage[1] + (m // A + 1))
            return bank[m % A]

        def freed(stage, key):
            return a_free[stage[0][key] % A]

        def rounds(eng, body):
            with eng.Fori(0, B - 2) as b:
                body(b, stage_at(stage_round, b * round_uses + first_uses))
            body(B - 2, stage_at(stage_round, (B - 2) * round_uses + first_uses))

        def exists(b):
            return not isinstance(b, int) or b < B

        @block.tensor
        def _(pe):
            pe.wait_ge(k.sem("w0_loaded"), 16 * 7)

            def take(stage, key):
                m = stage[0][key]
                pe.wait_ge(a_free[m % A], stage[1] + (m // A + 1))
                return bank[m % A]

            def given(ins, stage, key):
                ins.then_inc(a_ready[stage[0][key] % A], 1)

            def transposes(b, stage):
                for j in range(TB):
                    pe.wait_ge(xn_ready, b * TB + (j + 1))
                    to = take(stage, ("tr", j))
                    for c in range(DC):
                        ins = pe.transpose(to[:, c * P:(c + 1) * P], xn[j][:, c * P:(c + 1) * P], k.ident[:, :])
                    given(ins, stage, ("tr", j))

            def low_rank(stage):
                for j in range(TB):
                    emptied(pe, stage, ("tr", j))
                to = take(stage, ("low", 0))
                for c in range(DC):
                    ins = pe.matmul(to[:, :], k.wgk0[:, c, :], xT[:, c, :], start=(c == 0), stop=(c == DC - 1))
                given(ins, stage, ("low", 0))

            def gates(stage, heads):
                emptied(pe, stage, ("low", 0))
                for h in heads:
                    to = take(stage, ("z", h))
                    given(pe.matmul(to[:, :], k.wgk1[:, h * DK:(h + 1) * DK], low[:, :], start=True, stop=True),
                          stage, ("z", h))

            def first_gates(stage):
                low_rank(stage)
                gates(stage, range(HG))

            def values_gates(stage, tiles):
                for j in tiles:
                    to = take(stage, ("vg", j))
                    for c in range(DC):
                        ins = pe.matmul(to[:, :], xT[:, c, j * P:(j + 1) * P], k.wvg[:, c, :],
                                        start=(c == 0), stop=(c == DC - 1))
                    given(ins, stage, ("vg", j))

            def projected(stage, name, weights, heads):
                for h in heads:
                    to = take(stage, (name, h))
                    for c in range(DC):
                        ins = pe.matmul(to[:, :], weights[:, c, h * DK:(h + 1) * DK], xT[:, c, :],
                                        start=(c == 0), stop=(c == DC - 1))
                    given(ins, stage, (name, h))

            def output(b, stage, j):
                pe.wait_ge(on_ready, b * TB + (j + 1))
                to = take(stage, ("o", j))
                flat = on[j % 2][:, :, :].rearrange("p h v -> p (h v)")
                for c in range(2):
                    ins = pe.transpose(to[:, c * P:(c + 1) * P], flat[:, c * P:(c + 1) * P], k.ident[:, :])
                given(ins, stage, ("o", j))
                emptied(pe, stage, ("o", j))
                pe.wait_ge(out_used, b * TB + (j + 1))
                for c in range(2):
                    ins = pe.matmul(ps_out[:, :], oT[:, c, :], k.wo0[:, c, :], start=(c == 0), stop=(c == 1))
                ins.then_inc(out_ready, 1)

            def recurrence(b, stage, within, after):
                for j in range(TB):
                    tokens = slice(j * P, (j + 1) * P)
                    for half in range(2):
                        pe.wait_ge(at_masked, (b * TB + j) * 2 + (half + 1))
                        for h in range(HG):
                            hh = half * HG + h
                            ins = pe.matmul(ps_at[half][:, h, :], kp[:, hh, tokens], qp[:, hh, tokens],
                                            start=True, stop=True)
                        ins.then_inc(at_ready, 1)
                    for half in range(2):
                        to = take(stage, ("kt", j, half))
                        for h in range(HG):
                            ins = pe.transpose(to[:, h * P:(h + 1) * P], kp[:, half * HG + h, tokens], k.ident[:, :])
                        given(ins, stage, ("kt", j, half))
                    within[j]()
                    emptied(pe, stage, ("kt", j, 0))
                    emptied(pe, stage, ("kt", j, 1))
                    if j == 0:
                        pe.wait_ge(v_ready, b + 1)
                    pe.wait_ge(kv_used, b * TB + (j + 1))
                    for h in range(H0):
                        ins = pe.matmul(ps_kv[:, h, :], kT[:, h, :], v[:, j, h * DV:(h + 1) * DV],
                                        start=True, stop=True)
                    ins.then_inc(kv_ready, 1)
                    pe.wait_ge(sm_ready, b * TB + (j + 1))
                    pe.wait_ge(at_masked, (b * TB + j) * 2 + 4)
                    pe.wait_ge(o_copied, b * TB + (j + 1))
                    for h in range(H0):
                        pe.matmul(ps_o[:, h, :], qp[:, h, tokens], state_mid[j % 2][:, h, :], start=True, stop=False)
                        ins = pe.matmul(ps_o[:, h, :], atm[:, h, :], v[:, j, h * DV:(h + 1) * DV],
                                        start=False, stop=True)
                    ins.then_inc(o_ready, 1)
                    if j:
                        output(b, stage, j - 1)
                    after[j]()

            def scaled(stage):
                for h in range(H0 - A, H0):
                    emptied(pe, stage, ("k", h))

            transposes(0, FIRST)
            low_rank(FIRST)
            gates(FIRST, range(H0))
            values_gates(FIRST, range(TB))
            projected(FIRST, "q", k.wq0, range(H0))
            projected(FIRST, "k", k.wk0, range(H0))
            scaled(FIRST)
            nothing = [lambda: None] * TB
            def one_round(b, stage):
                recurrence(b, stage,
                           [lambda: transposes(b + 1, stage), lambda: gates(stage, range(HG, H0)),
                            lambda: values_gates(stage, range(TB // 2, TB)), lambda: None],
                           [lambda: first_gates(stage), lambda: values_gates(stage, range(TB // 2)),
                            lambda: None, lambda: None])
                projected(stage, "q", k.wq0, range(3))
                output(b, stage, TB - 1)
                projected(stage, "q", k.wq0, range(3, H0))
                projected(stage, "k", k.wk0, range(H0))
                scaled(stage)

            rounds(pe, one_round)
            recurrence(B - 1, FINAL, nothing, nothing)
            output(B - 1, FINAL, TB - 1)

        @block.scalar
        def _(act):
            act.wait_ge(k.sem("w0_loaded"), 16 * 7)
            act.preload_act_table_set("natural_log_exp_and_others")

            def deviations(b):
                act.wait_ge(stats_done, (b + 1) * (2 * TB))
                act.activation(ln_var[:, :], mv[:, :, 1], ACT.Ln,
                               bias=k.eps[:, 0:1]).then_inc(lnv_ready, 1)
                act.wait_ge(lnv_ready, b + 1)
                act.activation(rstd[:, :], ln_var[:, :], ACT.Exp,
                               scale=-0.5).then_inc(rstd_ready, 1)

            def xT_copies(stage):
                for j in range(TB):
                    src = use(act, stage, ("tr", j))
                    act.activation(xT[:, :, j * P:(j + 1) * P], src[:, 0:D].rearrange("p (c t) -> p c t", c=DC),
                                   ACT.Copy).then_inc(freed(stage, ("tr", j)), 1)

            def low_copy(stage):
                src = use(act, stage, ("low", 0))
                act.activation(low[:, :], src[:, :], ACT.Copy).then_inc(freed(stage, ("low", 0)), 1)

            def z_copies(stage, heads):
                for h in heads:
                    src = use(act, stage, ("z", h))
                    act.activation(zm[:, h, :], src[:, :], ACT.Identity, bias=k.bgk1[:, h:h + 1])\
                       .then_inc(freed(stage, ("z", h)), 1)

            def exps(b, half):
                part = za[:, half * HG:(half + 1) * HG, :]
                act.wait_ge(abs_ready, b * 2 + (half + 1))
                act.activation(part, part, ACT.Exp, scale=-1.0).then_inc(act_steps, 1)

            def lns(b, half):
                part = za[:, half * HG:(half + 1) * HG, :]
                act.wait_ge(act_steps, b * 2 + (half + 1))
                act.activation(part, part, ACT.Ln, bias=1.0).then_inc(soft_ready, 1)

            def vg_copies(stage, tiles):
                for j in tiles:
                    src = use(act, stage, ("vg", j))
                    act.activation(sig[:, j, :], src[:, VW:2 * VW], ACT.Exp, scale=-1.0)
                    act.activation(vg[:, j, :], src[:, :], ACT.Copy).then_inc(freed(stage, ("vg", j)), 1)

            def sigmoids(b, stage):
                for j in range(TB):
                    emptied(act, stage, ("vg", j))
                act.activation(sig[:, :, :], sig[:, :, :], ACT.Ln, bias=1.0).then_inc(sig_ready, 1)
                act.wait_ge(sig_ready, b * 2 + 1)
                act.activation(sig[:, :, :], sig[:, :, :], ACT.Exp, scale=-1.0).then_inc(sig_ready, 1)

            def decays(b, half):
                hs = slice(half * HG, (half + 1) * HG)
                act.wait_ge(cen_ready, b * 2 + (half + 1))
                act.activation(e_mid_next[:, hs, :], mid[:, hs, :], ACT.Exp, scale=1.0 / GATE_NORM)
                act.activation(e_all_next[:, hs, :], chunks(zm[:, hs, :])[:, :, :, SUB - 1], ACT.Exp,
                               scale=1.0 / GATE_NORM).then_inc(edge_ready, 1)
                act.wait_ge(edge_ready, b * 2 + (half + 1))
                act.activation(zm[:, hs, :], za[:, hs, :], ACT.Exp, scale=1.0 / GATE_NORM).then_inc(up_ready, 1)
                act.wait_ge(up_ready, b * 2 + (half + 1))
                act.activation(za[:, hs, :], za[:, hs, :], ACT.Exp, scale=-1.0 / GATE_NORM).then_inc(down_ready, 1)

            def kT_copies(stage, j):
                for half in range(2):
                    src = use(act, stage, ("kt", j, half))
                    act.activation(kT[:, half * HG:(half + 1) * HG, :],
                                   src[:, :].rearrange("p (h d) -> p h d", h=HG), ACT.Copy)\
                       .then_inc(freed(stage, ("kt", j, half)), 1)

            def o_copy(b, j):
                act.wait_ge(o_ready, b * TB + (j + 1))
                act.activation(o[j % 2][:, :, :], ps_o[:, :, :], ACT.Copy).then_inc(o_copied, 1)

            def oT_copy(stage, j):
                src = use(act, stage, ("o", j))
                act.activation(oT[:, :, :], src[:, 0:D].rearrange("p (c t) -> p c t", c=2),
                               ACT.Copy).then_inc(freed(stage, ("o", j)), 1)

            def inverse_rms(b, j):
                act.wait_ge(ms_ready, b * TB + (j + 1))
                act.activation(ln_ms[:, :], ms[:, :], ACT.Ln, bias=k.eps[:, 0:1], scale=1.0 / DV).then_inc(ln_steps, 1)
                act.wait_ge(ln_steps, b * TB + (j + 1))
                act.activation(rms[:, :], ln_ms[:, :], ACT.Exp, scale=-0.5).then_inc(rms_ready, 1)

            def recurrence(b, stage, within, after):
                for j in range(TB):
                    kT_copies(stage, j)
                    within[j]()
                    o_copy(b, j)
                    if j:
                        oT_copy(stage, j - 1)
                    inverse_rms(b, j)
                    after[j]()

            deviations(0)
            xT_copies(FIRST)
            low_copy(FIRST)
            z_copies(FIRST, range(H0))
            for half in range(2):
                exps(0, half)
            for half in range(2):
                lns(0, half)
            vg_copies(FIRST, range(TB))
            sigmoids(0, FIRST)
            for half in range(2):
                decays(0, half)
            deviations(1)
            nothing = [lambda: None] * TB
            def one_round(b, stage):
                def first_gates():
                    low_copy(stage)
                    z_copies(stage, range(HG))

                def first_softplus():
                    exps(b + 1, 0)
                    lns(b + 1, 0)
                    vg_copies(stage, range(TB // 2))
                    exps(b + 1, 1)

                def second_softplus():
                    vg_copies(stage, range(TB // 2, TB))
                    lns(b + 1, 1)

                def first_decays():
                    decays(b + 1, 0)
                    sigmoids(b + 1, stage)

                recurrence(b, stage,
                           [lambda: xT_copies(stage), lambda: z_copies(stage, range(HG, H0)),
                            second_softplus, lambda: None],
                           [first_gates, first_softplus, first_decays, lambda: decays(b + 1, 1)])
                oT_copy(stage, TB - 1)
                if exists(b + 2):
                    deviations(b + 2)

            rounds(act, one_round)
            recurrence(B - 1, FINAL, nothing, nothing)
            oT_copy(FINAL, TB - 1)

        @block.gpsimd
        def _(pool):
            def gate_weights(b, stage):
                s = Steps(pool, pool_steps, b, 1)
                for j in range(TB):
                    emptied(pool, stage, ("vg", j))
                if not isinstance(b, int) or b > 0:
                    pool.wait_ge(o_ready, b * TB)
                pool_copy(pool, k, v[:, :, :], vg[:, :, 0:VW]).then_inc(v_ready, 1)
                if not isinstance(b, int) or b > 0:
                    pool.wait_ge(on_ready, b * TB)
                pool.wait_ge(sig_ready, b * 2 + 2)
                s.mark(pool.tensor_tensor(gw[:, :, :], vg[:, :, VW:2 * VW], sig[:, :, :], ALU.mult))
                s.settle()
                s.close()
                all_gw = gw[:, :, :].rearrange("p t (h v) -> p (t h) v", v=DV)
                pool.tensor_tensor(all_gw, all_gw, k.gnorm[:, :].unsqueeze(1).to_broadcast([P, TB * H0, DV]),
                                   ALU.mult).then_inc(gw_ready, 1)

            def gather(b, j):
                if exists(b):
                    gather_tile(pool, k, 0, b * TB + j, j % 2, rows, at)

            def squares(b, after):
                for j in range(TB):
                    pool.wait_ge(o_copied, b * TB + (j + 2))
                    pool.tensor_tensor(sq[:, :, :], o[j % 2][:, :, :], o[j % 2][:, :, :], ALU.mult).then_inc(sq_ready, 1)
                    after(j)

            def one_round(b, stage):
                squares(b, lambda j: gather(b + 2, j) if j < 2 else None)
                gate_weights(b + 1, stage)
                gather(b + 2, 2)
                gather(b + 2, 3)

            pool.sem_inc(k.sem("c_rows_used"), 2)
            for j in range(TB):
                gather(0, j)
            gather(1, 0)
            gather(1, 1)
            gate_weights(0, FIRST)
            gather(1, 2)
            gather(1, 3)
            rounds(pool, one_round)
            squares(B - 1, lambda j: None)

        @block.vector
        def _(dve):
            dve.wait_ge(k.sem("x_loaded"), 16)
            for a in range(A):
                dve.sem_inc(a_free[a], 1)
            dve.sem_inc(at_masked, 2)
            dve.sem_inc(kv_used, 1)
            dve.sem_inc(o_copied, 1)
            dve.sem_inc(out_used, 1)

            def row_statistics(b, j):
                n = b * TB + j
                s = Steps(dve, stats_done, n, 2)
                dve.sem_inc(s.passed, 1)
                s.mark(dve.bn_stats(raw[:, j, :], k.X[:, n, :]))
                s.settle_apart()
                s.mark(dve.bn_aggr(mv[:, j, :], raw[:, j, :]))
                s.close()

            def prepared(b, m):
                if exists(b):
                    j, part = m // 4, m % 4
                    if part < 3:
                        for row in (2 * part, 2 * part + 1):
                            add_row(dve, k, 0, b * TB + j, j % 2, rows, row)
                    else:
                        rows_all_added(dve, k, 0, b * TB + j)
                        row_statistics(b, j)

            def normalise(b):
                dve.wait_ge(rstd_ready, b + 1)
                for j in range(TB):
                    dve.tensor_scalar(xn[j][:, :], k.X[:, b * TB + j, :], mv[:, j, 0:1], rstd[:, j:j + 1],
                                      ALU.subtract, ALU.mult).then_inc(xn_ready, 1)
                dve.wait_ge(xn_ready, (b + 1) * TB)

            def absolute(b, stage, half):
                hs = slice(half * HG, (half + 1) * HG)
                for h in range(HG * (half + 1) - A, HG * (half + 1)):
                    emptied(dve, stage, ("z", h))
                dve.scalar_tensor_tensor(out=za[:, hs, :], in0=zm[:, hs, :], scalar=-1.0, in1=zm[:, hs, :],
                                         op0=ALU.mult, op1=ALU.max).then_inc(abs_ready, 1)

            def log_gates(b, half):
                s = Steps(dve, gate_steps, b * 2 + half, 3)
                hs = slice(half * HG, (half + 1) * HG)
                dve.wait_ge(soft_ready, b * 2 + (half + 1))
                s.mark(dve.scalar_tensor_tensor(out=zm[:, hs, :], in0=zm[:, hs, :], scalar=0.0, in1=za[:, hs, :],
                                                op0=ALU.min, op1=ALU.subtract))
                s.settle()
                for h in range(half * HG, (half + 1) * HG):
                    ins = dve.tensor_tensor_scan(zm[:, h, :], k.chunk_keep[:, :], zm[:, h, :], 0.0, ALU.mult, ALU.add)
                s.mark(ins)
                s.settle()
                s.mark(dve.tensor_copy(mid[:, hs, :], chunks(zm[:, hs, :])[:, :, :, MID]))
                s.settle()
                s.close()
                for h in range(half * HG, (half + 1) * HG):
                    ins = dve.tensor_tensor(za[:, h, :].rearrange("p (c s) -> p c s", s=SUB),
                                            zm[:, h, :].rearrange("p (c s) -> p c s", s=SUB),
                                            over(mid[:, h, :], SUB), ALU.subtract)
                ins.then_inc(cen_ready, 1)

            def scale(b, stage, name, first, last):
                assert 4 * TB == 2 * H0
                dst, dec, by = (qp, zm, DK ** -0.5) if name == "q" else (kp, za, 1.0)
                for h in range(first, last):
                    if h % HG == 0:
                        dve.wait_ge(up_ready if name == "q" else down_ready, b * 2 + (h // HG + 1))
                    src = use(dve, stage, (name, h))
                    dve.scalar_tensor_tensor(out=dst[:, h, :], in0=src[:, :], scalar=by, in1=dec[:, h, :],
                                             op0=ALU.mult, op1=ALU.mult).then_inc(freed(stage, (name, h)), 1)
                    prepared(b + 1, h if name == "q" else H0 + h)

            def edges(b, stage):
                s = Steps(dve, edges_taken, b, 4)
                s.mark(dve.tensor_copy(e_rest[:, :, :], chunks(zm[:, :, :])[:, :, :, SUB - 1]))
                s.mark(dve.tensor_copy(e_mid[:, :, :], e_mid_next[:, :, :]))
                s.mark(dve.tensor_copy(e_all[:, :, :], e_all_next[:, :, :]))
                s.mark(dve.memset(state[:, :, :], 0.0))
                scale(b, stage, "k", 0, H0)
                s.settle()
                s.close()
                for h in range(H0 - A, H0):
                    emptied(dve, stage, ("k", h))

            def add_out(b, j):
                dve.wait_ge(out_ready, b * TB + (j + 1))
                x = k.X[:, b * TB + j, :]
                dve.tensor_tensor(x, ps_out[:, :], x, ALU.add).then_inc(out_used, 1)

            def recurrence(b, stage, begin, within, after):
                s = Steps(dve, dve_steps, b, TB * 3)
                for j in range(TB):
                    for half in range(2):
                        dve.wait_ge(at_ready, (b * TB + j) * 2 + (half + 1))
                        dve.tensor_tensor(atm[:, half * HG:(half + 1) * HG, :], ps_at[half][:, :, :],
                                          k.causal[:, :].unsqueeze(1).to_broadcast([P, HG, SUB]),
                                          ALU.mult).then_inc(at_masked, 1)
                    dve.tensor_tensor(state_mid[j % 2][:, :, :], state[:, :, :], over(e_mid[:, :, j], DV),
                                      ALU.mult).then_inc(sm_ready, 1)
                    s.mark(dve.tensor_tensor(state[:, :, :], state[:, :, :], over(e_all[:, :, j], DV), ALU.mult))
                    begin[j]()
                    if j >= 2:
                        add_out(b, j - 2)
                    dve.wait_ge(kv_ready, b * TB + (j + 1))
                    dve.tensor_tensor(kv_dec[:, :, :], ps_kv[:, :, :], over(e_rest[:, :, j], DV),
                                      ALU.mult).then_inc(kv_used, 1)
                    dve.wait_ge(kv_used, b * TB + (j + 2))
                    s.settle()
                    s.mark(dve.tensor_tensor(state[:, :, :], state[:, :, :], kv_dec[:, :, :], ALU.add))
                    s.settle()
                    within[j]()
                    dve.wait_ge(sq_ready, b * TB + (j + 1))
                    dve.tensor_reduce(ms[:, :], sq[:, :, :], AX, ALU.add).then_inc(ms_ready, 1)
                    dve.wait_ge(rms_ready, b * TB + (j + 1))
                    s.mark(dve.tensor_tensor(on[j % 2][:, :, :], o[j % 2][:, :, :], over(rms[:, :], DV), ALU.mult))
                    s.settle()
                    if j == 0:
                        dve.wait_ge(gw_ready, b + 1)
                    dve.tensor_tensor(on[j % 2][:, :, :], on[j % 2][:, :, :],
                                      gw[:, j, :].rearrange("p (h v) -> p h v", h=H0), ALU.mult).then_inc(on_ready, 1)
                    after[j]()
                s.close()

            for m in range(4 * TB):
                prepared(0, m)
            normalise(0)
            for half in range(2):
                absolute(0, FIRST, half)
            for half in range(2):
                log_gates(0, half)
            scale(0, FIRST, "q", 0, H0)
            edges(0, FIRST)
            nothing = [lambda: None] * TB
            def one_round(b, stage):
                recurrence(b, stage,
                           [lambda: normalise(b + 1), lambda: None, lambda: log_gates(b + 1, 0),
                            lambda: log_gates(b + 1, 1)],
                           [lambda: None, lambda: absolute(b + 1, stage, 0), lambda: None, lambda: None],
                           [lambda: None, lambda: absolute(b + 1, stage, 1), lambda: None, lambda: None])
                add_out(b, TB - 2)
                scale(b + 1, stage, "q", 0, 3)
                add_out(b, TB - 1)
                scale(b + 1, stage, "q", 3, H0)
                edges(b + 1, stage)

            rounds(dve, one_round)
            recurrence(B - 1, FINAL, nothing, nothing, nothing)
            add_out(B - 1, TB - 2)
            add_out(B - 1, TB - 1)


def latent_attention(nc, k):
    UP = 2 * TB
    U2 = 2 * UP
    NU = PAIRS * UP
    TLAG = 3
    VLAG = UP + TLAG
    OLAG = VLAG + UP
    LAST = NU - UP + OLAG
    PRE = TB + 2 + PAIRS
    QB = PRE // 2
    assert PRE % 2 == 0 and TB % 2 == 0
    xn_ready = k.sem("m_xn_ready")
    bank_ready = [k.sem(f"m_bank_ready{u}") for u in range(2)]
    bank_free = [k.sem(f"m_bank_free{u}") for u in range(2)]
    high_ready = k.sem("m_high_parts_ready")
    q_staged, s_ready, nmax_ready, p_ready = (k.sem("m_queries_staged"), k.sem("m_scores_ready"),
                                              k.sem("m_neg_max_ready"), k.sem("m_probs_ready"))
    scaled, pT_raw, pT_ready = k.sem("m_normalised"), k.sem("m_pT_psum_ready"), k.sem("m_pT_ready")
    v_ready, o_copied = k.sem("m_values_ready"), k.sem("m_o_copied")
    out_ready, out_used = k.sem("m_out_ready"), k.sem("m_out_used")
    inv_steps = k.sem("m_inverse_steps")
    TR, LATT, LATK, Q = 0, TB, TB + 1, TB + 2
    with ExitStack() as ctx:
        sb, ps = scoped(nc, ctx)
        xn = [sb(f"m_xn{u}", [P, D]) for u in range(2)]
        xT = sb("m_xT", [P, DC, T])
        latT = [sb(f"m_latT_{part}", [P, T], F32R) for part in ("high", "low")]
        lat = sb("m_lat", [P, TB, LAT])
        qa = sb("m_qa", [P, H1, T], F32R)
        qs = [sb(f"m_qs{u}", [P, 2, T], F32R) for u in range(2)]
        nmax = sb("m_nmax", [P, 2])
        rsum = sb("m_rsum", [P, 4])
        rinv = sb("m_rinv", [P, 2])
        prob = [sb(f"m_prob{u}", [P, T]) for u in range(4)]
        pT = [sb(f"m_pT{u}", [P, 2, TB, T]) for u in range(2)]
        oT = sb("m_oT", [P, PAIRS, T])
        bank = [ps(f"m_bank{u}", [P, 512]) for u in range(2)]
        ps_s = [ps(f"m_ps_s{u}", [P, T]) for u in range(2)]
        ps_p = [ps(f"m_ps_p{u}", [P, TB, P]) for u in range(2)]
        ps_v = [ps(f"m_ps_v{u}", [P, T]) for u in range(2)]
        block = ctx.enter_context(nc.Block())

        def live(m, lag):
            return not isinstance(m, int) or 0 <= m - lag < NU

        def place(u, lag):
            w = (u - lag) % U2
            return w // UP, w % UP // 2, w % 2

        def steps(eng, body):
            for m in range(U2):
                body(m, m, 0)
            with eng.Fori(1, NU // U2) as i:
                for u in range(U2):
                    body(i * U2 + u, u, i)
            for m in range(NU, LAST + 1):
                body(m, m - NU, NU // U2)

        def pair_at(m, u, i, lag):
            w = u - lag
            if w % UP or (isinstance(m, int) and not 0 <= m - lag < NU):
                return None
            return i * 2 + w // UP

        @block.tensor
        def _(pe):
            pe.wait_ge(k.sem("w1_loaded"), 16 * 3)
            with pe.Fori(0, B) as b:
                def take(m):
                    pe.wait_ge(bank_free[m % 2], b * QB + (m // 2 + 1))
                    return bank[m % 2]

                for j in range(TB):
                    pe.wait_ge(xn_ready, b * TB + (j + 1))
                    to = take(TR + j)
                    for c in range(DC):
                        ins = pe.transpose(to[:, c * P:(c + 1) * P], xn[j % 2][:, c * P:(c + 1) * P], k.ident[:, :])
                    ins.then_inc(bank_ready[j % 2], 1)
                for j in range(TB - 2, TB):
                    pe.wait_ge(bank_free[j % 2], b * QB + (j // 2 + 2))
                to = take(LATT)
                for c in range(DC):
                    ins = pe.matmul(to[:, :], k.wkv1[:, c, :], xT[:, c, :], start=(c == 0), stop=(c == DC - 1))
                ins.then_inc(bank_ready[LATT % 2], 1)
                to = take(LATK)
                for j in range(TB):
                    for c in range(DC):
                        ins = pe.matmul(to[:, j * LAT:(j + 1) * LAT], xT[:, c, j * P:(j + 1) * P], k.wkv1[:, c, 0:LAT],
                                        start=(c == 0), stop=(c == DC - 1))
                ins.then_inc(bank_ready[LATK % 2], 1)
                for p in range(PAIRS):
                    to = take(Q + p)
                    for c in range(DC):
                        ins = pe.matmul(to[:, :], k.absorb[:, c, p * P:(p + 1) * P], xT[:, c, :],
                                        start=(c == 0), stop=(c == DC - 1))
                    ins.then_inc(bank_ready[(Q + p) % 2], 1)

                def step(m, u, i):
                    g = b * NU + m
                    if live(m, 0):
                        par, tile, hh = place(u, 0)
                        if u % UP == 0:
                            pe.wait_ge(q_staged, b * PAIRS + i * 2 + (u // UP + 1))
                        pe.wait_ge(p_ready, g + 1)
                        query = qs[par][:, hh, tile * P:(tile + 1) * P]
                        pe.matmul(ps_s[u % 2][:, :], query, latT[0][:, :], start=True, stop=False)
                        pe.matmul(ps_s[u % 2][:, :], query, latT[1][:, :], start=False, stop=True).then_inc(s_ready, 1)
                    if live(m, TLAG):
                        pe.wait_ge(scaled, g - (TLAG - 1))
                        pe.wait_ge(pT_ready, g - (TLAG - 1))
                        for t in range(TB):
                            ins = pe.transpose(ps_p[(u - TLAG) % 2][:, t, :], prob[(u - TLAG) % 4][:, t * P:(t + 1) * P],
                                               k.ident[:, :])
                        ins.then_inc(pT_raw, 1)
                    for part in range(UP):
                        pair = pair_at(m, u, i, VLAG + part)
                        if pair is None:
                            continue
                        par = place(u, VLAG + part)[0]
                        half, t = part // TB, part % TB
                        queries = slice(half * (T // 2), (half + 1) * (T // 2))
                        if part == 0:
                            pe.wait_ge(pT_ready, b * NU + pair * UP + (UP + 2))
                            pe.wait_ge(o_copied, b * PAIRS + pair + 1)
                        for hh in range(2):
                            ins = pe.matmul(ps_v[par][hh * LAT:(hh + 1) * LAT, queries], lat[:, t, :],
                                            pT[par][:, hh, t, queries], start=(t == 0), stop=(t == TB - 1))
                        if part == UP - 1:
                            ins.then_inc(v_ready, 1)

                steps(pe, step)
                pe.wait_ge(o_copied, b * PAIRS + (PAIRS + 2))
                for t in range(TB):
                    if t >= 2:
                        pe.wait_ge(out_used, b * TB + (t - 1))
                    for p in range(PAIRS):
                        ins = pe.matmul(ps_s[t % 2][:, 0:D], oT[:, p, t * P:(t + 1) * P], k.mix[:, p, :],
                                        start=(p == 0), stop=(p == PAIRS - 1))
                    ins.then_inc(out_ready, 1)

        @block.scalar
        def _(act):
            row_std(act, k)
            with act.Fori(0, B) as b:
                def use(m):
                    act.wait_ge(bank_ready[m % 2], b * QB + (m // 2 + 1))
                    return bank[m % 2]

                for j in range(TB):
                    act.activation(xT[:, :, j * P:(j + 1) * P], use(TR + j)[:, 0:D].rearrange("p (c t) -> p c t", c=DC),
                                   ACT.Copy).then_inc(bank_free[j % 2], 1)
                act.activation(latT[0][:, :], use(LATT), ACT.Copy).then_inc(high_ready, 1)
                act.activation(lat[:, :, :], use(LATK)[:, 0:TB * LAT].rearrange("p (t l) -> p t l", l=LAT),
                               ACT.Copy).then_inc(bank_free[LATK % 2], 1)
                for p in range(PAIRS):
                    src = use(Q + p)
                    act.activation(qa[0:LAT, 2 * p, :], src[0:LAT, :], ACT.Copy)
                    act.activation(qa[LAT:P, 2 * p + 1, :], src[LAT:P, :], ACT.Copy).then_inc(high_ready, 1)

                def step(m, u, i):
                    g = b * NU + m
                    if live(m, TLAG):
                        par, tile, hh = place(u, TLAG)
                        act.wait_ge(pT_raw, g - (TLAG - 1))
                        act.activation(pT[par][:, hh, :, tile * P:(tile + 1) * P], ps_p[(u - TLAG) % 2][:, :, :],
                                       ACT.Copy).then_inc(pT_ready, 1)
                    if live(m, 0):
                        act.wait_ge(nmax_ready, g + 1)
                        act.activation(prob[u % 4][:, :], ps_s[u % 2][:, :], ACT.Exp, bias=nmax[:, u % 2:u % 2 + 1],
                                       accum_out=rsum[:, u % 4:u % 4 + 1]).then_inc(p_ready, 1)
                    pair = pair_at(m, u, i, OLAG)
                    if pair is not None:
                        act.wait_ge(v_ready, b * PAIRS + pair + 1)
                        act.activation(oT[:, pair, :], ps_v[place(u, OLAG)[0]][:, :], ACT.Copy).then_inc(o_copied, 1)

                steps(act, step)

        @block.gpsimd
        def _(pool):
            for sem in bank_free:
                pool.sem_inc(sem, 1)
            for sem in (p_ready, pT_ready, o_copied):
                pool.sem_inc(sem, 2)
            with pool.Fori(0, B) as b:
                def stage(i, par):
                    pair = i * 2 + par
                    pool_copy(pool, k, qs[par][:, :, :], qa[:, bass.ds(pair * 2, 2), :].bitcast(F32)).then_inc(q_staged, 1)

                for par in range(2):
                    pool.wait_ge(bank_free[(Q + par) % 2], b * QB + ((Q + par) // 2 + 2))
                    pool.sem_inc(k.sem("passed"), 1)
                    stage(0, par)
                for m in range(Q + PAIRS - 2, Q + PAIRS):
                    pool.wait_ge(bank_free[m % 2], b * QB + (m // 2 + 2))
                    pool.sem_inc(k.sem("passed"), 1)
                with pool.Fori(1, PAIRS // 2) as i:
                    for par in range(2):
                        pool.wait_ge(s_ready, b * NU + i * U2 + (par - 1) * UP)
                        pool.sem_inc(k.sem("passed"), 1)
                        stage(i, par)

        @block.vector
        def _(dve):
            row_stats(dve, k)
            row_rstd(dve, k)
            with dve.Fori(0, B) as b:
                for j in range(TB):
                    if j >= 2:
                        dve.wait_ge(bank_ready[j % 2], b * QB + j // 2)
                    layernorm(dve, k, b * TB + j, xn[j % 2][:, :], xn_ready)
                dve.wait_ge(high_ready, b * (PAIRS + 1) + 1)
                dve.tensor_tensor(latT[1][:, :], bank[LATT % 2], latT[0][:, :].bitcast(F32),
                                  ALU.subtract).then_inc(bank_free[LATT % 2], 1)
                for p in range(PAIRS):
                    src = bank[(Q + p) % 2]
                    dve.wait_ge(high_ready, b * (PAIRS + 1) + (p + 2))
                    dve.tensor_tensor(qa[LAT:P, 2 * p, :], src[0:LAT, :], qa[0:LAT, 2 * p, :].bitcast(F32), ALU.subtract)
                    dve.tensor_tensor(qa[0:LAT, 2 * p + 1, :], src[LAT:P, :], qa[LAT:P, 2 * p + 1, :].bitcast(F32),
                                      ALU.subtract).then_inc(bank_free[(Q + p) % 2], 1)

                def step(m, u, i):
                    g = b * NU + m
                    if live(m, 0):
                        v = slice(u % 2, u % 2 + 1)
                        dve.wait_ge(s_ready, g + 1)
                        dve.tensor_reduce(nmax[:, v], ps_s[u % 2][:, :], AX, ALU.max, negate=True).then_inc(nmax_ready, 1)
                    if live(m, 1):
                        v, w = (u - 1) % 2, (u - 1) % 4
                        dve.wait_ge(p_ready, g + 2)
                        dve.reciprocal(rinv[:, v:v + 1], rsum[:, w:w + 1]).then_inc(inv_steps, 1)
                        dve.wait_ge(inv_steps, g)
                        dve.tensor_scalar(prob[w][:, :], prob[w][:, :], rinv[:, v:v + 1], None, ALU.mult)\
                           .then_inc(scaled, 1)

                steps(dve, step)
                for t in range(TB):
                    x = k.X[:, b * TB + t, :]
                    dve.wait_ge(out_ready, b * TB + (t + 1))
                    dve.tensor_tensor(x, ps_s[t % 2][:, 0:D], x, ALU.add).then_inc(out_used, 1)
    k.norms += 1


def expert_layer(nc, k, r):
    with ExitStack() as ctx:
        k.wgu = [ctx.enter_context(nc.sbuf_tensor(f"e{r}_wgu{u}", [P, DC, 2 * M0], F32)) for u in range(AHEAD)]
        k.wdn = [ctx.enter_context(nc.sbuf_tensor(f"e{r}_wdn{u}", [MH, 2, D], F32)) for u in range(AHEAD)]
        route(nc, k, r)
        routed_experts(nc, k, r)


def macaron(nc, w, out):
    with ExitStack() as ctx:
        k = Kit(nc, ctx)
        Steps.passed = k.sem("passed")
        k.w, k.norms = w, 0
        k.X = k.sb("x", [P, NT, D])
        k.row_raw = k.sb("row_raw", [P, NT, 6])
        k.row_mv = k.sb("row_mv", [P, NT, 2])
        k.row_rstd = k.sb("row_rstd", [P, NT])
        k.gateT = k.sb("gateT", [P, DC, E0])
        k.sguT = k.sb("sguT", [P, DC, 2 * MS])
        k.sdT = k.sb("sdT", [P, 3, D])
        k.wvg = k.sb("wvg", [P, DC, 2 * H0 * DV])
        k.wgk0 = k.sb("wgk0", [P, DC, P])
        k.wgk1 = k.sb("wgk1", [P, H0 * DK])
        k.bgk1 = k.sb("bgk1", [P, H0])
        k.wq0 = k.sb("wq0", [P, DC, H0 * DK])
        k.wk0 = k.sb("wk0", [P, DC, H0 * DK])
        k.wo0 = k.sb("wo0", [P, DC, D])
        k.gnorm_row = k.sb("gnorm_row", [1, DV])
        k.gnorm = k.sb("gnorm", [P, DV])
        k.wr1 = k.sb("wr1", [P, DC, E1])
        k.wkv1 = k.sb("wkv1", [P, DC, 2 * LAT])
        k.be1 = k.sb("be1", [P, D])
        k.absorb = k.sb("absorb", [P, DC, H1 * LAT])
        k.mix = k.sb("mix", [P, PAIRS, D])
        k.ident = k.sb("ident", [P, P])
        k.before_bf = k.sb("before_bf", [P, P], BF16)
        k.ones_bf = k.sb("ones_bf", [P, P], BF16)
        k.causal = k.sb("causal", [P, SUB])
        k.chunk_keep = k.sb("chunk_keep", [P, T])
        k.eps = k.sb("eps", [P, 1])
        k.zeros = k.sb("zeros", [P, P])
        k.last_slot = k.sb("last_slot", [E0, CAP])
        k.iota64 = k.sb("iota64", [P, E0])
        k.iota_slot = k.sb("iota_slot", [P, CAP])
        k.token_part = k.sb("token_part", [P, 2, NT])
        k.token1 = k.sb("token1", [P, NT])
        k.member_sum = k.sb("member_sum", [P, 2, E0], BF16)
        k.weight = k.sb("weight", [P, NT, TOPK])
        k.slot = k.sb("slot", [P, NT, TOPK], U32)
        k.table = k.sb("table", [CAP, E0], U32)
        k.xn_rows = nc.dram_tensor("xn_rows", [N, D], F32, kind="Internal").ap()
        k.slot_rows = nc.dram_tensor("slot_rows", [E0 * CAP, D], F32, kind="Internal").ap()
        load_and_prepare(nc, k, w)
        expert_layer(nc, k, 0)
        linear_attention(nc, k)
        k.we1 = k.sb("we1", [P, DC, E1, D])
        expert_layer(nc, k, 1)
        dense_experts(nc, k, 0, combine=1)
        latent_attention(nc, k)
        dense_experts(nc, k, 1, store=out)


def arrange(a):
    import numpy as np

    c = np.ascontiguousarray
    down = a["L0_ffn_Wd"].transpose(0, 2, 1)
    down_chunks = np.zeros((E0, MH, 2, D), down.dtype)
    down_chunks[:, :, 0] = down[:, 0:MH]
    down_chunks[:, 2 * MH - M0:, 1] = down[:, MH:M0]
    gu = np.concatenate([a["L0_ffn_Wg"].transpose(0, 2, 1), a["L0_ffn_Wu"].transpose(0, 2, 1)], axis=2)
    return {
        "x": c(a["L0_attn_hidden_states"].reshape(N, D)),
        "wqT1": c(a["L1_attn_W_q"].T), "upT1": c(a["L1_attn_W_kv_up"].T), "wo1": c(a["L1_attn_W_o"]),
        "gateT": c(a["L0_ffn_gate_weight"].T),
        "sguT": c(np.concatenate([a["L0_ffn_Sg"].T, a["L0_ffn_Su"].T], axis=1)),
        "sdT": c(a["L0_ffn_Sd"].T),
        "wvg": c(np.concatenate([a["L0_attn_Wv"], a["L0_attn_Wg"]], axis=1)),
        "wgk0": c(a["L0_attn_Wgk0"]), "wgk1": c(a["L0_attn_Wgk1"]),
        "bgk1": c(a["L0_attn_bgk1"].reshape(H0, DK).T), "gnorm": c(a["L0_attn_g_norm_w"]),
        "wq0": c(a["L0_attn_Wq"]), "wk0": c(a["L0_attn_Wk"]), "wo0": c(a["L0_attn_Wo"]),
        "wr1": c(a["L1_ffn_Wr"]),
        "wkv1": c(np.concatenate([a["L1_attn_W_kv_down"], a["L1_attn_W_kv_down"]], axis=1)),
        "we1": c(a["L1_ffn_We"]), "be1": c(a["L1_ffn_be"]),
        "wgu0": c(gu.reshape(E0, DC, P, 2 * M0).transpose(0, 2, 1, 3)),
        "wdn0": c(down_chunks),
    }


def build(nc, arrays):
    w = {n: nc.dram_tensor(n, a.shape, F32, kind="ExternalInput").ap() for n, a in arrays.items()}
    out = nc.dram_tensor("out", [N, D], F32, kind="ExternalOutput").ap()
    macaron(nc, w, out)


def kernel(**inputs):
    import concourse.bacc as bacc
    import numpy as np
    from concourse.bass_utils import run_bass_kernel_spmd

    arrays = arrange({n: np.asarray(a) for n, a in inputs.items()})
    nc = bacc.Bacc("TRN2", target_bir_lowering=False, num_devices=1)
    build(nc, arrays)
    result = run_bass_kernel_spmd(nc, [arrays], core_ids=[0])
    return result.results[0]["out"].reshape(B, T, D)
```
